# Optimizing a Trainium2 kernel written in Bass

```python
import numpy as np
import jax
import jax.numpy as jnp

def _softmax(x, axis=-1):
    return jax.nn.softmax(x, axis=axis)

def _gelu(x):
    return jax.nn.gelu(x, approximate=True)

def _silu(x):
    return jax.nn.silu(x)

def _sigmoid(x):
    return jax.nn.sigmoid(x)

def _layernorm(x, axis=-1, eps=1e-05):
    m = jnp.mean(x, axis=axis, keepdims=True)
    v = jnp.var(x, axis=axis, keepdims=True)
    return (x - m) / jnp.sqrt(v + eps)

def _scatter_add(tgt, idx, src, axis=0):
    return tgt.at[idx].add(src)

def _segment_sum(src, seg, n):
    return jax.ops.segment_sum(src, seg, n)
kernel_name = 'mk_xattn_seq_d2_seqx_r4_999e5a'

def setup_inputs(seed: int=0):
    np.random.seed(seed)
    _w = jnp.asarray

    def _rec_inputs():
        import jax
        import jax.numpy as jnp
        _rk = jax.random.key(seed)
        x = -0.000929 + 1 * jax.random.normal(jax.random.fold_in(_rk, 1), (1, 2048, 256), jnp.float32)
        _lenS = 2048 - jax.random.randint(jax.random.fold_in(_rk, 7), (1,), 0, max(1, 2048 // 4) + 1, jnp.int32)
        _lenS2 = 1601 - jax.random.randint(jax.random.fold_in(_rk, 8), (1,), 0, max(1, 1601 // 4) + 1, jnp.int32)
        _ctx_768P = jax.random.normal(jax.random.fold_in(_rk, 11), (1, 16, 192), jnp.float32)
        _ctx_768c = jax.random.dirichlet(jax.random.fold_in(_rk, 511), 0.3 * jnp.ones((16,), jnp.float32), (1, 1601))
        _ctx_768t = jnp.einsum('bsk,bkd->bsd', _ctx_768c, _ctx_768P)
        _ctx_768t = _ctx_768t * jax.lax.rsqrt(jnp.mean(jnp.square(_ctx_768t)) + 1e-12) * 0.953939
        ctx_768 = -5.15168e-05 + 0.999825 * (_ctx_768t + 0.3 * jax.random.normal(jax.random.fold_in(_rk, 611), (1, 1601, 192), jnp.float32))
        return (x, ctx_768)
    x, ctx_768 = _rec_inputs()

    def _L0_xattn_setup():
        import jax, jax.numpy as jnp
        import numpy as np
        LN_EPS = 1e-05

        def _ln(x, g, b):
            m = jnp.mean(x, axis=-1, keepdims=True)
            v = jnp.mean((x - m) ** 2, axis=-1, keepdims=True)
            return (x - m) / jnp.sqrt(v + LN_EPS) * g + b
        key = jax.random.key(seed)
        ks = jax.random.split(key, 8)
        B, N, S, D, T = (16, 64, 512, 256, 192)

        def xavier(k, shape):
            fan_in, fan_out = shape
            lim = (6.0 / (fan_in + fan_out)) ** 0.5
            return jax.random.uniform(k, shape, minval=-lim, maxval=lim, dtype=jnp.float32)
        return {'prev_states': jax.random.normal(ks[0], (B, N, D), dtype=jnp.float32), 'input_tokens': jax.random.normal(ks[1], (B, S, T), dtype=jnp.float32), 'W_proj': xavier(ks[2], (T, D)), 'b_proj': jnp.zeros((D,), jnp.float32), 'g_state': jnp.ones((D,), jnp.float32), 'beta_state': jnp.zeros((D,), jnp.float32), 'g_input': jnp.ones((D,), jnp.float32), 'beta_input': jnp.zeros((D,), jnp.float32), 'g_out': jnp.ones((D,), jnp.float32), 'beta_out': jnp.zeros((D,), jnp.float32), 'W_u': xavier(ks[3], (2 * D, D)), 'b_u': jnp.full((D,), -1.0, jnp.float32), 'W_r': xavier(ks[4], (2 * D, D)), 'b_r': jnp.zeros((D,), jnp.float32), 'W_n': xavier(ks[5], (2 * D, D)), 'b_n': jnp.zeros((D,), jnp.float32)}
    _L0_xattn_all = _L0_xattn_setup()
    _L0_xattn_in = {k: v for k, v in _L0_xattn_all.items() if k in ('W_proj', 'b_proj', 'g_state', 'beta_state', 'g_input', 'beta_input', 'g_out', 'beta_out', 'W_u', 'b_u', 'W_r', 'b_r', 'W_n', 'b_n')}
    del _L0_xattn_all

    def _L1_xattn_setup():
        import jax, jax.numpy as jnp
        import numpy as np
        B, S, L = (2, 512, 128)
        WIDTH, HEADS, CTX = (256, 16, 192)
        HD = WIDTH // HEADS
        EPS = 1e-05

        def _layernorm(x, g, b):
            m = jnp.mean(x, axis=-1, keepdims=True)
            v = jnp.mean(jnp.square(x - m), axis=-1, keepdims=True)
            return (x - m) * jax.lax.rsqrt(v + EPS) * g + b

        def _mha(q_in, kv_in, wq, bq, wk, bk, wv, bv, wo, bo):
            b = q_in.shape[0]
            q = (q_in @ wq.T + bq).reshape(b, -1, HEADS, HD).transpose(0, 2, 1, 3)
            k = (kv_in @ wk.T + bk).reshape(b, -1, HEADS, HD).transpose(0, 2, 1, 3)
            v = (kv_in @ wv.T + bv).reshape(b, -1, HEADS, HD).transpose(0, 2, 1, 3)
            scores = jnp.einsum('bhqd,bhkd->bhqk', q, k) * HD ** (-0.5)
            p = jax.nn.softmax(scores, axis=-1)
            o = jnp.einsum('bhqk,bhkd->bhqd', p, v)
            o = o.transpose(0, 2, 1, 3).reshape(b, -1, WIDTH)
            return o @ wo.T + bo
        key = jax.random.key(seed)
        ks = jax.random.split(key, 32)

        def xav(k, shape, gain=1.0):
            fan_out, fan_in = shape
            a = gain * np.sqrt(6.0 / (fan_in + fan_out))
            return jax.random.uniform(k, shape, jnp.float32, -a, a)
        g2 = 1.0 / np.sqrt(2.0)
        inp = {'x': jax.random.normal(ks[0], (B, S, WIDTH), jnp.float32), 'context': jax.random.normal(ks[1], (B, L, CTX), jnp.float32), 'ln1_g': jnp.ones((WIDTH,), jnp.float32), 'ln1_b': jnp.zeros((WIDTH,), jnp.float32), 'ln2_g': jnp.ones((WIDTH,), jnp.float32), 'ln2_b': jnp.zeros((WIDTH,), jnp.float32), 'ln3_g': jnp.ones((WIDTH,), jnp.float32), 'ln3_b': jnp.zeros((WIDTH,), jnp.float32), 'sa_wq': xav(ks[2], (WIDTH, WIDTH), g2), 'sa_bq': jnp.zeros((WIDTH,), jnp.float32), 'sa_wk': xav(ks[3], (WIDTH, WIDTH), g2), 'sa_bk': jnp.zeros((WIDTH,), jnp.float32), 'sa_wv': xav(ks[4], (WIDTH, WIDTH), g2), 'sa_bv': jnp.zeros((WIDTH,), jnp.float32), 'sa_wo': xav(ks[5], (WIDTH, WIDTH), 1.0), 'sa_bo': jnp.zeros((WIDTH,), jnp.float32), 'ca_wq': xav(ks[6], (WIDTH, WIDTH), g2), 'ca_bq': jnp.zeros((WIDTH,), jnp.float32), 'ca_wk': xav(ks[7], (WIDTH, CTX), g2), 'ca_bk': jnp.zeros((WIDTH,), jnp.float32), 'ca_wv': xav(ks[8], (WIDTH, CTX), g2), 'ca_bv': jnp.zeros((WIDTH,), jnp.float32), 'ca_wo': xav(ks[9], (WIDTH, WIDTH), 1.0), 'ca_bo': jnp.zeros((WIDTH,), jnp.float32), 'mlp_w1': 0.02 * jax.random.normal(ks[10], (4 * WIDTH, WIDTH), jnp.float32), 'mlp_b1': jnp.zeros((4 * WIDTH,), jnp.float32), 'mlp_w2': 0.02 * jax.random.normal(ks[11], (WIDTH, 4 * WIDTH), jnp.float32), 'mlp_b2': jnp.zeros((WIDTH,), jnp.float32)}
        return inp
    _L1_xattn_all = _L1_xattn_setup()
    _L1_xattn_in = {k: v for k, v in _L1_xattn_all.items() if k in ('ln1_g', 'ln1_b', 'ln2_g', 'ln2_b', 'ln3_g', 'ln3_b', 'sa_wq', 'sa_bq', 'sa_wk', 'sa_bk', 'sa_wv', 'sa_bv', 'sa_wo', 'sa_bo', 'ca_wq', 'ca_bq', 'ca_wk', 'ca_bk', 'ca_wv', 'ca_bv', 'ca_wo', 'ca_bo', 'mlp_w1', 'mlp_b1', 'mlp_w2', 'mlp_b2')}
    del _L1_xattn_all
    return {'x': x, 'ctx_768': ctx_768, 'L0_xattn_W_proj': _L0_xattn_in['W_proj'], 'L0_xattn_b_proj': _L0_xattn_in['b_proj'], 'L0_xattn_g_state': _L0_xattn_in['g_state'], 'L0_xattn_beta_state': _L0_xattn_in['beta_state'], 'L0_xattn_g_input': _L0_xattn_in['g_input'], 'L0_xattn_beta_input': _L0_xattn_in['beta_input'], 'L0_xattn_g_out': _L0_xattn_in['g_out'], 'L0_xattn_beta_out': _L0_xattn_in['beta_out'], 'L0_xattn_W_u': _L0_xattn_in['W_u'], 'L0_xattn_b_u': _L0_xattn_in['b_u'], 'L0_xattn_W_r': _L0_xattn_in['W_r'], 'L0_xattn_b_r': _L0_xattn_in['b_r'], 'L0_xattn_W_n': _L0_xattn_in['W_n'], 'L0_xattn_b_n': _L0_xattn_in['b_n'], 'L1_xattn_ln1_g': _L1_xattn_in['ln1_g'], 'L1_xattn_ln1_b': _L1_xattn_in['ln1_b'], 'L1_xattn_ln2_g': _L1_xattn_in['ln2_g'], 'L1_xattn_ln2_b': _L1_xattn_in['ln2_b'], 'L1_xattn_ln3_g': _L1_xattn_in['ln3_g'], 'L1_xattn_ln3_b': _L1_xattn_in['ln3_b'], 'L1_xattn_sa_wq': _L1_xattn_in['sa_wq'], 'L1_xattn_sa_bq': _L1_xattn_in['sa_bq'], 'L1_xattn_sa_wk': _L1_xattn_in['sa_wk'], 'L1_xattn_sa_bk': _L1_xattn_in['sa_bk'], 'L1_xattn_sa_wv': _L1_xattn_in['sa_wv'], 'L1_xattn_sa_bv': _L1_xattn_in['sa_bv'], 'L1_xattn_sa_wo': _L1_xattn_in['sa_wo'], 'L1_xattn_sa_bo': _L1_xattn_in['sa_bo'], 'L1_xattn_ca_wq': _L1_xattn_in['ca_wq'], 'L1_xattn_ca_bq': _L1_xattn_in['ca_bq'], 'L1_xattn_ca_wk': _L1_xattn_in['ca_wk'], 'L1_xattn_ca_bk': _L1_xattn_in['ca_bk'], 'L1_xattn_ca_wv': _L1_xattn_in['ca_wv'], 'L1_xattn_ca_bv': _L1_xattn_in['ca_bv'], 'L1_xattn_ca_wo': _L1_xattn_in['ca_wo'], 'L1_xattn_ca_bo': _L1_xattn_in['ca_bo'], 'L1_xattn_mlp_w1': _L1_xattn_in['mlp_w1'], 'L1_xattn_mlp_b1': _L1_xattn_in['mlp_b1'], 'L1_xattn_mlp_w2': _L1_xattn_in['mlp_w2'], 'L1_xattn_mlp_b2': _L1_xattn_in['mlp_b2']}

def reference(x, ctx_768, L0_xattn_W_proj, L0_xattn_b_proj, L0_xattn_g_state, L0_xattn_beta_state, L0_xattn_g_input, L0_xattn_beta_input, L0_xattn_g_out, L0_xattn_beta_out, L0_xattn_W_u, L0_xattn_b_u, L0_xattn_W_r, L0_xattn_b_r, L0_xattn_W_n, L0_xattn_b_n, L1_xattn_ln1_g, L1_xattn_ln1_b, L1_xattn_ln2_g, L1_xattn_ln2_b, L1_xattn_ln3_g, L1_xattn_ln3_b, L1_xattn_sa_wq, L1_xattn_sa_bq, L1_xattn_sa_wk, L1_xattn_sa_bk, L1_xattn_sa_wv, L1_xattn_sa_bv, L1_xattn_sa_wo, L1_xattn_sa_bo, L1_xattn_ca_wq, L1_xattn_ca_bq, L1_xattn_ca_wk, L1_xattn_ca_bk, L1_xattn_ca_wv, L1_xattn_ca_bv, L1_xattn_ca_wo, L1_xattn_ca_bo, L1_xattn_mlp_w1, L1_xattn_mlp_b1, L1_xattn_mlp_w2, L1_xattn_mlp_b2):
    import jax
    import jax.numpy as jnp

    def _L0_xattn_ref(prev_states, input_tokens, W_proj, b_proj, g_state, beta_state, g_input, beta_input, g_out, beta_out, W_u, b_u, W_r, b_r, W_n, b_n):
        import jax, jax.numpy as jnp
        import numpy as np
        LN_EPS = 1e-05

        def _ln(x, g, b):
            m = jnp.mean(x, axis=-1, keepdims=True)
            v = jnp.mean((x - m) ** 2, axis=-1, keepdims=True)
            return (x - m) / jnp.sqrt(v + LN_EPS) * g + b
        D = prev_states.shape[-1]
        tok = input_tokens @ W_proj + b_proj
        scores = jnp.einsum('bnd,bsd->bns', prev_states, tok) / jnp.sqrt(jnp.float32(D))
        attn = jax.nn.softmax(scores, axis=-1)
        routed = jnp.einsum('bns,bsd->bnd', attn, tok)
        ps_n = _ln(prev_states, g_state, beta_state)
        in_n = _ln(routed, g_input, beta_input)
        concat = jnp.concatenate([ps_n, in_n], axis=-1)
        u = jax.nn.sigmoid(concat @ W_u + b_u)
        r = jax.nn.sigmoid(concat @ W_r + b_r)
        reset_in = jnp.concatenate([r * ps_n, in_n], axis=-1)
        cand = jnp.tanh(reset_in @ W_n + b_n)
        new_state = (1.0 - u) * prev_states + u * cand
        return _ln(new_state, g_out, beta_out)

    def _L1_xattn_ref(x, context, ln1_g, ln1_b, ln2_g, ln2_b, ln3_g, ln3_b, sa_wq, sa_bq, sa_wk, sa_bk, sa_wv, sa_bv, sa_wo, sa_bo, ca_wq, ca_bq, ca_wk, ca_bk, ca_wv, ca_bv, ca_wo, ca_bo, mlp_w1, mlp_b1, mlp_w2, mlp_b2):
        import jax, jax.numpy as jnp
        import numpy as np
        B, S, L = (2, 512, 128)
        WIDTH, HEADS, CTX = (256, 16, 192)
        HD = WIDTH // HEADS
        EPS = 1e-05

        def _layernorm(x, g, b):
            m = jnp.mean(x, axis=-1, keepdims=True)
            v = jnp.mean(jnp.square(x - m), axis=-1, keepdims=True)
            return (x - m) * jax.lax.rsqrt(v + EPS) * g + b

        def _mha(q_in, kv_in, wq, bq, wk, bk, wv, bv, wo, bo):
            b = q_in.shape[0]
            q = (q_in @ wq.T + bq).reshape(b, -1, HEADS, HD).transpose(0, 2, 1, 3)
            k = (kv_in @ wk.T + bk).reshape(b, -1, HEADS, HD).transpose(0, 2, 1, 3)
            v = (kv_in @ wv.T + bv).reshape(b, -1, HEADS, HD).transpose(0, 2, 1, 3)
            scores = jnp.einsum('bhqd,bhkd->bhqk', q, k) * HD ** (-0.5)
            p = jax.nn.softmax(scores, axis=-1)
            o = jnp.einsum('bhqk,bhkd->bhqd', p, v)
            o = o.transpose(0, 2, 1, 3).reshape(b, -1, WIDTH)
            return o @ wo.T + bo
        h = _layernorm(x, ln1_g, ln1_b)
        x = x + _mha(h, h, sa_wq, sa_bq, sa_wk, sa_bk, sa_wv, sa_bv, sa_wo, sa_bo)
        h = _layernorm(x, ln2_g, ln2_b)
        x = x + _mha(h, context, ca_wq, ca_bq, ca_wk, ca_bk, ca_wv, ca_bv, ca_wo, ca_bo)
        h = _layernorm(x, ln3_g, ln3_b)
        h = jax.nn.gelu(h @ mlp_w1.T + mlp_b1, approximate=False) @ mlp_w2.T + mlp_b2
        return x + h
    x = _L0_xattn_ref(x, ctx_768, L0_xattn_W_proj, L0_xattn_b_proj, L0_xattn_g_state, L0_xattn_beta_state, L0_xattn_g_input, L0_xattn_beta_input, L0_xattn_g_out, L0_xattn_beta_out, L0_xattn_W_u, L0_xattn_b_u, L0_xattn_W_r, L0_xattn_b_r, L0_xattn_W_n, L0_xattn_b_n)
    x = _L1_xattn_ref(x, ctx_768, L1_xattn_ln1_g, L1_xattn_ln1_b, L1_xattn_ln2_g, L1_xattn_ln2_b, L1_xattn_ln3_g, L1_xattn_ln3_b, L1_xattn_sa_wq, L1_xattn_sa_bq, L1_xattn_sa_wk, L1_xattn_sa_bk, L1_xattn_sa_wv, L1_xattn_sa_bv, L1_xattn_sa_wo, L1_xattn_sa_bo, L1_xattn_ca_wq, L1_xattn_ca_bq, L1_xattn_ca_wk, L1_xattn_ca_bk, L1_xattn_ca_wv, L1_xattn_ca_bv, L1_xattn_ca_wo, L1_xattn_ca_bo, L1_xattn_mlp_w1, L1_xattn_mlp_b1, L1_xattn_mlp_w2, L1_xattn_mlp_b2)
    return x

_drawn_inputs = setup_inputs


def setup_inputs(seed=0):
    import zlib

    import numpy as np

    out = dict(_drawn_inputs(seed))
    spreads = {'L0_xattn_b_proj': (0.0, 0.1),
     'L0_xattn_g_state': (1.0, 0.2),
     'L0_xattn_beta_state': (0.0, 0.1),
     'L0_xattn_g_input': (1.0, 0.2),
     'L0_xattn_beta_input': (0.0, 0.1),
     'L0_xattn_g_out': (1.0, 0.2),
     'L0_xattn_beta_out': (0.0, 0.1),
     'L0_xattn_b_u': (-1.0, 0.2),
     'L0_xattn_b_r': (0.0, 0.8),
     'L0_xattn_b_n': (0.0, 0.1),
     'L1_xattn_ln1_g': (1.0, 0.2),
     'L1_xattn_ln1_b': (0.0, 0.1),
     'L1_xattn_ln2_g': (1.0, 0.6),
     'L1_xattn_ln2_b': (0.0, 0.8),
     'L1_xattn_ln3_g': (1.0, 0.6),
     'L1_xattn_ln3_b': (0.0, 0.8),
     'L1_xattn_sa_bq': (0.0, 0.8),
     'L1_xattn_sa_bk': (0.0, 0.8),
     'L1_xattn_sa_bv': (0.0, 0.1),
     'L1_xattn_sa_bo': (0.0, 0.1),
     'L1_xattn_ca_bq': (0.0, 0.8),
     'L1_xattn_ca_bk': (0.0, 0.8),
     'L1_xattn_ca_bv': (0.0, 0.1),
     'L1_xattn_ca_bo': (0.0, 0.1),
     'L1_xattn_mlp_b1': (0.0, 0.1),
     'L1_xattn_mlp_b2': (0.0, 0.1)}
    factors = {}
    for name, (base, spread) in spreads.items():
        noise = np.random.default_rng([zlib.crc32(name.encode()), seed]).standard_normal(out[name].shape)
        drawn = base * np.exp(spread * noise) if base else spread * noise
        out[name] = jnp.asarray(drawn.astype(out[name].dtype))
    for name, factor in factors.items():
        out[name] = (out[name] * factor).astype(out[name].dtype)
    return out
```

```python
from contextlib import ExitStack

import numpy as np

import concourse.bass as bass
from concourse import mybir

F32 = mybir.dt.float32
BF16 = mybir.dt.bfloat16
I32 = mybir.dt.int32
ALU = mybir.AluOpType
ACT = mybir.ActivationFunctionType
AX = mybir.AxisListType.X

P = 128
T = 2048
L = 1601
D = 256
CTX = 192
KC = CTX // 2
TILES = T // P
CHUNK = 512
CHUNKS = T // CHUNK
TPC = CHUNK // P
LT = -(-L // P)
LLAST = L - (LT - 1) * P
HEADS, HD = 16, 16
GROUPS = 4
GH = HEADS // GROUPS
HID = 4 * D
SCALE = HD ** -0.5
SCALE0 = D ** -0.5
EPS = 1e-5
ROWS = 6 * HD
SROW = ROWS
NROW = ROWS + 3
QBLOCK = (0, 0, 0, 1, 1, 2)
KBLOCK = (0, 1, 2, 0, 1, 0)
BOUND = 32.0 / SCALE
AMGM = 64.0
ONES2 = float(np.frombuffer(np.array([0x3F803F80], np.uint32).tobytes(), np.float32)[0])

COLS = ["L0_xattn_b_proj", "L0_xattn_g_state", "L0_xattn_beta_state", "L0_xattn_g_input",
        "L0_xattn_beta_input", "L0_xattn_b_r", "L1_xattn_ln1_g", "L1_xattn_ln1_b",
        "L1_xattn_ln2_g", "L1_xattn_ln2_b", "L1_xattn_ln3_g", "L1_xattn_ln3_b",
        "L1_xattn_sa_bq", "L1_xattn_sa_bk", "L1_xattn_ca_bq", "L1_xattn_ca_bk",
        "L1_xattn_mlp_b1"]
ROWS0 = ["L0_xattn_b_proj", "L0_xattn_b_u", "L0_xattn_b_n", "L0_xattn_g_out", "L0_xattn_beta_out",
         "L1_xattn_ca_bv"]
ROWS1 = ["L1_xattn_sa_bv", "L1_xattn_sa_bo", "L1_xattn_ca_bo", "L1_xattn_mlp_b2"]
NCOL = 2 * (len(COLS) - 1) + HID // P



REST = [
    {"y": [6, 8, 10, 12], "h": [17, 19], "u": [22, 26], "n": [30]},
    {"y": [5, 7, 9, 11], "h": [14, 16], "m": [18, 19, 20, 21, 22, 23, 24, 25], "o": [30, 33, 36, 39]},
]
GELU_STEP = 27


class Map:

    def __init__(self, nc, start, end):
        self.nc, self.at, self.end = nc, start, end

    def region(self, nbytes):
        off = self.at
        self.at += -(-nbytes // 32) * 32
        assert self.at <= self.end, (self.at, self.end)
        return off

    def put(self, name, shape, dt, off):
        return self.nc.alloc_sbuf_tensor_at(name, shape, dt, offset=off)

    def new(self, name, shape, dt):
        size = 2 if dt == BF16 else 4
        return self.put(name, shape, dt, self.region(int(np.prod(shape[1:])) * size))


class Chain:

    def __init__(self, eng, sem):
        self.eng, self.sem, self.base, self.n = eng, sem, 0, 0

    def __call__(self, ins):
        self.n += 1
        ins.then_inc(self.sem, 1)
        self.eng.wait_ge(self.sem, self.base + self.n)


def wait(eng, s, value):
    if not isinstance(value, int) or value > 0:
        eng.wait_ge(s, value)


def pieces(keys):
    return [(n, min(CHUNK, keys - n)) for n in range(0, keys, CHUNK)]


def program(nc, d, out):
    ctx = ExitStack()
    with ctx:
        build(nc, ctx, d, out)


def build(nc, ctx, d, out):
    def sem(name):
        return ctx.enter_context(nc.semaphore(name))

    m = Map(nc, -(-nc.sbuf_base // 32) * 32, nc.sbuf_usable_end)
    ident = m.new("ident", [P, P], F32)
    spread = m.new("spread", [P, P], F32)
    headsum = m.new("headsum", [P, 2, HEADS], F32)
    cols = m.new("cols", [P, NCOL], F32)
    rows1 = m.new("rows1", [P, len(ROWS1), D], F32)
    X = m.new("X", [P, TILES, D], F32)
    small = m.new("small", [P, 256], F32)
    flag = m.new("flag", [1, 2], I32)
    oKST = m.region(HEADS * T * 2)
    oV = m.region(TILES * HEADS * 32 * 4)
    oQST = m.region(HEADS * CHUNK * 2)
    oP = m.region(4 * 2 * CHUNK * 4)
    oON = m.region(GROUPS * CHUNK * 4 + 2 * CHUNK * 4)
    oREC = m.region(CHUNK * 4)
    oWOP = m.region(GROUPS * D * 4)
    oXH = m.region(TPC * D * 4 + 2 * CHUNK * 4)
    Rp = m.new("Rp", [HEADS, 3, CHUNK], BF16)
    W1 = m.new("W1", [P, 2, HID], F32)
    oSCR = m.region(HID // P * CHUNK * 4)

    stack = m.put("stack", [P, HEADS * T], BF16, oKST)
    KST = [stack[:, 0:HEADS * n].rearrange("p (h n) -> p h n", h=HEADS) for n in (T, L + 3)]
    V = m.put("V", [P, TILES, HEADS, 32], F32, oV)
    QST = m.put("QST", [P, HEADS, CHUNK], BF16, oQST)
    PX = m.put("PX", [P, 4, 2, CHUNK], F32, oP)
    ONF = m.put("ONF", [P, GROUPS, CHUNK], F32, oON)
    OT = m.put("OT", [P, 2, CHUNK], F32, oON + GROUPS * CHUNK * 4)
    REC = m.put("REC", [P, CHUNK], F32, oREC)
    WOP = m.put("WOP", [P, GROUPS, D], F32, oWOP)
    XH = m.put("XH", [P, TPC, D], F32, oXH)
    HC = m.put("HC", [P, 2, CHUNK], F32, oXH + TPC * D * 4)
    W2 = m.put("W2", [P, HID // P, D], F32, oKST + -(-HEADS * (L + 3) * 2 // 32) * 32)
    HIDT = m.put("HIDT", [P, HID // P, CHUNK], F32, oSCR)
    s = Map(nc, oSCR, m.at)
    FQ = s.new("FQ", [P, CHUNK], F32)
    FR = s.new("FR", [P, CHUNK], F32)
    SQ = s.new("SQ", [P, 2, CHUNK], F32)
    PARTS = s.new("PARTS", [P, 3, CHUNK], BF16)
    R = s.new("R", [HEADS, CHUNK], F32)
    CAWQ = s.new("CAWQ", [P, 2, D], F32)
    hF = m.put("hF", [P, 2, T], F32, oP)
    SAW = m.put("SAW", [P, 3, 2, D], F32, oXH)
    s = Map(nc, oKST, oV)
    ctxT = s.new("ctxT", [KC, 2, L], F32)
    tokF = s.new("tokF", [P, 2, L], F32)
    tokT = s.new("tokT", [P, LT, D], F32)
    WPJ = s.new("WPJ", [KC, 2, D], F32)
    CAKV = s.new("CAKV", [KC, 2, 2, D], F32)
    PR = s.new("PR", [P, L], F32)
    PT = s.new("PT", [P, LT, P], F32)
    rows0 = s.new("rows0", [P, len(ROWS0), D], F32)
    s = Map(nc, oQST, oP)
    CF = s.new("CF", [P, 2, 4, P], F32)
    XT = s.new("XT", [P, 2, 2, P], F32)
    XHS = s.new("XHS", [P, 2, 2, D], F32)
    XH1 = s.new("XH1", [P, 2, D], F32)
    RPS = s.new("RPS", [P, 2, P], F32)
    TR = s.new("TR", [P, 2, P], F32)
    TU = s.new("TU", [P, D], F32)
    W0 = m.put("W0", [P, 3, 4, D], F32, oON)
    UZ = m.put("UZ", [P, D], F32, oREC)
    CZ = m.put("CZ", [P, D], F32, oREC + D * 4)
    CD = m.put("CD", [P, D], F32, oWOP)
    E1 = m.put("E1", [P, D], F32, oWOP + D * 4)
    E2 = m.put("E2", [P, D], F32, oWOP + 2 * D * 4)
    PS = ctx.enter_context(nc.psum_tensor("PS", [P, 8, CHUNK], F32))
    flat = PS[:, :, :].rearrange("p b n -> p (b n)")

    qd = [nc.dram_tensor(f"q_parts_{a}", [3, D, T], BF16, kind="Internal").ap() for a in range(2)]
    kd = [nc.dram_tensor(f"k_parts_{a}", [3, D, (T, L)[a]], BF16, kind="Internal").ap() for a in range(2)]
    sd = [nc.dram_tensor(f"shift_{a}", [3, HEADS, T], BF16, kind="Internal").ap() for a in range(2)]
    vd = nc.dram_tensor("v_cross", [P, LT * HEADS * 32], F32, kind="Internal").ap()

    def col(name, c=0):
        i = 2 * COLS.index(name) + c
        return cols[:, i:i + 1]

    def row(name):
        if name in ROWS0:
            return rows0[:, ROWS0.index(name), :]
        return rows1[:, ROWS1.index(name), :]

    BRH, NEGM, NEGR, SUM0, RS0, STAT, AG, NVAR, NA, NB, NY, NI = 0, 2, 4, 6, 8, 10, 40, 50, 54, 58, 62, 66
    KM, KMT, NCF, QM, QMT, TB, FM, MX = 70, 80, 82, 84, 92, 94, 96, 128

    def sm(o, n=1, p=P):
        return small[0:p, o:o + n]

    names = """const_loaded x_loaded w0_loaded wproj_loaded ctx_loaded saw_loaded w1_loaded w2_loaded
        v_cleared ones_set half_bias dve_chain dve_stepped pool_stepped
        ctx_unit ctx_unit_taken parts_ready parts_stored squares norms norms_taken shift_ready shift_stored
        v_cross_stored v_cross_loaded
        l0_scores l0_negmax l0_exp l0_pT l0_pT_act l0_pT_dve l0_routed l0_hat l0_hatT l0_concat
        l0_gates l0_rtanh l0_ubiased l0_utanh l0_rps l0_candps l0_candz l0_cand l0_x1hat l0_hT l0_hF
        qkv_unit qkv_unit_taken wop_cleared out_stored""".split()
    S = {n: sem(n) for n in names}
    s_xt = [sem(f"xt_loaded{i}") for i in range(2)]
    per = """scores exp pv heads sums normed y y_taken hat hT hc unit unit_taken gelu mlp
        mlp_taken out_ready flag_row flag wop g_q g_scores g_max g_rows g_split g_stored g_chain""".split()
    A = [{n: sem(f"{('self', 'cross')[a]}_{n}") for n in per} for a in range(2)]
    s_kst = [[sem(f"k_stack{a}_{g}") for g in range(GROUPS)] for a in range(2)]
    s_qst = [[sem(f"q_stack{a}_{g}") for g in range(GROUPS)] for a in range(2)]

    NKS = (TILES, LT)
    KEYS = (T, L)

    def key_rows(a, kt):
        return min(P, KEYS[a] - kt * P)

    CK, SK, SQU, CQ = 0, 2 * CHUNKS, 4 * CHUNKS, 6 * CHUNKS

    units1 = ([("tokF", n, w, mm) for n, w in pieces(L) for mm in range(2)]
              + [("tokT", kt, 0, 0) for kt in range(LT)]
              + [("k", n, w, mm) for n, w in pieces(L) for mm in range(2)]
              + [("v", kt, 0, 0) for kt in range(LT)])
    units3 = ([("k", n, w, mm) for n, w in pieces(T) for mm in range(2)]
              + [("q", n, w, mm) for n, w in pieces(T) for mm in range(2)]
              + [("v", kt, 0, 0) for kt in range(TILES)])

    def events(a, c):
        NK = NKS[a]
        ev = {t: [] for t in range(GROUPS * NK)}
        for g in range(GROUPS):
            if g or c is not None:
                ev[g * NK + 2].append(("sums", g))
        if c is not None:
            for kind, at in REST[a].items():
                for i, t in enumerate(at):
                    ev[t].append((kind, i))
        return ev

    block = ctx.enter_context(nc.Block())

    @block.sync
    def _(sp):
        sp.dma_start(ctxT[:], d["ctxT"].rearrange("(c p) l -> p c l", p=KC)).then_inc(S["ctx_loaded"], 16)
        sp.dma_start(WPJ[:], d["Wproj"].rearrange("(c p) n -> p c n", p=KC)).then_inc(S["wproj_loaded"], 16)
        for i, n in enumerate(("cak", "cav")):
            sp.dma_start(CAKV[:, i], d[n].rearrange("(c p) n -> p c n", p=KC)).then_inc(S["wproj_loaded"], 16)
        sp.dma_start(cols[:], d["cols"]).then_inc(S["const_loaded"], 16)
        for i in range(len(ROWS0)):
            sp.dma_start(rows0[:, i, :], d["rows0"][i, :].partition_broadcast(P)).then_inc(S["const_loaded"], 16)
        for i in range(len(ROWS1)):
            sp.dma_start(rows1[:, i, :], d["rows1"][i, :].partition_broadcast(P)).then_inc(S["const_loaded"], 16)
        sp.dma_start(headsum[:], d["headsum"]).then_inc(S["const_loaded"], 16)
        sp.dma_start(ident[:], d["ident"]).then_inc(S["const_loaded"], 16)
        sp.dma_start(spread[:], d["spread"]).then_inc(S["const_loaded"], 16)
        for i in range(2):
            sp.dma_start(XT[:, i], d["xT"].rearrange("(c p) t -> p c t", p=P)[:, :, i * P:(i + 1) * P]) \
                .then_inc(s_xt[i], 16)
        sp.dma_start(X[:], d["x"].rearrange("(n p) d -> p n d", p=P)).then_inc(S["x_loaded"], 16)
        for i, n in enumerate(("Wu", "Wr", "Wn")):
            sp.dma_start(W0[:, i], d[n].rearrange("(c p) n -> p c n", p=P)).then_inc(S["w0_loaded"], 16)
        for i, n in enumerate(("saq", "sak", "sav")):
            sp.dma_start(SAW[:, i], d[n].rearrange("(c p) n -> p c n", p=P)).then_inc(S["saw_loaded"], 16)
        sp.dma_start(CAWQ[:], d["caq"].rearrange("(c p) n -> p c n", p=P)).then_inc(S["saw_loaded"], 16)
        sp.dma_start(W1[:], d["w1T"].rearrange("(c p) n -> p c n", p=P)).then_inc(S["w1_loaded"], 16)
        with sp.Fori(1, TILES // 2) as k:
            for par in range(2):
                sp.wait_ge(S["l0_scores"], 2 * k - 1 + par)
                sp.dma_start(XT[:, par], d["xT"].rearrange("(c p) t -> p c t", p=P)
                             [:, :, bass.ds((2 * k + par) * P, P)]).then_inc(s_xt[par], 16)
        sp.wait_ge(S["wop_cleared"], 1)
        for j in range(GH):
            sp.dma_start(WOP[32 * j:32 * j + HD, :, :],
                         d["sawo"].rearrange("(g j d) n -> j d g n", g=GROUPS, j=GH)[j]) \
                .then_inc(A[0]["wop"], 16)
        for a in range(2):
            steps = GROUPS * NKS[a]
            sp.wait_ge(S["parts_stored"], 16 * (SK if a else SQU))
            if a == 0:
                sp.wait_ge(S["l0_hF"], TILES)
            else:
                sp.wait_ge(A[0]["scores"], 2 * CHUNKS * GROUPS * NKS[0])
            for g in range(GROUPS):
                for b, part in enumerate(KBLOCK):
                    sp.dma_start(KST[a][b * HD:(b + 1) * HD, g * GH:(g + 1) * GH, 0:KEYS[a]],
                                 kd[a][part, g * GH * HD:(g + 1) * GH * HD, :]
                                 .rearrange("(j d) n -> d j n", j=GH)).then_inc(s_kst[a][g], 16)
            if a == 1:
                sp.wait_ge(A[0]["pv"], CHUNKS * GROUPS * NKS[0])
                sp.wait_ge(S["v_cross_stored"], 16)
                sp.dma_start(V[:, 0:LT].rearrange("p k h e -> p (k h e)"), vd).then_inc(S["v_cross_loaded"], 16)
                sp.dma_start(W2[:], d["w2T"].rearrange("(c p) n -> p c n", p=P)).then_inc(S["w2_loaded"], 16)
                sp.wait_ge(A[0]["y"], CHUNKS * TPC)
                for j in range(GH):
                    sp.dma_start(WOP[32 * j:32 * j + HD, :, :],
                                 d["cawo"].rearrange("(g j d) n -> j d g n", g=GROUPS, j=GH)[j]) \
                        .then_inc(A[1]["wop"], 16)
            sp.wait_ge(S["parts_stored"], 16 * (CQ + 2 * CHUNKS * a))
            sp.wait_ge(S["shift_stored"], 16 * CHUNKS * (a + 1))

            def load_q(c, g, s_to):
                for b, part in enumerate(QBLOCK):
                    sp.dma_start(QST[b * HD:(b + 1) * HD, g * GH:(g + 1) * GH, :],
                                 qd[a][part, g * GH * HD:(g + 1) * GH * HD, bass.ds(c * CHUNK, CHUNK)]
                                 .rearrange("(j d) n -> d j n", j=GH)).then_inc(s_to, 16)

            sp.wait_ge(A[a]["flag"], 1)
            bounded = sp.value_load(flag[0:1, a:a + 1], min_val=0, max_val=1)
            with sp.If(bounded < 1):
                with sp.Fori(0, CHUNKS) as c:
                    for g in range(GROUPS):
                        if g:
                            sp.wait_ge(A[a]["g_max"], (c * GROUPS + g) * GH * TPC)
                        load_q(c, g, A[a]["g_q"])
                    sp.wait_ge(A[a]["g_split"], c + 1)
                    sp.dma_start(sd[a][:, :, bass.ds(c * CHUNK, CHUNK)].rearrange("r h n -> h r n"), Rp[:]) \
                        .then_inc(A[a]["g_stored"], 16)
                sp.wait_ge(A[a]["g_stored"], 16 * CHUNKS)

            def load_stack(c, g, first):
                if not first:
                    sp.wait_ge(A[a]["scores"], ((c - 1) * steps + (g + 1) * NKS[a]) * 2)
                load_q(c, g, s_qst[a][g])
                sp.dma_start(QST[SROW:NROW, g * GH:(g + 1) * GH, :],
                             sd[a][:, g * GH:(g + 1) * GH, bass.ds(c * CHUNK, CHUNK)]).then_inc(s_qst[a][g], 16)

            for g in range(GROUPS):
                load_stack(0, g, True)
            with sp.Fori(1, CHUNKS) as c:
                for g in range(GROUPS):
                    load_stack(c, g, False)

    @block.gpsimd
    def _(gp):
        gp.memset(V[:], 0.0).then_inc(S["v_cleared"], 1)
        gp.wait_ge(S["v_cleared"], 1)
        gp.memset(V[:, :, :, HD:HD + 1], 1.0).then_inc(S["v_cleared"], 1)

        def store_parts(u, dst, n, w, mm):
            gp.wait_ge(S["parts_ready"], u + 1)
            gp.sem_inc(S["pool_stepped"], 1)
            gp.dma_start(dst[:, mm * P:(mm + 1) * P, bass.ds(n, w)].rearrange("r p n -> p r n"),
                         PARTS[:, :, 0:w]).then_inc(S["parts_stored"], 16)

        def store_shift(i, a, n):
            gp.wait_ge(S["shift_ready"], i + 1)
            gp.sem_inc(S["pool_stepped"], 1)
            gp.dma_start(sd[a][:, :, bass.ds(n, CHUNK)].rearrange("r h n -> h r n"), Rp[:]) \
                .then_inc(S["shift_stored"], 16)

        for i, (n, w) in enumerate(pieces(L)):
            for mm in range(2):
                store_parts(CK + 2 * i + mm, kd[1], n, w, mm)
        gp.wait_ge(S["ctx_unit_taken"], len(units1))
        gp.dma_start(vd, V[:, 0:LT].rearrange("p k h e -> p (k h e)")).then_inc(S["v_cross_stored"], 16)
        gp.wait_ge(S["l0_hF"], TILES)
        gp.memset(WOP[:], 0.0).then_inc(S["wop_cleared"], 1)
        gp.wait_ge(S["wop_cleared"], 1)
        gp.memset(stack[SROW:NROW, :].bitcast(F32), ONES2).then_inc(S["ones_set"], 1)
        for i in range(CHUNKS):
            for mm in range(2):
                store_parts(SK + 2 * i + mm, kd[0], i * CHUNK, CHUNK, mm)
        for i in range(CHUNKS):
            for mm in range(2):
                store_parts(SQU + 2 * i + mm, qd[0], i * CHUNK, CHUNK, mm)
            store_shift(i, 0, i * CHUNK)
        with gp.Fori(0, CHUNKS) as c:
            for mm in range(2):
                store_parts(CQ + 2 * c + mm, qd[1], c * CHUNK, CHUNK, mm)
            store_shift(CHUNKS + c, 1, c * CHUNK)
        with gp.Fori(0, CHUNKS) as c:
            for tt in range(TPC):
                gp.wait_ge(A[1]["out_ready"], c * TPC + tt + 1)
                gp.sem_inc(S["pool_stepped"], 1)
                gp.dma_start(out[bass.ds((c * TPC + tt) * P, P), :], XH[:, tt, :]) \
                    .then_inc(S["out_stored"], 16)
        gp.wait_ge(S["out_stored"], 16 * TILES)

    @block.scalar
    def _(act):
        act.wait_ge(S["const_loaded"], 16 * (4 + len(ROWS0) + len(ROWS1)))
        for c in range(2):
            act.mul(sm(BRH + c), col("L0_xattn_b_r", c), 0.5).then_inc(S["half_bias"], 1)
        act.wait_ge(S["half_bias"], 2)

        def l0(i, par, exp, gates, tail):
            if exp:
                act.wait_ge(S["l0_negmax"], i + 1)
                wait(act, S["l0_pT"], 4 * i)
                act.activation(PR[:], flat[:, 0:L], ACT.Exp, bias=sm(NEGM + par), scale=SCALE0,
                               accum_out=sm(SUM0 + par)).then_inc(S["l0_exp"], 1)
            if gates:
                act.wait_ge(S["l0_gates"], i - 1)
                wait(act, S["l0_rps"], i - 2)
                for c in range(2):
                    ins = act.activation(TR[:, c, :], PS[:, 7, c * P:(c + 1) * P], ACT.Tanh,
                                         bias=sm(BRH + c), scale=0.5)
                ins.then_inc(S["l0_rtanh"], 1)
                act.wait_ge(S["l0_ubiased"], i - 1)
                act.activation(TU[:], UZ[:], ACT.Tanh, scale=0.5).then_inc(S["l0_utanh"], 1)
            if exp:
                for k in (0, 2):
                    act.wait_ge(S["l0_pT"], 4 * i + k + 1)
                    act.copy(PT[:, 4 * k:4 * k + 4, :].rearrange("p k q -> p (k q)"), PS[:, 4, :]) \
                        .then_inc(S["l0_pT_act"], 1)
            if gates:
                act.wait_ge(S["l0_candz"], i - 1)
                act.activation(CD[:], CZ[:], ACT.Tanh).then_inc(S["l0_cand"], 1)

        for i in range(4):
            l0(i, i % 2, True, i >= 2, False)
        with act.Fori(2, TILES // 2) as k:
            for par in range(2):
                l0(2 * k + par, par, True, True, False)
        for i in range(TILES, TILES + 2):
            l0(i, i % 2, False, True, True)

        for a in range(2):
            NK, at = NKS[a], A[a]
            steps = GROUPS * NK

            def gelu(q):
                act.wait_ge(at["unit_taken"], HID // P * (q + 1))
                act.activation(HIDT[:], HIDT[:], ACT.Gelu).then_inc(at["gelu"], 1)

            def chunk(c, first):
                for t in range(steps):
                    kr = key_rows(a, t % NK)
                    for half in range(2):
                        h = (c * steps + t) * 2 + half
                        act.wait_ge(at["scores"], h + 1)
                        if half == 0:
                            wait(act, at["pv"], c * steps + t - 1)
                        act.activation(PX[0:kr, (2 * t + half) % 4, :, :], PS[0:kr, 2 * half:2 * half + 2, :],
                                       ACT.Exp, scale=SCALE).then_inc(at["exp"], 1)
                    if a == 1 and t == GELU_STEP and not first:
                        gelu(c - 1)

            chunk(0, True)
            with act.Fori(1, CHUNKS) as c:
                chunk(c, False)
            if a == 1:
                gelu(CHUNKS - 1)

    @block.tensor
    def _(pe):
        def norm(i, w, bank):
            pe.wait_ge(S["squares"], i + 1)
            for mm in range(2):
                ins = pe.matmul(PS[0:HEADS, bank, 0:w], headsum[:, mm, :], SQ[:, mm, 0:w],
                                start=(mm == 0), stop=(mm == 1))
            ins.then_inc(S["norms"], 1)

        pe.wait_ge(S["ctx_loaded"], 16)
        pe.wait_ge(S["wproj_loaded"], 48)
        for u, (kind, n, w, mm) in enumerate(units1):
            wait(pe, S["ctx_unit_taken"], u - 3)
            bank = u % 4
            for c in range(2):
                if kind in ("tokF", "k"):
                    lhs = (WPJ[:, c, mm * P:(mm + 1) * P] if kind == "tokF" else
                           CAKV[:, 0, c, mm * P:(mm + 1) * P])
                    ins = pe.matmul(PS[:, bank, 0:w], lhs, ctxT[:, c, n:n + w], start=(c == 0), stop=(c == 1))
                else:
                    kr = key_rows(1, n)
                    rhs = WPJ[:, c, :] if kind == "tokT" else CAKV[:, 1, c, :]
                    ins = pe.matmul(PS[0:kr, bank, 0:D], ctxT[:, c, n * P:n * P + kr], rhs,
                                    start=(c == 0), stop=(c == 1))
            ins.then_inc(S["ctx_unit"], 1)
            if kind == "k" and mm == 1:
                if u == units1.index(("k", 0, CHUNK, 1)):
                    pe.wait_ge(S["const_loaded"], 16 * (4 + len(ROWS0) + len(ROWS1)))
                wait(pe, S["norms_taken"], n // CHUNK)
                norm(n // CHUNK, w, 6)

        pe.wait_ge(S["ctx_unit_taken"], len(units1))
        pe.wait_ge(S["norms_taken"], CHUNKS)
        pe.wait_ge(S["w0_loaded"], 48)

        def l0(i, par, turn, scores, routed, gates, h):
            if scores:
                pe.wait_ge(s_xt[par], 16 * (turn + 1))
                wait(pe, S["l0_exp"], i)
                for b, (n, w) in enumerate(pieces(L)):
                    for c in range(2):
                        ins = pe.matmul(PS[:, b, 0:w], XT[:, par, c, :], tokF[:, c, n:n + w],
                                        start=(c == 0), stop=(c == 1))
                ins.then_inc(S["l0_scores"], 1)
            if h:
                pe.wait_ge(S["l0_x1hat"], i - 2)
                for c in range(2):
                    ins = pe.transpose(PS[:, 7, c * P:(c + 1) * P], XH1[:, 1 - par, c * P:(c + 1) * P], ident[:])
                ins.then_inc(S["l0_hT"], 1)
            if routed:
                pe.wait_ge(S["l0_pT_act"], 2 * i)
                pe.wait_ge(S["l0_pT_dve"], 2 * i)
                for kt in range(LT):
                    kr = key_rows(1, kt)
                    ins = pe.matmul(PS[:, 6, 0:D], PT[0:kr, kt, :], tokT[0:kr, kt, :],
                                    start=(kt == 0), stop=(kt == LT - 1))
                ins.then_inc(S["l0_routed"], 1)
            if gates:
                pe.wait_ge(S["l0_concat"], i - 1)
                if h:
                    pe.wait_ge(S["l0_hF"], i - 2)
                for mm in range(2):
                    for c in range(4):
                        pe.matmul(PS[:, 7, mm * P:(mm + 1) * P], W0[:, 1, c, mm * P:(mm + 1) * P],
                                  CF[:, par, c, :], start=(c == 0), stop=(c == 3))
                for c in range(4):
                    ins = pe.matmul(PS[:, 7, D:2 * D], CF[:, par, c, :], W0[:, 0, c, :],
                                    start=(c == 0), stop=(c == 3))
                ins.then_inc(S["l0_gates"], 1)
            if scores:
                pe.wait_ge(S["l0_exp"], i + 1)
                for k in range(4):
                    if k >= 2:
                        if k == 2:
                            pe.wait_ge(S["l0_pT_act"], 2 * i + 1)
                        else:
                            pe.wait_ge(S["l0_pT_dve"], 2 * i + 1)
                    for kt in range(4 * k, min(4 * k + 4, LT)):
                        kr = key_rows(1, kt)
                        ins = pe.transpose(PS[0:kr, 4 + k % 2, (kt % 4) * P:(kt % 4 + 1) * P],
                                           PR[:, kt * P:kt * P + kr], ident[:])
                    ins.then_inc(S["l0_pT"], 1)
            if routed:
                pe.wait_ge(S["l0_hat"], i)
                if scores:
                    pe.wait_ge(S["l0_pT_act"], 2 * i + 2)
                for k in range(4):
                    ins = pe.transpose(PS[:, 4, k * P:(k + 1) * P],
                                       XHS[:, 1 - par, k // 2, (k % 2) * P:(k % 2 + 1) * P], ident[:])
                ins.then_inc(S["l0_hatT"], 1)
            if gates:
                pe.wait_ge(S["l0_rps"], i - 1)
                for c in range(4):
                    ins = pe.matmul(PS[:, 6, 0:D], RPS[:, c, :] if c < 2 else CF[:, par, c, :],
                                    W0[:, 2, c, :], start=(c == 0), stop=(c == 3))
                ins.then_inc(S["l0_candps"], 1)

        for i in range(4):
            l0(i, i % 2, i // 2, True, i >= 1, i >= 2, i >= 3)
        with pe.Fori(2, TILES // 2) as k:
            for par in range(2):
                l0(2 * k + par, par, k, True, True, True, True)
        for i in range(TILES, TILES + 3):
            l0(i, i % 2, 0, False, i < TILES + 1, i < TILES + 2, True)

        pe.wait_ge(S["l0_hF"], TILES)
        pe.wait_ge(S["saw_loaded"], 64)
        for u, (kind, n, w, mm) in enumerate(units3):
            wait(pe, S["qkv_unit_taken"], u - 3)
            for c in range(2):
                if kind == "v":
                    ins = pe.matmul(PS[:, u % 4, 0:D], hF[:, c, n * P:(n + 1) * P], SAW[:, 2, c, :],
                                    start=(c == 0), stop=(c == 1))
                else:
                    ins = pe.matmul(PS[:, u % 4, :], SAW[:, "qk".index(kind), c, mm * P:(mm + 1) * P],
                                    hF[:, c, n:n + w], start=(c == 0), stop=(c == 1))
            ins.then_inc(S["qkv_unit"], 1)
            if kind != "v" and mm == 1:
                i = CHUNKS * (1 + "kq".index(kind)) + n // CHUNK
                pe.wait_ge(S["norms_taken"], i)
                norm(i, w, 6)
        pe.wait_ge(S["qkv_unit_taken"], len(units3))
        pe.wait_ge(S["ones_set"], 1)

        for a in range(2):
            NK, at = NKS[a], A[a]
            steps = GROUPS * NK
            pe.wait_ge(at["flag_row"], 1)
            pe.matmul(PS[0:1, 7, 0:HEADS], sm(TB + a, 1, HEADS), ident[0:HEADS, 0:HEADS], start=True,
                      stop=True).then_inc(at["flag_row"], 1)
            pe.wait_ge(at["flag"], 1)
            for g in range(GROUPS):
                pe.wait_ge(s_kst[a][g], 16 * len(KBLOCK))
            bounded = pe.value_load(flag[0:1, a:a + 1], min_val=0, max_val=1)
            with pe.If(bounded < 1):
                with pe.Fori(0, CHUNKS) as c:
                    for g in range(GROUPS):
                        pe.wait_ge(at["g_q"], 16 * len(QBLOCK) * (c * GROUPS + g + 1))
                        for j in range(GH):
                            for tt in range(TPC):
                                if g or j or tt:
                                    pe.wait_ge(at["g_max"], (c * GROUPS + g) * GH * TPC + j * TPC + tt)
                                for b, (n, w) in enumerate(pieces(KEYS[a])):
                                    ins = pe.matmul(PS[:, b, 0:w], QST[0:ROWS, g * GH + j, tt * P:(tt + 1) * P],
                                                    KST[a][0:ROWS, g * GH + j, n:n + w], start=True, stop=True)
                                ins.then_inc(at["g_scores"], 1)
                    pe.wait_ge(at["g_max"], (c + 1) * GROUPS * GH * TPC)
                    for tt in range(TPC):
                        ins = pe.matmul(PS[0:HEADS, 4, tt * P:(tt + 1) * P], sm(MX + tt * HEADS, HEADS),
                                        ident[:], start=True, stop=True)
                    ins.then_inc(at["g_rows"], 1)
                pe.wait_ge(at["g_split"], CHUNKS)
            if a == 1:
                pe.wait_ge(S["v_cross_loaded"], 16)

            def scores(c, t, half, first):
                h = (c * steps + t) * 2 + half
                g, kt = t // NK, t % NK
                kr = key_rows(a, kt)
                if kt == 0 and half == 0:
                    pe.wait_ge(s_qst[a][g], 16 * (len(QBLOCK) + 1) * (c + 1))
                wait(pe, at["exp"], h - 1)
                for jj in range(2):
                    head = g * GH + 2 * half + jj
                    ins = pe.matmul(PS[0:kr, 2 * half + jj, :], KST[a][0:NROW, head, kt * P:kt * P + kr],
                                    QST[0:NROW, head, :], start=True, stop=True)
                ins.then_inc(at["scores"], 1)

            def pv(c, t):
                g, kt = t // NK, t % NK
                kr = key_rows(a, kt)
                pe.wait_ge(at["exp"], (c * steps + t) * 2 + 2)
                if kt == 0:
                    wait(pe, at["heads"], c * GROUPS + g - 1)
                for j in range(GH):
                    ins = pe.matmul(PS[32 * j:32 * j + 32, 4 + g % 2, :], V[0:kr, kt, g * GH + j, :],
                                    PX[0:kr, (2 * t + j // 2) % 4, j % 2, :],
                                    start=(kt == 0), stop=(kt == NK - 1))
                ins.then_inc(at["pv"], 1)

            def sums(c, g):
                u = c * GROUPS + g - 1
                pe.wait_ge(at["heads"], u + 1)
                wait(pe, at["normed"], u)
                pe.matmul(PS[:, 6, :], spread[:], OT[:, (g - 1) % 2, :], start=True, stop=True) \
                    .then_inc(at["sums"], 1)

            def piece(kind, i, q):
                if kind == "y":
                    if i == 0:
                        pe.wait_ge(at["normed"], (q + 1) * GROUPS)
                        pe.wait_ge(at["wop"], 16 * GH)
                    else:
                        pe.wait_ge(at["y_taken"], q * TPC + i)
                    for g in range(GROUPS):
                        ins = pe.matmul(PS[:, 7, 0:D], ONF[:, g, i * P:(i + 1) * P], WOP[:, g, :],
                                        start=(g == 0), stop=(g == GROUPS - 1))
                    ins.then_inc(at["y"], 1)
                if kind == "h":
                    pe.wait_ge(at["hat"], q + 1)
                    if i == 1:
                        pe.wait_ge(at["hc"], 2 * q + 1)
                    for tt in range(TPC):
                        ins = pe.transpose(PS[:, 7, tt * P:(tt + 1) * P], XH[:, tt, i * P:(i + 1) * P], ident[:])
                    ins.then_inc(at["hT"], 1)
                if kind == "u":
                    pe.wait_ge(at["hc"], 2 * q + 2)
                    if i:
                        pe.wait_ge(at["unit_taken"], 2 * q + i)
                    for c in range(2):
                        ins = pe.matmul(PS[:, 7, :], CAWQ[:, c, i * P:(i + 1) * P], HC[:, c, :],
                                        start=(c == 0), stop=(c == 1))
                    ins.then_inc(at["unit"], 1)
                if kind == "n":
                    norm(3 * CHUNKS + q, CHUNK, 7)
                if kind == "m":
                    pe.wait_ge(at["hc"], 2 * q + 2)
                    if i:
                        pe.wait_ge(at["unit_taken"], HID // P * q + i)
                    for c in range(2):
                        ins = pe.matmul(PS[:, 7, :], W1[:, c, i * P:(i + 1) * P], HC[:, c, :],
                                        start=(c == 0), stop=(c == 1))
                    ins.then_inc(at["unit"], 1)
                if kind == "o":
                    pe.wait_ge(at["gelu"], q + 1)
                    if i:
                        pe.wait_ge(at["mlp_taken"], q * TPC + i)
                    for k in range(HID // P):
                        ins = pe.matmul(PS[:, 7, 0:D], HIDT[:, k, i * P:(i + 1) * P], W2[:, k, :],
                                        start=(k == 0), stop=(k == HID // P - 1))
                    ins.then_inc(at["mlp"], 1)

            if a == 1:
                pe.wait_ge(S["w1_loaded"], 16)
                pe.wait_ge(S["w2_loaded"], 16)

            def chunk(c, first):
                ev = events(a, None if first else c)
                scores(c, 0, 0, first)
                for t in range(steps):
                    scores(c, t, 1, first)
                    if t:
                        pv(c, t - 1)
                    elif not first:
                        pv(c - 1, steps - 1)
                    for kind, i in ev[t]:
                        if kind == "sums":
                            sums(c, i)
                        else:
                            piece(kind, i, c - 1)
                    if t + 1 < steps:
                        scores(c, t + 1, 0, first)

            chunk(0, True)
            with pe.Fori(1, CHUNKS) as c:
                chunk(c, False)
            pv(CHUNKS - 1, steps - 1)
            sums(CHUNKS, 0)
            for kind, at_steps in REST[a].items():
                for i in range(len(at_steps)):
                    piece(kind, i, CHUNKS - 1)

    @block.vector
    def _(ve):
        ch = Chain(ve, S["dve_chain"])

        def rsqrt(n, link):
            v, a_, b_, y = sm(NVAR, n), sm(NA, n), sm(NB, n), sm(NY, n)
            link(ve.tensor_scalar(v, v, EPS, None, ALU.add))
            link(ve.tensor_scalar(sm(NI, n).bitcast(I32), v.bitcast(I32), 1, None, ALU.logical_shift_right))
            link(ve.tensor_scalar(y.bitcast(I32), sm(NI, n).bitcast(I32), -1.0, float(0x5f3759df),
                                  ALU.mult, ALU.add))
            for _ in range(3):
                link(ve.tensor_tensor(a_, y, y, ALU.mult))
                link(ve.scalar_tensor_tensor(out=b_, in0=a_, scalar=-0.5, in1=v, op0=ALU.mult, op1=ALU.mult))
                link(ve.scalar_tensor_tensor(out=y, in0=b_, scalar=1.5, in1=y, op0=ALU.add, op1=ALU.mult))

        def stats(src, i, link):
            ve.sem_inc(S["dve_stepped"], 1)
            link(ve.bn_stats(sm(STAT + 6 * i, 6), src))
            ve.sem_inc(S["dve_stepped"], 1)
            link(ve.bn_aggr(sm(AG + 2 * i, 2), sm(STAT + 6 * i, 6)))
            link(ve.tensor_copy(sm(NVAR + i), sm(AG + 2 * i + 1)))

        def three(dst, src, tmp, link):
            link(ve.tensor_copy(dst[0], src))
            link(ve.tensor_tensor(tmp, src, dst[0], ALU.subtract))
            link(ve.tensor_copy(dst[1], tmp))
            return ve.tensor_tensor(dst[2], tmp, dst[1], ALU.subtract)

        def parts(i, w, mm):
            u = 2 * i + mm
            wait(ve, S["parts_stored"], 16 * u)
            three([PARTS[:, r, 0:w] for r in range(3)], FQ[:, 0:w], FR[:, 0:w], ch) \
                .then_inc(S["parts_ready"], 1)
            ve.wait_ge(S["parts_ready"], u + 1)
            ins = ve.tensor_tensor(SQ[:, mm, 0:w], FQ[:, 0:w], FQ[:, 0:w], ALU.mult)
            if mm == 0:
                ch(ins)
            else:
                ins.then_inc(S["squares"], 1)
                ve.wait_ge(S["squares"], i + 1)

        def k_norm(i, a, n, w):
            ve.wait_ge(S["norms"], i + 1)
            ve.tensor_reduce(sm(KM + 4 * a + n, 1, HEADS), PS[0:HEADS, 6, 0:w], AX, ALU.max) \
                .then_inc(S["norms_taken"], 1)
            ve.wait_ge(S["norms_taken"], i + 1)
            if n == CHUNKS - 1:
                ch(ve.tensor_reduce(sm(KMT + a, 1, HEADS), sm(KM + 4 * a, 4, HEADS), AX, ALU.max))
                ch(ve.tensor_scalar(sm(NCF + a, 1, HEADS), sm(KMT + a, 1, HEADS), -1.0 / (2 * AMGM), None,
                                    ALU.mult))

        def q_norm(i, a, n, bank):
            ve.wait_ge(S["norms"], i + 1)
            ch(ve.tensor_scalar(R[:], PS[0:HEADS, bank, :], sm(NCF + a, 1, HEADS), -AMGM / 2,
                                ALU.mult, ALU.add))
            ve.tensor_reduce(small[0:HEADS, bass.ds(QM + n, 1)], PS[0:HEADS, bank, :], AX, ALU.max) \
                .then_inc(S["norms_taken"], 1)
            ve.wait_ge(S["norms_taken"], i + 1)
            wait(ve, S["shift_stored"], 16 * (i - 2 * CHUNKS))
            three([Rp[:, r, :] for r in range(3)], R[:], FR[0:HEADS, :], ch).then_inc(S["shift_ready"], 1)
            ve.wait_ge(S["shift_ready"], i - 2 * CHUNKS + 1)

        ve.wait_ge(S["const_loaded"], 16 * (4 + len(ROWS0) + len(ROWS1)))
        for u, (kind, n, w, mm) in enumerate(units1):
            ve.wait_ge(S["ctx_unit"], u + 1)
            bank = u % 4
            if kind == "tokF":
                ve.tensor_scalar(tokF[:, mm, n:n + w], PS[:, bank, 0:w], col("L0_xattn_b_proj", mm), None,
                                 ALU.add).then_inc(S["ctx_unit_taken"], 1)
                ve.wait_ge(S["ctx_unit_taken"], u + 1)
            elif kind == "tokT":
                kr = key_rows(1, n)
                ve.tensor_tensor(tokT[0:kr, n, :], PS[0:kr, bank, 0:D], row("L0_xattn_b_proj")[0:kr],
                                 ALU.add).then_inc(S["ctx_unit_taken"], 1)
                ve.wait_ge(S["ctx_unit_taken"], u + 1)
            elif kind == "v":
                kr = key_rows(1, n)
                if n == 0:
                    ve.wait_ge(S["v_cleared"], 2)
                ve.tensor_tensor(V[0:kr, n, :, 0:HD],
                                 PS[0:kr, bank, 0:D].rearrange("p (h e) -> p h e", h=HEADS),
                                 row("L1_xattn_ca_bv")[0:kr].rearrange("p (h e) -> p h e", h=HEADS),
                                 ALU.add).then_inc(S["ctx_unit_taken"], 1)
                ve.wait_ge(S["ctx_unit_taken"], u + 1)
            else:
                ve.tensor_scalar(FQ[:, 0:w], PS[:, bank, 0:w], col("L1_xattn_ca_bk", mm), None, ALU.add) \
                    .then_inc(S["ctx_unit_taken"], 1)
                ve.wait_ge(S["ctx_unit_taken"], u + 1)
                parts(CK // 2 + n // CHUNK, w, mm)
                if mm == 1:
                    k_norm(n // CHUNK, 1, n // CHUNK, w)
        ve.wait_ge(S["ctx_unit_taken"], len(units1))
        ve.wait_ge(S["x_loaded"], 16)

        def l0(i, par, scores, routed, gates, h):
            if scores:
                ve.wait_ge(S["l0_scores"], i + 1)
                ch(ve.tensor_reduce(sm(NEGR + par), flat[:, 0:L], AX, ALU.max, negate=True))
                ve.tensor_scalar(sm(NEGM + par), sm(NEGR + par), SCALE0, None, ALU.mult) \
                    .then_inc(S["l0_negmax"], 1)
                ve.wait_ge(S["l0_negmax"], i + 1)
            if h:
                ve.wait_ge(S["l0_hT"], i - 2)
                for c in range(2):
                    ins = ve.tensor_scalar(hF[:, c, bass.ds((i - 3) * P, P)], PS[:, 7, c * P:(c + 1) * P],
                                           col("L1_xattn_ln1_g", c), col("L1_xattn_ln1_b", c),
                                           ALU.mult, ALU.add)
                ins.then_inc(S["l0_hF"], 1)
                ve.wait_ge(S["l0_hF"], i - 2)
            if routed:
                ve.wait_ge(S["l0_routed"], i)
                ch(ve.reciprocal(sm(RS0), sm(SUM0 + 1 - par)))
                ch(ve.tensor_scalar(E1[:], PS[:, 6, 0:D], sm(RS0), None, ALU.mult))
                xt = X[:, bass.ds(i - 1, 1), :].rearrange("p o d -> p (o d)")
                stats(xt, 0, ch)
                stats(E1[:], 1, ch)
                rsqrt(2, ch)
                ve.tensor_scalar(XHS[:, 1 - par, 0, :], xt, sm(AG), sm(NY), ALU.subtract, ALU.mult)
                ve.tensor_scalar(XHS[:, 1 - par, 1, :], E1[:], sm(AG + 2), sm(NY + 1), ALU.subtract,
                                 ALU.mult).then_inc(S["l0_hat"], 1)
                ve.wait_ge(S["l0_hat"], i)
            if gates:
                ve.wait_ge(S["l0_rtanh"], i - 1)
                ve.tensor_tensor(UZ[:], PS[:, 7, D:2 * D], row("L0_xattn_b_u"), ALU.add) \
                    .then_inc(S["l0_ubiased"], 1)
                ve.wait_ge(S["l0_ubiased"], i - 1)
                ch(ve.tensor_scalar(RPS[:], TR[:], 0.5, 0.5, ALU.mult, ALU.add))
                ve.tensor_tensor(RPS[:], RPS[:], CF[:, par, 0:2, :], ALU.mult).then_inc(S["l0_rps"], 1)
                ve.wait_ge(S["l0_rps"], i - 1)
            if scores:
                ve.wait_ge(S["l0_pT"], 4 * i + 2)
                ve.tensor_copy(PT[:, 4:8, :].rearrange("p k q -> p (k q)"), PS[:, 5, :]) \
                    .then_inc(S["l0_pT_dve"], 1)
                ve.wait_ge(S["l0_pT_dve"], 2 * i + 1)
                ve.wait_ge(S["l0_pT"], 4 * i + 4)
                ve.tensor_copy(PT[0:LLAST, LT - 1, :], PS[0:LLAST, 5, 0:P]).then_inc(S["l0_pT_dve"], 1)
                ve.wait_ge(S["l0_pT_dve"], 2 * i + 2)
            if routed:
                ve.wait_ge(S["l0_hatT"], i)
                for k, (g_, b_) in enumerate(2 * [("L0_xattn_g_state", "L0_xattn_beta_state")]
                                             + 2 * [("L0_xattn_g_input", "L0_xattn_beta_input")]):
                    ins = ve.tensor_scalar(CF[:, 1 - par, k, :], PS[:, 4, k * P:(k + 1) * P],
                                           col(g_, k % 2), col(b_, k % 2), ALU.mult, ALU.add)
                ins.then_inc(S["l0_concat"], 1)
                ve.wait_ge(S["l0_concat"], i)
            if gates:
                ve.wait_ge(S["l0_candps"], i - 1)
                ve.tensor_tensor(CZ[:], PS[:, 6, 0:D], row("L0_xattn_b_n"), ALU.add) \
                    .then_inc(S["l0_candz"], 1)
                ve.wait_ge(S["l0_candz"], i - 1)
                ve.wait_ge(S["l0_cand"], i - 1)
                xt = X[:, bass.ds(i - 2, 1), :].rearrange("p o d -> p (o d)")
                ch(ve.tensor_tensor(E2[:], CD[:], xt, ALU.subtract))
                ch(ve.scalar_tensor_tensor(out=E2[:], in0=TU[:], scalar=1.0, in1=E2[:],
                                           op0=ALU.add, op1=ALU.mult))
                ch(ve.scalar_tensor_tensor(out=E2[:], in0=E2[:], scalar=0.5, in1=xt,
                                           op0=ALU.mult, op1=ALU.add))
                stats(E2[:], 0, ch)
                rsqrt(1, ch)
                ch(ve.tensor_scalar(E2[:], E2[:], sm(AG), sm(NY), ALU.subtract, ALU.mult))
                ch(ve.tensor_tensor(E2[:], E2[:], row("L0_xattn_g_out"), ALU.mult))
                ch(ve.tensor_tensor(xt, E2[:], row("L0_xattn_beta_out"), ALU.add))
                stats(xt, 0, ch)
                rsqrt(1, ch)
                ve.tensor_scalar(XH1[:, par, :], xt, sm(AG), sm(NY), ALU.subtract, ALU.mult) \
                    .then_inc(S["l0_x1hat"], 1)
                ve.wait_ge(S["l0_x1hat"], i - 1)

        for i in range(4):
            l0(i, i % 2, True, i >= 1, i >= 2, i >= 3)
        per_tile = 58
        before = ch.n
        with ve.Fori(2, TILES // 2) as k:
            for par in range(2):
                ch.base, ch.n = before + (2 * k + par - 4) * per_tile, 0
                l0(2 * k + par, par, True, True, True, True)
                assert ch.n == per_tile, ch.n
        ch.base, ch.n = 0, before + (TILES - 4) * per_tile
        for i in range(TILES, TILES + 3):
            l0(i, i % 2, False, i < TILES + 1, i < TILES + 2, True)

        for u, (kind, n, w, mm) in enumerate(units3):
            ve.wait_ge(S["qkv_unit"], u + 1)
            if kind == "v":
                if n == 0:
                    ve.wait_ge(S["v_cross_stored"], 16)
                ve.tensor_tensor(V[:, n, :, 0:HD],
                                 PS[:, u % 4, 0:D].rearrange("p (h e) -> p h e", h=HEADS),
                                 row("L1_xattn_sa_bv").rearrange("p (h e) -> p h e", h=HEADS),
                                 ALU.add).then_inc(S["qkv_unit_taken"], 1)
                ve.wait_ge(S["qkv_unit_taken"], u + 1)
                continue
            ve.tensor_scalar(FQ[:], PS[:, u % 4, :], col("L1_xattn_sa_b" + kind, mm), None, ALU.add) \
                .then_inc(S["qkv_unit_taken"], 1)
            ve.wait_ge(S["qkv_unit_taken"], u + 1)
            parts((SK if kind == "k" else SQU) // 2 + n // CHUNK, w, mm)
            if mm == 1 and kind == "k":
                k_norm(CHUNKS + n // CHUNK, 0, n // CHUNK, w)
            elif mm == 1:
                q_norm(2 * CHUNKS + n // CHUNK, 0, n // CHUNK, 6)

        for a in range(2):
            NK, at = NKS[a], A[a]
            ve.wait_ge(S["norms_taken"], (3 + a) * CHUNKS)
            ch(ve.tensor_reduce(sm(QMT, 1, HEADS), sm(QM, CHUNKS, HEADS), AX, ALU.max))
            ve.tensor_tensor(sm(TB + a, 1, HEADS), sm(QMT, 1, HEADS), sm(KMT + a, 1, HEADS), ALU.mult) \
                .then_inc(at["flag_row"], 1)
            ve.wait_ge(at["flag_row"], 2)
            ch(ve.tensor_reduce(sm(FM, 1, 1), PS[0:1, 7, 0:HEADS], AX, ALU.max))
            ve.tensor_scalar(flag[0:1, a:a + 1], sm(FM, 1, 1), BOUND * BOUND, None, ALU.is_le) \
                .then_inc(at["flag"], 1)
            ve.wait_ge(at["flag"], 1)
            bounded = ve.value_load(flag[0:1, a:a + 1], min_val=0, max_val=1)
            with ve.If(bounded < 1):
                gch = Chain(ve, at["g_chain"])
                with ve.Fori(0, CHUNKS) as c:
                    gch.base, gch.n = c * 3, 0
                    for g in range(GROUPS):
                        for j in range(GH):
                            for tt in range(TPC):
                                n = (c * GROUPS + g) * GH * TPC + j * TPC + tt
                                ve.wait_ge(at["g_scores"], n + 1)
                                ve.tensor_reduce(sm(MX + tt * HEADS + g * GH + j), flat[:, 0:KEYS[a]], AX,
                                                 ALU.max, negate=True).then_inc(at["g_max"], 1)
                                ve.wait_ge(at["g_max"], n + 1)
                    ve.wait_ge(at["g_rows"], c + 1)
                    three([Rp[:, r, :] for r in range(3)], PS[0:HEADS, 4, :], FR[0:HEADS, :], gch) \
                        .then_inc(at["g_split"], 1)
                    ve.wait_ge(at["g_split"], c + 1)
                    ve.wait_ge(at["g_stored"], 16 * (c + 1))

            def sums(c, g):
                u = c * GROUPS + g - 1
                par = (g - 1) % 2
                ve.wait_ge(at["pv"], (u + 1) * NK)
                ve.tensor_copy(OT[:, par, :], PS[:, 4 + par, :]).then_inc(at["heads"], 1)
                ve.wait_ge(at["heads"], u + 1)
                ve.wait_ge(at["sums"], u + 1)
                ch(ve.reciprocal(REC[:], PS[:, 6, :]))
                if g == 1 and not isinstance(c, int):
                    ve.wait_ge(at["y"], c * TPC)
                ve.tensor_tensor(ONF[:, (g - 1) % GROUPS, :], OT[:, par, :], REC[:], ALU.mult) \
                    .then_inc(at["normed"], 1)
                ve.wait_ge(at["normed"], u + 1)

            def piece(kind, i, q):
                if kind in "yo":
                    xt = X[:, bass.ds(q * TPC + i, 1), :].rearrange("p o d -> p (o d)")
                if kind == "y":
                    ve.wait_ge(at["y"], q * TPC + i + 1)
                    ve.tensor_tensor(XH[:, i, :], PS[:, 7, 0:D], row(("L1_xattn_sa_bo", "L1_xattn_ca_bo")[a]),
                                     ALU.add).then_inc(at["y_taken"], 1)
                    ve.wait_ge(at["y_taken"], q * TPC + i + 1)
                    ch(ve.tensor_tensor(xt, XH[:, i, :], xt, ALU.add))
                    stats(xt, i, ch)
                    if i == TPC - 1:
                        rsqrt(TPC, ch)
                        for tt in range(TPC):
                            ins = ve.tensor_scalar(
                                XH[:, tt, :], X[:, bass.ds(q * TPC + tt, 1), :].rearrange("p o d -> p (o d)"),
                                sm(AG + 2 * tt), sm(NY + tt), ALU.subtract, ALU.mult)
                        ins.then_inc(at["hat"], 1)
                        ve.wait_ge(at["hat"], q + 1)
                if kind == "h":
                    ln = ("L1_xattn_ln2_", "L1_xattn_ln3_")[a]
                    ve.wait_ge(at["hT"], 2 * q + i + 1)
                    ve.tensor_scalar(HC[:, i, :], PS[:, 7, :], col(ln + "g", i), col(ln + "b", i),
                                     ALU.mult, ALU.add).then_inc(at["hc"], 1)
                    ve.wait_ge(at["hc"], 2 * q + i + 1)
                if kind == "u":
                    ve.wait_ge(at["unit"], 2 * q + i + 1)
                    ve.tensor_scalar(FQ[:], PS[:, 7, :], col("L1_xattn_ca_bq", i), None, ALU.add) \
                        .then_inc(at["unit_taken"], 1)
                    ve.wait_ge(at["unit_taken"], 2 * q + i + 1)
                    parts(CQ // 2 + q, CHUNK, i)
                if kind == "n":
                    q_norm(3 * CHUNKS + q, 1, q, 7)
                if kind == "m":
                    ve.wait_ge(at["unit"], HID // P * q + i + 1)
                    ve.tensor_scalar(HIDT[:, i, :], PS[:, 7, :], col("L1_xattn_mlp_b1", i), None, ALU.add) \
                        .then_inc(at["unit_taken"], 1)
                    ve.wait_ge(at["unit_taken"], HID // P * q + i + 1)
                if kind == "o":
                    ve.wait_ge(at["mlp"], q * TPC + i + 1)
                    ve.tensor_tensor(XH[:, i, :], PS[:, 7, 0:D], row("L1_xattn_mlp_b2"), ALU.add) \
                        .then_inc(at["mlp_taken"], 1)
                    ve.wait_ge(at["mlp_taken"], q * TPC + i + 1)
                    ve.tensor_tensor(XH[:, i, :], XH[:, i, :], xt, ALU.add).then_inc(at["out_ready"], 1)
                    ve.wait_ge(at["out_ready"], q * TPC + i + 1)

            def chunk(c, first):
                ev = events(a, None if first else c)
                for t in range(GROUPS * NK):
                    for kind, i in ev[t]:
                        if kind == "sums":
                            sums(c, i)
                        else:
                            piece(kind, i, c - 1)
                if a == 1 and not first:
                    ve.wait_ge(S["out_stored"], 16 * TPC * c)

            chunk(0, True)
            before = ch.n
            per_chunk = (43, 32)[a]
            with ve.Fori(1, CHUNKS) as c:
                ch.base, ch.n = before + (c - 1) * per_chunk, 0
                chunk(c, False)
                assert ch.n == per_chunk, ch.n
            ch.base, ch.n = 0, before + (CHUNKS - 1) * per_chunk
            sums(CHUNKS, 0)
            for kind, at_steps in REST[a].items():
                for i in range(len(at_steps)):
                    piece(kind, i, CHUNKS - 1)


INPUTS = ["x", "xT", "ctxT", "Wproj", "Wu", "Wr", "Wn", "saq", "sak", "sav", "caq", "cak", "cav",
          "sawo", "cawo", "w1T", "w2T", "cols", "rows0", "rows1", "headsum", "ident", "spread"]


def kernel(**inputs):
    import numpy as _np
    import concourse.bacc as _bacc
    from concourse import mybir as _mybir
    from concourse.bass_utils import run_bass_kernel_spmd as _run

    v = {n: _np.asarray(a) for n, a in inputs.items()}
    x, c = v["x"][0], v["ctx_768"][0]
    data = {
        "x": x, "xT": x.T, "ctxT": c.T, "Wproj": v["L0_xattn_W_proj"],
        "Wu": v["L0_xattn_W_u"], "Wr": v["L0_xattn_W_r"], "Wn": v["L0_xattn_W_n"],
        "saq": v["L1_xattn_sa_wq"].T, "sak": v["L1_xattn_sa_wk"].T, "sav": v["L1_xattn_sa_wv"].T,
        "caq": v["L1_xattn_ca_wq"].T, "cak": v["L1_xattn_ca_wk"].T, "cav": v["L1_xattn_ca_wv"].T,
        "sawo": v["L1_xattn_sa_wo"].T, "cawo": v["L1_xattn_ca_wo"].T,
        "w1T": v["L1_xattn_mlp_w1"].T, "w2T": v["L1_xattn_mlp_w2"].T,
        "cols": _np.concatenate([v[n].reshape(-1, P).T for n in COLS], 1),
        "rows0": _np.stack([v[n] for n in ROWS0]),
        "rows1": _np.stack([v[n] for n in ROWS1]),
    }
    headsum = _np.zeros((P, 2, HEADS), _np.float32)
    spread = _np.zeros((P, P), _np.float32)
    for p in range(P):
        for half in range(2):
            headsum[p, half, 8 * half + p // HD] = 1.0
        spread[32 * (p // 32) + HD, p] = 1.0
    data.update(headsum=headsum, spread=spread, ident=_np.eye(P, dtype=_np.float32))

    nc = _bacc.Bacc("TRN2", target_bir_lowering=False, num_devices=1)
    arrays, d = {}, {}
    for n in INPUTS:
        a = _np.ascontiguousarray(data[n])
        arrays[f"in_{n}"] = a
        d[n] = nc.dram_tensor(f"in_{n}", a.shape, _mybir.dt.from_np(a.dtype), kind="ExternalInput").ap()
    out = nc.dram_tensor("out", (T, D), _mybir.dt.float32, kind="ExternalOutput").ap()
    program(nc, d, out)
    r = _run(nc, [arrays], core_ids=[0])
    return r.results[0]["out"].reshape(1, T, D)
```

```python
from contextlib import ExitStack

import numpy as np

import concourse.bass as bass
from concourse import mybir

F32 = mybir.dt.float32
BF16 = mybir.dt.bfloat16
I32 = mybir.dt.int32
ALU = mybir.AluOpType
ACT = mybir.ActivationFunctionType
AX = mybir.AxisListType.X

P = 128
T = 2048
L = 1601
D = 256
CTX = 192
KC = CTX // 2
TILES = T // P
CHUNK = 512
CHUNKS = T // CHUNK
TPC = CHUNK // P
LT = -(-L // P)
LLAST = L - (LT - 1) * P
HEADS, HD = 16, 16
GROUPS = 4
GH = HEADS // GROUPS
HID = 4 * D
SCALE = HD ** -0.5
SCALE0 = D ** -0.5
EPS = 1e-5
ROWS = 6 * HD
SROW = ROWS
NROW = ROWS + 3
QBLOCK = (0, 0, 0, 1, 1, 2)
KBLOCK = (0, 1, 2, 0, 1, 0)
BOUND = 32.0 / SCALE
AMGM = 64.0

COLS = ["L0_xattn_b_proj", "L0_xattn_g_state", "L0_xattn_beta_state", "L0_xattn_g_input",
        "L0_xattn_beta_input", "L0_xattn_b_r", "L1_xattn_ln1_g", "L1_xattn_ln1_b",
        "L1_xattn_ln2_g", "L1_xattn_ln2_b", "L1_xattn_ln3_g", "L1_xattn_ln3_b",
        "L1_xattn_sa_bq", "L1_xattn_sa_bk", "L1_xattn_ca_bq", "L1_xattn_ca_bk",
        "L1_xattn_mlp_b1"]
ROWS0 = ["L0_xattn_b_proj", "L0_xattn_b_u", "L0_xattn_b_n", "L0_xattn_g_out", "L0_xattn_beta_out",
         "L1_xattn_ca_bv"]
ROWS1 = ["L1_xattn_sa_bv", "L1_xattn_sa_bo", "L1_xattn_ca_bo", "L1_xattn_mlp_b2"]
NCOL = 2 * (len(COLS) - 1) + HID // P



PARTS_OF = {"y": 2, "h": 1, "u": 2, "n": 2, "m": 2, "o": 4}
REST = [
    {"y": [5, 6, 8, 9, 11, 12, 14, 15], "h": [21, 23], "u": [26, 28, 30, 32], "n": [38, 40]},
    {"y": list(range(5, 13)), "h": [17, 18], "m": list(range(19, 27)) + list(range(29, 35)) + [35, 35],
     "o": [37, 38, 39, 40, 42, 42, 43, 44, 45, 45, 46, 47, 48, 48, 49, 50]},
]
HAT_STEP = (16, 13)
GELU_STEP = 36
LOOK = 3


class Map:

    def __init__(self, nc, start, end):
        self.nc, self.at, self.end = nc, start, end

    def region(self, nbytes):
        off = self.at
        self.at += -(-nbytes // 32) * 32
        assert self.at <= self.end, (self.at, self.end)
        return off

    def put(self, name, shape, dt, off):
        return self.nc.alloc_sbuf_tensor_at(name, shape, dt, offset=off)

    def new(self, name, shape, dt):
        size = 2 if dt == BF16 else 4
        return self.put(name, shape, dt, self.region(int(np.prod(shape[1:])) * size))


class Chain:

    def __init__(self, eng, sem):
        self.eng, self.sem, self.base, self.n = eng, sem, 0, 0

    def __call__(self, ins):
        self.n += 1
        ins.then_inc(self.sem, 1)
        self.eng.wait_ge(self.sem, self.base + self.n)


def wait(eng, s, value):
    if not isinstance(value, int) or value > 0:
        eng.wait_ge(s, value)


def pieces(keys):
    return [(n, min(CHUNK, keys - n)) for n in range(0, keys, CHUNK)]


def program(nc, d, out):
    ctx = ExitStack()
    with ctx:
        build(nc, ctx, d, out)


def build(nc, ctx, d, out):
    def sem(name):
        return ctx.enter_context(nc.semaphore(name))

    m = Map(nc, -(-nc.sbuf_base // 32) * 32, nc.sbuf_usable_end)
    ident = m.new("ident", [P, P], F32)
    spread = m.new("spread", [P, P], F32)
    headsum = m.new("headsum", [P, 2, HEADS], F32)
    cols = m.new("cols", [P, NCOL], F32)
    rows1 = m.new("rows1", [P, len(ROWS1), D], F32)
    X = m.new("X", [P, TILES, D], F32)
    small = m.new("small", [P, 256], F32)
    flag = m.new("flag", [1, 2], I32)
    oKST = m.region(HEADS * T * 2)
    oV = m.region(TILES * HEADS * 32 * 4)
    oQST = m.region(HEADS * CHUNK * 2)
    oP = m.region(4 * 2 * CHUNK * 4)
    oON = m.region(GROUPS * CHUNK * 4 + 2 * CHUNK * 4)
    oREC = m.region(CHUNK * 4)
    oWOP = m.region(GROUPS * D * 4)
    oXH = m.region(TPC * D * 4 + 2 * CHUNK * 4)
    Rp = m.new("Rp", [HEADS, 3, CHUNK], BF16)
    oW1 = m.region(2 * HID * 4)
    oSCR = m.region(10 * CHUNK * 4)

    stack = m.put("stack", [P, HEADS * T], BF16, oKST)
    KST = [stack[:, 0:HEADS * n].rearrange("p (h n) -> p h n", h=HEADS) for n in (T, L + 3)]
    V = m.put("V", [P, TILES, HEADS, 32], F32, oV)
    QST = m.put("QST", [P, HEADS, CHUNK], BF16, oQST)
    PX = m.put("PX", [P, 4, 2, CHUNK], F32, oP)
    ONF = m.put("ONF", [P, GROUPS, CHUNK], F32, oON)
    OT = m.put("OT", [P, 2, CHUNK], F32, oON + GROUPS * CHUNK * 4)
    REC = m.put("REC", [P, CHUNK], F32, oREC)
    WOP = m.put("WOP", [P, GROUPS, D], F32, oWOP)
    XH = m.put("XH", [P, TPC, D], F32, oXH)
    HC = m.put("HC", [P, 2, CHUNK], F32, oXH + TPC * D * 4)
    W1 = m.put("W1", [P, 2, HID], F32, oW1)
    W2 = m.put("W2", [P, HID // P, D], F32, oKST + -(-HEADS * (L + 3) * 2 // 32) * 32)
    HIDT = m.put("HIDT", [P, HID // P, CHUNK], F32, oSCR)
    s = Map(nc, oSCR, m.at)
    FQ = s.new("FQ", [P, 2, CHUNK], F32)
    FR = s.new("FR", [P, CHUNK], F32)
    SQ = s.new("SQ", [P, 2, CHUNK], F32)
    PARTS = s.new("PARTS", [P, 2, 3, CHUNK], BF16)
    R = s.new("R", [HEADS, CHUNK], F32)
    CAWQ = s.new("CAWQ", [P, 2, D], F32)
    XH1 = m.put("XH1", [P, 2, TPC, D], F32, oW1)
    NQ = m.put("NQ", [HEADS, CHUNKS, CHUNK], F32, oON)
    hF = m.put("hF", [P, 2, T], F32, oP)
    SAW = m.put("SAW", [P, 3, 2, D], F32, oXH)
    s = Map(nc, oKST, oV)
    ctxT = s.new("ctxT", [KC, 2, L], F32)
    tokF = s.new("tokF", [P, 2, L], F32)
    tokT = s.new("tokT", [P, LT, D], F32)
    WPJ = s.new("WPJ", [KC, 2, D], F32)
    CAKV = s.new("CAKV", [KC, 2, 2, D], F32)
    PR = s.new("PR", [P, L], F32)
    PT = s.new("PT", [P, LT, P], F32)
    rows0 = s.new("rows0", [P, len(ROWS0), D], F32)
    s = Map(nc, oQST, oP)
    CF = s.new("CF", [P, 2, 4, P], F32)
    XT = s.new("XT", [P, 2, 2, P], F32)
    XHS = s.new("XHS", [P, 2, 2, D], F32)
    RPS = s.new("RPS", [P, 2, P], F32)
    TR = s.new("TR", [P, 2, P], F32)
    TU = s.new("TU", [P, D], F32)
    W0 = m.put("W0", [P, 3, 4, D], F32, oON)
    UZ = m.put("UZ", [P, D], F32, oREC)
    CZ = m.put("CZ", [P, D], F32, oREC + D * 4)
    CD = m.put("CD", [P, D], F32, oWOP)
    E1 = m.put("E1", [P, D], F32, oWOP + D * 4)
    E2 = m.put("E2", [P, D], F32, oWOP + 2 * D * 4)
    PS = ctx.enter_context(nc.psum_tensor("PS", [P, 8, CHUNK], F32))
    flat = PS[:, :, :].rearrange("p b n -> p (b n)")

    qd = [nc.dram_tensor(f"q_parts_{a}", [3, D, T], BF16, kind="Internal").ap() for a in range(2)]
    kd = [nc.dram_tensor(f"k_parts_{a}", [3, D, (T, L)[a]], BF16, kind="Internal").ap() for a in range(2)]
    sd = [nc.dram_tensor(f"shift_{a}", [3, HEADS, T], BF16, kind="Internal").ap() for a in range(2)]
    vd = nc.dram_tensor("v_cross", [P, LT * HEADS * 32], F32, kind="Internal").ap()

    def col(name, c=0):
        i = 2 * COLS.index(name) + c
        return cols[:, i:i + 1]

    def row(name):
        if name in ROWS0:
            return rows0[:, ROWS0.index(name), :]
        return rows1[:, ROWS1.index(name), :]

    BRH, NEGM, NEGR, SUM0, RS0, STAT, AG, NVAR, NA, NB, NY, NI = 0, 2, 4, 6, 8, 10, 40, 50, 54, 58, 62, 66
    KM, KMT, NCF, QM, QMT, TB, FM, MX = 70, 80, 82, 84, 92, 94, 96, 128
    LN1 = 128
    AGX, NYX = 192, 224

    def sm(o, n=1, p=P):
        return small[0:p, o:o + n]

    names = """const_loaded x_loaded w0_loaded wproj_loaded ctx_loaded saw_loaded w1_loaded w2_loaded
        v_cleared ones_loaded half_bias dve_chain dve_stepped pool_stepped
        ctx_unit ctx_taken_act ctx_taken_dve parts_ready parts_stored0 parts_stored1 squares norms norms_taken shift_ready shift_stored
        v_cross_stored
        l0_scores l0_negmax l0_exp l0_pT l0_pT_taken l0_routed l0_hat l0_hatT l0_concat
        l0_gates l0_rtanh l0_ubiased l0_utanh l0_rps l0_candps l0_candz l0_cand l0_x1
        ln1_hat ln1_T ln1_taken qkv_unit v_unit_taken wop_cleared out_stored""".split()
    S = {n: sem(n) for n in names}
    s_xt = [sem(f"xt_loaded{i}") for i in range(2)]
    per = """scores exp pv heads sums sums_taken normed y y_taken hat hT hc unit unit_taken gelu mlp
        mlp_taken out_ready flag_row flag wop g_q g_scores g_max g_rows g_split g_stored g_chain""".split()
    A = [{n: sem(f"{('self', 'cross')[a]}_{n}") for n in per} for a in range(2)]
    s_kst = [[sem(f"k_stack{a}_{g}") for g in range(GROUPS)] for a in range(2)]
    s_vst = [sem(f"v_cross_loaded{g}") for g in range(GROUPS)]
    s_qst = [[sem(f"q_stack{a}_{g}") for g in range(GROUPS)] for a in range(2)]

    NKS = (TILES, LT)
    KEYS = (T, L)

    def key_rows(a, kt):
        return min(P, KEYS[a] - kt * P)

    CK, SQK, CQ = 0, 2 * CHUNKS, 6 * CHUNKS

    def numbered(entries):
        out, u = [], 0
        for e in entries:
            out.append((None if e[0] in ("norm", "T", "LN") else u,) + e)
            u += e[0] not in ("norm", "T", "LN")
        return out

    pcs = pieces(L)
    stage1 = ([("tokF", n, w, mm) for n, w in pcs for mm in range(2)] + [("tokT", kt, 0, 0) for kt in range(LT)])
    for i, (n, w) in enumerate(pcs):
        stage1 += [("k", n, w, mm) for mm in range(2)]
        stage1 += [("v", kt, 0, 0) for kt in range(LT * i // len(pcs), LT * (i + 1) // len(pcs))]
        stage1 += [("norm", i, w, 0)]
    stage1 = numbered(stage1)
    stage3 = [("T", 0, 0, 0)]
    for n in range(CHUNKS):
        stage3 += [("q", n * CHUNK, CHUNK, mm) for mm in range(2)]
        if 2 <= n + 1 < CHUNKS:
            stage3 += [("LN", n + 1, 0, 0)]
        stage3 += [("k", n * CHUNK, CHUNK, 0), ("norm", CHUNKS + 2 * n, CHUNK, 0), ("k", n * CHUNK, CHUNK, 1)]
        stage3 += [("v", kt, 0, 0) for kt in range(n * TPC, (n + 1) * TPC)]
        if n + 1 < CHUNKS:
            stage3 += [("T", n + 1, 0, 0)]
        stage3 += [("norm", CHUNKS + 2 * n + 1, CHUNK, 0)]
    stage3 = numbered(stage3)

    def taken(plan, u, before):
        kinds = [e[1] for e in plan if e[0] is not None]
        kind = kinds[u]
        if kind in ("k", "q"):
            return S["squares"], before + sum(k in ("k", "q") for k in kinds[:u + 1])
        if kind == "tokF":
            return S["ctx_taken_act"], kinds[:u + 1].count("tokF")
        if before:
            return S["v_unit_taken"], kinds[:u + 1].count("v")
        return S["ctx_taken_dve"], sum(k in ("tokT", "v") for k in kinds[:u + 1])

    def wait_parts_stored(eng, units):
        for mm in range(2):
            eng.wait_ge(S[f"parts_stored{mm}"], 8 * units)

    def events(a, c):
        NK = NKS[a]
        ev = {t: [] for t in range(GROUPS * NK)}
        for g in range(GROUPS):
            if g or c is not None:
                ev[g * NK].append(("copy", g, 0, True))
                ev[g * NK + 2].append(("sums", g, 0, True))
                ev[g * NK + 3].append(("divide", g, 0, False))
                ev[g * NK + 4].append(("divide", g, 1, True))
        if c is not None:
            for kind, at in REST[a].items():
                n = PARTS_OF[kind]
                for j, t in enumerate(at):
                    ev[t].append((kind, j // n, j % n, j % n == n - 1))
            ev[HAT_STEP[a]].append(("hat", 0, 0, True))
        return ev

    block = ctx.enter_context(nc.Block())

    @block.sync
    def _(sp):
        sp.dma_start(ctxT[:], d["ctxT"].rearrange("(c p) l -> p c l", p=KC)).then_inc(S["ctx_loaded"], 16)
        sp.dma_start(WPJ[:], d["Wproj"].rearrange("(c p) n -> p c n", p=KC)).then_inc(S["wproj_loaded"], 16)
        for i, n in enumerate(("cak", "cav")):
            sp.dma_start(CAKV[:, i], d[n].rearrange("(c p) n -> p c n", p=KC)).then_inc(S["wproj_loaded"], 16)
        sp.dma_start(cols[:], d["cols"]).then_inc(S["const_loaded"], 16)
        for i in range(len(ROWS0)):
            sp.dma_start(rows0[:, i, :], d["rows0"][i, :].partition_broadcast(P)).then_inc(S["const_loaded"], 16)
        for i in range(len(ROWS1)):
            sp.dma_start(rows1[:, i, :], d["rows1"][i, :].partition_broadcast(P)).then_inc(S["const_loaded"], 16)
        sp.dma_start(headsum[:], d["headsum"]).then_inc(S["const_loaded"], 16)
        sp.dma_start(ident[:], d["ident"]).then_inc(S["const_loaded"], 16)
        sp.dma_start(spread[:], d["spread"]).then_inc(S["const_loaded"], 16)
        for i in range(2):
            sp.dma_start(XT[:, i], d["xT"].rearrange("(c p) t -> p c t", p=P)[:, :, i * P:(i + 1) * P]) \
                .then_inc(s_xt[i], 16)
        sp.dma_start(X[:], d["x"].rearrange("(n p) d -> p n d", p=P)).then_inc(S["x_loaded"], 16)
        for i, n in enumerate(("Wu", "Wr", "Wn")):
            sp.dma_start(W0[:, i], d[n].rearrange("(c p) n -> p c n", p=P)).then_inc(S["w0_loaded"], 16)
        for i, n in enumerate(("saq", "sak", "sav")):
            sp.dma_start(SAW[:, i], d[n].rearrange("(c p) n -> p c n", p=P)).then_inc(S["saw_loaded"], 16)
        sp.dma_start(CAWQ[:], d["caq"].rearrange("(c p) n -> p c n", p=P)).then_inc(S["saw_loaded"], 16)
        with sp.Fori(1, TILES // 2) as k:
            for par in range(2):
                sp.wait_ge(S["l0_scores"], 2 * k - 1 + par)
                sp.dma_start(XT[:, par], d["xT"].rearrange("(c p) t -> p c t", p=P)
                             [:, :, bass.ds((2 * k + par) * P, P)]).then_inc(s_xt[par], 16)
        sp.wait_ge(S["wop_cleared"], 1)
        for j in range(GH):
            sp.dma_start(WOP[32 * j:32 * j + HD, :, :],
                         d["sawo"].rearrange("(g j d) n -> j d g n", g=GROUPS, j=GH)[j]) \
                .then_inc(A[0]["wop"], 16)
        for a in range(2):
            steps = GROUPS * NKS[a]
            def load_q(c, g, s_to):
                for b, part in enumerate(QBLOCK):
                    sp.dma_start(QST[b * HD:(b + 1) * HD, g * GH:(g + 1) * GH, :],
                                 qd[a][part, g * GH * HD:(g + 1) * GH * HD, bass.ds(c * CHUNK, CHUNK)]
                                 .rearrange("(j d) n -> d j n", j=GH)).then_inc(s_to, 16)

            if a == 0:
                sp.wait_ge(S["l0_x1"], TILES)
                sp.dma_start(stack[SROW:NROW, :].bitcast(F32), d["ones"]).then_inc(S["ones_loaded"], 16)
                for n in range(CHUNKS):
                    if n == 1:
                        for g in range(GROUPS):
                            load_q(0, g, s_qst[0][g])
                    wait_parts_stored(sp, SQK + 4 * (n + 1))
                    for b, part in enumerate(KBLOCK):
                        sp.dma_start(KST[0][b * HD:(b + 1) * HD, :, n * CHUNK:(n + 1) * CHUNK],
                                     kd[0][part, :, n * CHUNK:(n + 1) * CHUNK]
                                     .rearrange("(j d) n -> d j n", j=HEADS)).then_inc(s_kst[0][0], 16)
            else:
                wait_parts_stored(sp, CQ + 2)
                sp.wait_ge(S["v_cross_stored"], 16)
                for g in range(GROUPS):
                    last = (CHUNKS - 1) * GROUPS * NKS[0] + (g + 1) * NKS[0]
                    sp.wait_ge(A[0]["scores"], 2 * last)
                    for b, part in enumerate(KBLOCK):
                        sp.dma_start(KST[1][b * HD:(b + 1) * HD, g * GH:(g + 1) * GH, 0:L],
                                     kd[1][part, g * GH * HD:(g + 1) * GH * HD, :]
                                     .rearrange("(j d) n -> d j n", j=GH)).then_inc(s_kst[1][g], 16)
                    load_q(0, g, s_qst[1][g])
                    sp.wait_ge(A[0]["pv"], last)
                    sp.dma_start(V[:, 0:LT, g * GH:(g + 1) * GH, :],
                                 vd.rearrange("p (k h e) -> p k h e", k=LT, h=HEADS)[:, :, g * GH:(g + 1) * GH, :]) \
                        .then_inc(s_vst[g], 16)
                sp.dma_start(W2[:], d["w2T"].rearrange("(c p) n -> p c n", p=P)).then_inc(S["w2_loaded"], 16)
                sp.wait_ge(A[0]["y"], CHUNKS * TPC)
                for j in range(GH):
                    sp.dma_start(WOP[32 * j:32 * j + HD, :, :],
                                 d["cawo"].rearrange("(g j d) n -> j d g n", g=GROUPS, j=GH)[j]) \
                        .then_inc(A[1]["wop"], 16)

            sp.wait_ge(A[a]["flag"], 1)
            bounded = sp.value_load(flag[0:1, a:a + 1], min_val=0, max_val=1)
            with sp.If(bounded < 1):
                wait_parts_stored(sp, CQ + 2 * CHUNKS * a)
                sp.wait_ge(S["shift_stored"], 16 * CHUNKS * (a + 1))
                for g in range(GROUPS):
                    sp.wait_ge(s_qst[a][g], 16 * len(QBLOCK))
                with sp.Fori(0, CHUNKS) as c:
                    for g in range(GROUPS):
                        if g:
                            sp.wait_ge(A[a]["g_max"], (c * GROUPS + g) * GH * TPC)
                        load_q(c, g, A[a]["g_q"])
                    sp.wait_ge(A[a]["g_split"], c + 1)
                    sp.dma_start(sd[a][:, :, bass.ds(c * CHUNK, CHUNK)].rearrange("r h n -> h r n"), Rp[:]) \
                        .then_inc(A[a]["g_stored"], 16)
                sp.wait_ge(A[a]["g_stored"], 16 * CHUNKS)
                for g in range(GROUPS):
                    load_q(0, g, A[a]["g_q"])

            def load_stack(c, g, first):
                if not first:
                    sp.wait_ge(A[a]["scores"], ((c - 1) * steps + (g + 1) * NKS[a]) * 2)
                    load_q(c, g, s_qst[a][g])
                sp.dma_start(QST[SROW:NROW, g * GH:(g + 1) * GH, :],
                             sd[a][:, g * GH:(g + 1) * GH, bass.ds(c * CHUNK, CHUNK)]).then_inc(s_qst[a][g], 16)

            sp.wait_ge(S["shift_stored"], 16 * (CHUNKS * a + 1))
            for g in range(GROUPS):
                load_stack(0, g, True)
            if a == 0:
                sp.wait_ge(S["ln1_T"], CHUNKS)
                sp.dma_start(W1[:], d["w1T"].rearrange("(c p) n -> p c n", p=P)).then_inc(S["w1_loaded"], 16)
            wait_parts_stored(sp, CQ + 2 * CHUNKS * a)
            sp.wait_ge(S["shift_stored"], 16 * CHUNKS * (a + 1))
            with sp.Fori(1, CHUNKS) as c:
                for g in range(GROUPS):
                    load_stack(c, g, False)

    @block.gpsimd
    def _(gp):
        gp.memset(V[:], 0.0).then_inc(S["v_cleared"], 1)
        gp.wait_ge(S["v_cleared"], 1)
        gp.memset(V[:, :, :, HD:HD + 1], 1.0).then_inc(S["v_cleared"], 1)

        def store_parts(u, dst, n, w, mm):
            gp.wait_ge(S["parts_ready"], u + 1)
            gp.sem_inc(S["pool_stepped"], 1)
            gp.dma_start(dst[:, mm * P:(mm + 1) * P, bass.ds(n, w)].rearrange("r p n -> p r n"),
                         PARTS[:, mm, :, 0:w]).then_inc(S[f"parts_stored{mm}"], 16)

        def store_shift(i, a, n):
            gp.wait_ge(S["shift_ready"], i + 1)
            gp.sem_inc(S["pool_stepped"], 1)
            gp.dma_start(sd[a][:, :, bass.ds(n, CHUNK)].rearrange("r h n -> h r n"), Rp[:]) \
                .then_inc(S["shift_stored"], 16)

        for i, (n, w) in enumerate(pieces(L)):
            for mm in range(2):
                store_parts(CK + 2 * i + mm, kd[1], n, w, mm)
        gp.wait_ge(S["ctx_taken_dve"], 2 * LT)
        gp.dma_start(vd, V[:, 0:LT].rearrange("p k h e -> p (k h e)")).then_inc(S["v_cross_stored"], 16)
        gp.wait_ge(S["l0_x1"], TILES)
        gp.memset(WOP[:], 0.0).then_inc(S["wop_cleared"], 1)
        for i in range(CHUNKS):
            for half, dst in enumerate((qd[0], kd[0])):
                for mm in range(2):
                    store_parts(SQK + 4 * i + 2 * half + mm, dst, i * CHUNK, CHUNK, mm)
        for i in range(CHUNKS):
            store_shift(i, 0, i * CHUNK)
        with gp.Fori(0, CHUNKS) as c:
            for mm in range(2):
                store_parts(CQ + 2 * c + mm, qd[1], c * CHUNK, CHUNK, mm)
            store_shift(CHUNKS + c, 1, c * CHUNK)
        with gp.Fori(0, CHUNKS) as c:
            for tt in range(TPC):
                gp.wait_ge(A[1]["out_ready"], c * TPC + tt + 1)
                gp.sem_inc(S["pool_stepped"], 1)
                gp.dma_start(out[bass.ds((c * TPC + tt) * P, P), :], XH[:, tt, :]) \
                    .then_inc(S["out_stored"], 16)
        gp.wait_ge(S["out_stored"], 16 * TILES)

    @block.scalar
    def _(act):
        act.wait_ge(S["const_loaded"], 16 * (4 + len(ROWS0) + len(ROWS1)))
        for c in range(2):
            act.mul(sm(BRH + c), col("L0_xattn_b_r", c), 0.5).then_inc(S["half_bias"], 1)
        act.wait_ge(S["half_bias"], 2)

        def split(u, bank, w, mm, bias):
            wait(act, S["parts_ready"], u - 1)
            wait(act, S[f"parts_stored{mm}"], 16 * (u // 2))
            wait(act, S["norms"], u // 2)
            act.activation(FQ[:, mm, 0:w], PS[:, bank, 0:w], ACT.Identity, bias=bias)
            act.activation(PARTS[:, mm, 0, 0:w], PS[:, bank, 0:w], ACT.Identity, bias=bias)
            act.activation(SQ[:, mm, 0:w], PS[:, bank, 0:w], ACT.Square, bias=bias).then_inc(S["squares"], 1)

        split_unit = CK
        for u, kind, n, w, mm in stage1:
            if kind == "tokF":
                act.wait_ge(S["ctx_unit"], u + 1)
                act.activation(tokF[:, mm, n:n + w], PS[:, u % 4, 0:w], ACT.Identity,
                               bias=col("L0_xattn_b_proj", mm)).then_inc(S["ctx_taken_act"], 1)
            if kind == "k":
                act.wait_ge(S["ctx_unit"], u + 1)
                split(split_unit, u % 4, w, mm, col("L1_xattn_ca_bk", mm))
                split_unit += 1

        def l0(i, par, exp, routed, gates):
            if exp:
                act.wait_ge(S["l0_negmax"], i + 1)
                wait(act, S["l0_pT"], 4 * i)
                act.activation(PR[:], flat[:, 0:L], ACT.Exp, bias=sm(NEGM + par), scale=SCALE0,
                               accum_out=sm(SUM0 + par)).then_inc(S["l0_exp"], 1)
            if gates:
                act.wait_ge(S["l0_gates"], i - 1)
                wait(act, S["l0_rps"], i - 2)
                for c in range(2):
                    ins = act.activation(TR[:, c, :], PS[:, 7, c * P:(c + 1) * P], ACT.Tanh,
                                         bias=sm(BRH + c), scale=0.5)
                ins.then_inc(S["l0_rtanh"], 1)
            if exp:
                for k in range(4):
                    act.wait_ge(S["l0_pT"], 4 * i + k + 1)
                    if k < 3:
                        act.copy(PT[:, 4 * k:4 * k + 4, :].rearrange("p k q -> p (k q)"), PS[:, 4 + k % 2, :]) \
                            .then_inc(S["l0_pT_taken"], 1)
                    else:
                        act.copy(PT[0:LLAST, LT - 1, :], PS[0:LLAST, 5, 0:P]).then_inc(S["l0_pT_taken"], 1)
            if routed:
                act.wait_ge(S["l0_hatT"], i)
                for k, (g_, b_) in enumerate(2 * [("L0_xattn_g_state", "L0_xattn_beta_state")]
                                             + 2 * [("L0_xattn_g_input", "L0_xattn_beta_input")]):
                    ins = act.activation(CF[:, 1 - par, k, :], PS[:, 4, k * P:(k + 1) * P], ACT.Identity,
                                         scale=col(g_, k % 2), bias=col(b_, k % 2))
                ins.then_inc(S["l0_concat"], 1)
            if gates:
                act.wait_ge(S["l0_ubiased"], i - 1)
                act.activation(TU[:], UZ[:], ACT.Tanh, scale=0.5).then_inc(S["l0_utanh"], 1)
                act.wait_ge(S["l0_candz"], i - 1)
                act.activation(CD[:], CZ[:], ACT.Tanh).then_inc(S["l0_cand"], 1)

        for i in range(4):
            l0(i, i % 2, True, i >= 1, i >= 2)
        with act.Fori(2, TILES // 2) as k:
            for par in range(2):
                l0(2 * k + par, par, True, True, True)
        for i in range(TILES, TILES + 2):
            l0(i, i % 2, False, i < TILES + 1, True)

        split_unit = SQK
        for u, kind, n, w, mm in stage3:
            if kind == "T":
                act.wait_ge(S["ln1_T"], n + 1)
                for c in range(2):
                    ins = act.activation(hF[:, c, n * CHUNK:(n + 1) * CHUNK], PS[:, 4 + c, :], ACT.Identity,
                                         scale=col("L1_xattn_ln1_g", c), bias=col("L1_xattn_ln1_b", c))
                ins.then_inc(S["ln1_taken"], 1)
            if kind in ("k", "q"):
                act.wait_ge(S["qkv_unit"], u + 1)
                split(split_unit, u % 4, w, mm, col("L1_xattn_sa_b" + kind, mm))
                split_unit += 1

        for a in range(2):
            NK, at = NKS[a], A[a]
            steps = GROUPS * NK

            def gelu(q):
                act.wait_ge(at["unit_taken"], HID // P * (q + 1))
                act.activation(HIDT[:], HIDT[:], ACT.Gelu).then_inc(at["gelu"], 1)

            def chunk(c, first):
                for t in range(steps):
                    kr = key_rows(a, t % NK)
                    for half in range(2):
                        h = (c * steps + t) * 2 + half
                        act.wait_ge(at["scores"], h + 1)
                        if half == 0:
                            wait(act, at["pv"], c * steps + t - 1)
                        slot = 2 * ((2 * t + half) % LOOK)
                        act.activation(PX[0:kr, (2 * t + half) % 4, :, :], PS[0:kr, slot:slot + 2, :],
                                       ACT.Exp, scale=SCALE).then_inc(at["exp"], 1)
                    if a == 1 and t == GELU_STEP and not first:
                        gelu(c - 1)

            chunk(0, True)
            with act.Fori(1, CHUNKS) as c:
                chunk(c, False)
            if a == 0:
                for mm in range(2):
                    act.wait_ge(at["unit"], 2 * (CHUNKS - 1) + mm + 1)
                    split(CQ + 2 * (CHUNKS - 1) + mm, mm, CHUNK, mm, col("L1_xattn_ca_bq", mm))
            if a == 1:
                for i in range(HID // P):
                    u = HID // P * (CHUNKS - 1) + i
                    act.wait_ge(at["unit"], u + 1)
                    if i == 0:
                        act.wait_ge(at["mlp"], (CHUNKS - 1) * TPC)
                    act.activation(HIDT[:, i, :], PS[:, i % 4, :], ACT.Gelu, bias=col("L1_xattn_mlp_b1", i)) \
                        .then_inc(at["unit_taken"], 1)

    @block.tensor
    def _(pe):
        def norm(i, w, bank, halves=range(2)):
            pe.wait_ge(S["squares"], 2 * (i + 1))
            for mm in halves:
                ins = pe.matmul(PS[0:HEADS, bank, 0:w], headsum[:, mm, :], SQ[:, mm, 0:w],
                                start=(mm == 0), stop=(mm == 1))
            if 1 in halves:
                ins.then_inc(S["norms"], 1)

        pe.wait_ge(S["ctx_loaded"], 16)
        pe.wait_ge(S["wproj_loaded"], 48)
        for u, kind, n, w, mm in stage1:
            if kind == "norm":
                if n == 0:
                    pe.wait_ge(S["const_loaded"], 16 * (4 + len(ROWS0) + len(ROWS1)))
                wait(pe, S["norms_taken"], n)
                norm(n, w, 6)
                continue
            if u >= 4:
                pe.wait_ge(*taken(stage1, u - 4, 0))
            bank = u % 4
            for c in range(2):
                if kind in ("tokF", "k"):
                    lhs = (WPJ[:, c, mm * P:(mm + 1) * P] if kind == "tokF" else
                           CAKV[:, 0, c, mm * P:(mm + 1) * P])
                    ins = pe.matmul(PS[:, bank, 0:w], lhs, ctxT[:, c, n:n + w], start=(c == 0), stop=(c == 1))
                else:
                    kr = key_rows(1, n)
                    rhs = WPJ[:, c, :] if kind == "tokT" else CAKV[:, 1, c, :]
                    ins = pe.matmul(PS[0:kr, bank, 0:D], ctxT[:, c, n * P:n * P + kr], rhs,
                                    start=(c == 0), stop=(c == 1))
            ins.then_inc(S["ctx_unit"], 1)

        pe.wait_ge(S["ctx_taken_act"], 2 * len(pcs))
        pe.wait_ge(S["ctx_taken_dve"], 2 * LT)
        pe.wait_ge(S["squares"], SQK)
        pe.wait_ge(S["norms_taken"], CHUNKS)
        pe.wait_ge(S["w0_loaded"], 48)

        def l0(i, par, turn, scores, routed, gates):
            if scores:
                pe.wait_ge(s_xt[par], 16 * (turn + 1))
                wait(pe, S["l0_exp"], i)
                for b, (n, w) in enumerate(pieces(L)):
                    for c in range(2):
                        ins = pe.matmul(PS[:, b, 0:w], XT[:, par, c, :], tokF[:, c, n:n + w],
                                        start=(c == 0), stop=(c == 1))
                ins.then_inc(S["l0_scores"], 1)
            if routed:
                pe.wait_ge(S["l0_pT_taken"], 4 * i)
                wait(pe, S["l0_candz"], i - 2)
                for kt in range(LT):
                    kr = key_rows(1, kt)
                    ins = pe.matmul(PS[:, 6, 0:D], PT[0:kr, kt, :], tokT[0:kr, kt, :],
                                    start=(kt == 0), stop=(kt == LT - 1))
                ins.then_inc(S["l0_routed"], 1)
            if gates:
                pe.wait_ge(S["l0_concat"], i - 1)
                wait(pe, S["l0_rps"], i - 2)
                for mm in range(2):
                    for c in range(4):
                        pe.matmul(PS[:, 7, mm * P:(mm + 1) * P], W0[:, 1, c, mm * P:(mm + 1) * P],
                                  CF[:, par, c, :], start=(c == 0), stop=(c == 3))
                for c in range(4):
                    ins = pe.matmul(PS[:, 7, D:2 * D], CF[:, par, c, :], W0[:, 0, c, :],
                                    start=(c == 0), stop=(c == 3))
                ins.then_inc(S["l0_gates"], 1)
            if scores:
                pe.wait_ge(S["l0_exp"], i + 1)
                for k in range(4):
                    if k >= 2:
                        pe.wait_ge(S["l0_pT_taken"], 4 * i + k - 1)
                    for kt in range(4 * k, min(4 * k + 4, LT)):
                        kr = key_rows(1, kt)
                        ins = pe.transpose(PS[0:kr, 4 + k % 2, (kt % 4) * P:(kt % 4 + 1) * P],
                                           PR[:, kt * P:kt * P + kr], ident[:])
                    ins.then_inc(S["l0_pT"], 1)
            if routed:
                pe.wait_ge(S["l0_hat"], i)
                if scores:
                    pe.wait_ge(S["l0_pT_taken"], 4 * i + 3)
                for k in range(4):
                    ins = pe.transpose(PS[:, 4, k * P:(k + 1) * P],
                                       XHS[:, 1 - par, k // 2, (k % 2) * P:(k % 2 + 1) * P], ident[:])
                ins.then_inc(S["l0_hatT"], 1)
            if gates:
                pe.wait_ge(S["l0_rps"], i - 1)
                for c in range(4):
                    ins = pe.matmul(PS[:, 6, 0:D], RPS[:, c, :] if c < 2 else CF[:, par, c, :],
                                    W0[:, 2, c, :], start=(c == 0), stop=(c == 3))
                ins.then_inc(S["l0_candps"], 1)

        for i in range(4):
            l0(i, i % 2, i // 2, True, i >= 1, i >= 2)
        with pe.Fori(2, TILES // 2) as k:
            for par in range(2):
                l0(2 * k + par, par, k, True, True, True)
        for i in range(TILES, TILES + 2):
            l0(i, i % 2, 0, False, i < TILES + 1, True)

        pe.wait_ge(S["l0_cand"], TILES)
        pe.wait_ge(S["saw_loaded"], 64)
        for u, kind, n, w, mm in stage3:
            if kind == "T":
                pe.wait_ge(S["ln1_hat"], n + 1)
                wait(pe, S["ln1_taken"], n)
                for c in range(2):
                    for tt in range(TPC):
                        ins = pe.transpose(PS[:, 4 + c, tt * P:(tt + 1) * P],
                                           XH1[:, n % 2, tt, c * P:(c + 1) * P], ident[:])
                ins.then_inc(S["ln1_T"], 1)
                continue
            if kind == "norm":
                pe.wait_ge(S["norms_taken"], n)
                norm(n, w, 6)
                continue
            if kind == "LN":
                continue
            if u >= 4:
                pe.wait_ge(*taken(stage3, u - 4, SQK))
            if kind == "q":
                pe.wait_ge(S["ln1_taken"], n // CHUNK + 1)
            for c in range(2):
                if kind == "v":
                    ins = pe.matmul(PS[:, u % 4, 0:D], hF[:, c, n * P:(n + 1) * P], SAW[:, 2, c, :],
                                    start=(c == 0), stop=(c == 1))
                else:
                    ins = pe.matmul(PS[:, u % 4, :], SAW[:, "qk".index(kind), c, mm * P:(mm + 1) * P],
                                    hF[:, c, n:n + w], start=(c == 0), stop=(c == 1))
            ins.then_inc(S["qkv_unit"], 1)
        pe.wait_ge(S["squares"], CQ)
        pe.wait_ge(S["v_unit_taken"], TILES)
        pe.wait_ge(S["ones_loaded"], 16)

        for a in range(2):
            NK, at = NKS[a], A[a]
            steps = GROUPS * NK
            pe.wait_ge(at["flag_row"], 1)
            pe.matmul(PS[0:1, 7, 0:HEADS], sm(TB + a, 1, HEADS), ident[0:HEADS, 0:HEADS], start=True,
                      stop=True).then_inc(at["flag_row"], 1)
            pe.wait_ge(at["flag"], 1)


            def wait_k_stack(g):
                if a == 0:
                    pe.wait_ge(s_kst[0][0], 16 * len(KBLOCK) * CHUNKS)
                else:
                    pe.wait_ge(s_kst[1][g], 16 * len(KBLOCK))

            bounded = pe.value_load(flag[0:1, a:a + 1], min_val=0, max_val=1)
            with pe.If(bounded < 1):
                for g in range(GROUPS):
                    wait_k_stack(g)
                with pe.Fori(0, CHUNKS) as c:
                    for g in range(GROUPS):
                        pe.wait_ge(at["g_q"], 16 * len(QBLOCK) * (c * GROUPS + g + 1))
                        for j in range(GH):
                            for tt in range(TPC):
                                if g or j or tt:
                                    pe.wait_ge(at["g_max"], (c * GROUPS + g) * GH * TPC + j * TPC + tt)
                                for b, (n, w) in enumerate(pieces(KEYS[a])):
                                    ins = pe.matmul(PS[:, b, 0:w], QST[0:ROWS, g * GH + j, tt * P:(tt + 1) * P],
                                                    KST[a][0:ROWS, g * GH + j, n:n + w], start=True, stop=True)
                                ins.then_inc(at["g_scores"], 1)
                    pe.wait_ge(at["g_max"], (c + 1) * GROUPS * GH * TPC)
                    for tt in range(TPC):
                        ins = pe.matmul(PS[0:HEADS, 4, tt * P:(tt + 1) * P], sm(MX + tt * HEADS, HEADS),
                                        ident[:], start=True, stop=True)
                    ins.then_inc(at["g_rows"], 1)
                pe.wait_ge(at["g_split"], CHUNKS)
                pe.wait_ge(at["g_q"], 16 * len(QBLOCK) * GROUPS * (CHUNKS + 1))

            def scores(c, n, first):
                h = c * steps * 2 + n
                t, half = n // 2, n % 2
                g, kt = t // NK, t % NK
                kr = key_rows(a, kt)
                if kt == 0 and half == 0:
                    if first:
                        wait_k_stack(g)
                    pe.wait_ge(s_qst[a][g], 16 * (len(QBLOCK) + 1) * (c + 1))
                wait(pe, at["exp"], h - 1 if n < 2 else h - 2)
                for jj in range(2):
                    head = g * GH + 2 * half + jj
                    ins = pe.matmul(PS[0:kr, 2 * (n % LOOK) + jj, :], KST[a][0:NROW, head, kt * P:kt * P + kr],
                                    QST[0:NROW, head, :], start=True, stop=True)
                ins.then_inc(at["scores"], 1)

            def pv(c, t):
                g, kt = t // NK, t % NK
                kr = key_rows(a, kt)
                pe.wait_ge(at["exp"], (c * steps + t) * 2 + 2)
                if a == 1 and kt == 0 and isinstance(c, int):
                    pe.wait_ge(s_vst[g], 16)
                if kt == 0:
                    wait(pe, at["heads"], c * GROUPS + g)
                for j in range(GH):
                    ins = pe.matmul(PS[32 * j:32 * j + 32, 6, :], V[0:kr, kt, g * GH + j, :],
                                    PX[0:kr, (2 * t + j // 2) % 4, j % 2, :],
                                    start=(kt == 0), stop=(kt == NK - 1))
                ins.then_inc(at["pv"], 1)

            def bank7_taken(c, kind, i):
                q = c - 1
                s_, value = {"sums": (at["sums_taken"], c * GROUPS + i), "y": (at["y_taken"], q * TPC + i + 1),
                             "h": (at["hc"], 2 * q + i + 1), "u": (at["unit_taken"], 2 * q + i + 1),
                             "n": (S["norms_taken"], 3 * CHUNKS + q + 1),
                             "m": (at["unit_taken"], HID // P * q + i + 1),
                             "o": (at["mlp_taken"], q * TPC + i + 1)}[kind]
                pe.wait_ge(s_, value)

            def sums(c, g):
                u = c * GROUPS + g - 1
                pe.wait_ge(at["heads"], u + 1)
                pe.matmul(PS[:, 7, :], spread[:], OT[:, (g - 1) % 2, :], start=True, stop=True) \
                    .then_inc(at["sums"], 1)

            def piece(kind, i, q, part, tail=False):
                whole = part is None
                first, last = whole or part == 0, whole or part == PARTS_OF[kind] - 1

                def share(n):
                    if whole:
                        return range(n)
                    w = n // PARTS_OF[kind]
                    return range(part * w, (part + 1) * w)

                bank = i % 4 if tail else 7
                if kind == "y":
                    if i == 0 and first:
                        pe.wait_ge(at["normed"], (q + 1) * GROUPS)
                        pe.wait_ge(at["wop"], 16 * GH)
                    for g in share(GROUPS):
                        ins = pe.matmul(PS[:, bank, 0:D], ONF[:, g, i * P:(i + 1) * P], WOP[:, g, :],
                                        start=(g == 0), stop=(g == GROUPS - 1))
                    if last:
                        ins.then_inc(at["y"], 1)
                if kind == "h":
                    pe.wait_ge(at["hat"], q + 1)
                    for tt in range(TPC):
                        ins = pe.transpose(PS[:, bank, tt * P:(tt + 1) * P],
                                           XH[:, tt, i * P:(i + 1) * P], ident[:])
                    ins.then_inc(at["hT"], 1)
                if kind in ("u", "m"):
                    if first:
                        pe.wait_ge(at["hc"], 2 * q + 2)
                        if tail and i >= 4:
                            pe.wait_ge(at["unit_taken"], HID // P * q + i - 3)
                    for c in share(2):
                        ins = pe.matmul(PS[:, bank, :], (CAWQ if kind == "u" else W1)[:, c, i * P:(i + 1) * P],
                                        HC[:, c, :], start=(c == 0), stop=(c == 1))
                    if last:
                        ins.then_inc(at["unit"], 1)
                if kind == "n":
                    norm(3 * CHUNKS + q, CHUNK, 7, share(2))
                if kind == "o":
                    if tail:
                        pe.wait_ge(at["unit_taken"], HID // P * CHUNKS)
                    elif first:
                        pe.wait_ge(at["gelu"], q + 1)
                    for k in share(HID // P):
                        ins = pe.matmul(PS[:, bank, 0:D], HIDT[:, k, i * P:(i + 1) * P], W2[:, k, :],
                                        start=(k == 0), stop=(k == HID // P - 1))
                    if last:
                        ins.then_inc(at["mlp"], 1)

            if a == 1:
                pe.wait_ge(S["w1_loaded"], 16)
                pe.wait_ge(S["w2_loaded"], 16)

            def chunk(c, first):
                ev = events(a, None if first else c)
                held = None if first else (c - 1, "sums", GROUPS - 1)
                scores(c, 0, first)
                for t in range(steps):
                    if t == 0:
                        if not first:
                            pv(c - 1, steps - 1)
                        scores(c, 1, first)
                        scores(c, 2, first)
                    else:
                        if 2 * t + 2 < 2 * steps:
                            scores(c, 2 * t + 2, first)
                        pv(c, t - 1)
                    for kind, i, part, last in ev[t]:
                        if kind in ("copy", "divide", "hat"):
                            continue
                        if held is not None and part == 0:
                            bank7_taken(*held)
                        held = (c, kind, i)
                        if kind == "sums":
                            sums(c, i)
                        else:
                            piece(kind, i, c - 1, part)
                    if 2 * t + 3 < 2 * steps:
                        scores(c, 2 * t + 3, first)

            chunk(0, True)
            with pe.Fori(1, CHUNKS) as c:
                chunk(c, False)
            pv(CHUNKS - 1, steps - 1)
            bank7_taken(CHUNKS - 1, "sums", GROUPS - 1)
            sums(CHUNKS, 0)
            for kind, at_steps in REST[a].items():
                for i in range(len(at_steps) // PARTS_OF[kind]):
                    piece(kind, i, CHUNKS - 1, None, True)

    @block.vector
    def _(ve):
        ch = Chain(ve, S["dve_chain"])

        def rsqrt(n, link, i=0, ag=None, y=None, tmp=None):
            y = sm(NY + i, n) if y is None else y
            v, a_, b_, bits = (sm(o, n) for o in tmp or (NVAR, NA, NB, NI))
            ag = AG + 2 * i if ag is None else ag
            var = sm(ag, 2 * n).rearrange("p (n two) -> p n two", two=2)[:, :, 1:2].rearrange("p n o -> p (n o)")
            link(ve.tensor_scalar(v, var, EPS, None, ALU.add))
            link(ve.tensor_scalar(bits.bitcast(I32), v.bitcast(I32), 1, None, ALU.logical_shift_right))
            link(ve.tensor_scalar(y.bitcast(I32), bits.bitcast(I32), -1.0, float(0x5f3759df),
                                  ALU.mult, ALU.add))
            for _ in range(3):
                link(ve.tensor_tensor(a_, y, y, ALU.mult))
                link(ve.scalar_tensor_tensor(out=b_, in0=a_, scalar=-0.5, in1=v, op0=ALU.mult, op1=ALU.mult))
                link(ve.scalar_tensor_tensor(out=y, in0=b_, scalar=1.5, in1=y, op0=ALU.add, op1=ALU.mult))

        def stats(src, i, link):
            ve.sem_inc(S["dve_stepped"], 1)
            link(ve.bn_stats(sm(STAT + 6 * i, 6), src))
            ve.sem_inc(S["dve_stepped"], 1)
            link(ve.bn_aggr(sm(AG + 2 * i, 2), sm(STAT + 6 * i, 6)))

        def three(dst, src, tmp, link):
            link(ve.tensor_copy(dst[0], src))
            link(ve.tensor_tensor(tmp, src, dst[0], ALU.subtract))
            link(ve.tensor_copy(dst[1], tmp))
            return ve.tensor_tensor(dst[2], tmp, dst[1], ALU.subtract)

        def parts(i, w, mm):
            u = 2 * i + mm
            wait(ve, S[f"parts_stored{mm}"], 16 * i)
            three([PARTS[:, mm, r, 0:w] for r in range(3)], FQ[:, mm, 0:w], FR[:, 0:w], ch) \
                .then_inc(S["parts_ready"], 1)
            ve.wait_ge(S["parts_ready"], u + 1)
            ve.tensor_tensor(SQ[:, mm, 0:w], FQ[:, mm, 0:w], FQ[:, mm, 0:w], ALU.mult).then_inc(S["squares"], 1)
            ve.wait_ge(S["squares"], u + 1)

        def lower_parts(u, w, mm):
            ve.wait_ge(S["squares"], u + 1)
            hi, mid, lo = (PARTS[:, mm, r, 0:w] for r in range(3))
            ch(ve.tensor_tensor(FR[:, 0:w], FQ[:, mm, 0:w], hi, ALU.subtract))
            ch(ve.tensor_copy(mid, FR[:, 0:w]))
            ve.tensor_tensor(lo, FR[:, 0:w], mid, ALU.subtract).then_inc(S["parts_ready"], 1)
            ve.wait_ge(S["parts_ready"], u + 1)

        def k_norm(i, a, n, w):
            ve.wait_ge(S["norms"], i + 1)
            ve.tensor_reduce(sm(KM + 4 * a + n, 1, HEADS), PS[0:HEADS, 6, 0:w], AX, ALU.max) \
                .then_inc(S["norms_taken"], 1)
            ve.wait_ge(S["norms_taken"], i + 1)
            if n == CHUNKS - 1:
                ch(ve.tensor_reduce(sm(KMT + a, 1, HEADS), sm(KM + 4 * a, 4, HEADS), AX, ALU.max))
                ch(ve.tensor_scalar(sm(NCF + a, 1, HEADS), sm(KMT + a, 1, HEADS), -1.0 / (2 * AMGM), None,
                                    ALU.mult))

        def shift_rows(j):
            wait(ve, S["shift_stored"], 16 * j)
            three([Rp[:, r, :] for r in range(3)], R[:], FR[0:HEADS, :], ch).then_inc(S["shift_ready"], 1)
            ve.wait_ge(S["shift_ready"], j + 1)

        def q_norm(i, n, bank):
            ve.wait_ge(S["norms"], i + 1)
            ch(ve.tensor_scalar(R[:], PS[0:HEADS, bank, :], sm(NCF + 1, 1, HEADS), -AMGM / 2,
                                ALU.mult, ALU.add))
            ve.tensor_reduce(small[0:HEADS, bass.ds(QM + n, 1)], PS[0:HEADS, bank, :], AX, ALU.max) \
                .then_inc(S["norms_taken"], 1)
            ve.wait_ge(S["norms_taken"], i + 1)
            shift_rows(CHUNKS + n)

        ve.wait_ge(S["const_loaded"], 16 * (4 + len(ROWS0) + len(ROWS1)))
        split_unit, took = CK, 0
        for u, kind, n, w, mm in stage1:
            if kind == "norm":
                k_norm(n, 1, n, w)
            if kind == "k":
                lower_parts(split_unit, w, mm)
                split_unit += 1
            if kind == "k" and split_unit == 1:
                ve.wait_ge(S["x_loaded"], 16)
                for i in range(TILES):
                    ins = ve.bn_stats(sm(96 + 6 * i, 6), X[:, i, :])
                ch(ins)
                for i in range(TILES):
                    ins = ve.bn_aggr(sm(AGX + 2 * i, 2), sm(96 + 6 * i, 6))
                ch(ins)
                rsqrt(TILES, ch, ag=AGX, y=sm(NYX, TILES), tmp=(128, 144, 160, 176))
            if kind in ("tokT", "v"):
                ve.wait_ge(S["ctx_unit"], u + 1)
                kr = key_rows(1, n)
                if kind == "tokT":
                    ve.tensor_tensor(tokT[0:kr, n, :], PS[0:kr, u % 4, 0:D], row("L0_xattn_b_proj")[0:kr],
                                     ALU.add).then_inc(S["ctx_taken_dve"], 1)
                else:
                    if n == 0:
                        ve.wait_ge(S["v_cleared"], 2)
                    ve.tensor_tensor(V[0:kr, n, :, 0:HD],
                                     PS[0:kr, u % 4, 0:D].rearrange("p (h e) -> p h e", h=HEADS),
                                     row("L1_xattn_ca_bv")[0:kr].rearrange("p (h e) -> p h e", h=HEADS),
                                     ALU.add).then_inc(S["ctx_taken_dve"], 1)
                took += 1
        ve.wait_ge(S["ctx_taken_dve"], took)
        def ln1(n):
            for tt in range(TPC):
                ins = ve.bn_stats(sm(LN1 + 6 * tt, 6), X[:, n * TPC + tt, :])
            ch(ins)
            for tt in range(TPC):
                ins = ve.bn_aggr(sm(LN1 + 24 + 2 * tt, 2), sm(LN1 + 6 * tt, 6))
            ch(ins)
            rsqrt(TPC, ch, ag=LN1 + 24, y=sm(LN1 + 32, TPC), tmp=tuple(LN1 + 36 + TPC * r for r in range(4)))
            wait(ve, S["ln1_T"], n - 1)
            for tt in range(TPC):
                ins = ve.tensor_scalar(XH1[:, n % 2, tt, :], X[:, n * TPC + tt, :], sm(LN1 + 24 + 2 * tt), sm(LN1 + 32 + tt),
                                       ALU.subtract, ALU.mult)
            ins.then_inc(S["ln1_hat"], 1)
            ve.wait_ge(S["ln1_hat"], n + 1)

        def l0(i, par, scores, routed, gates, finish):
            if scores:
                ve.wait_ge(S["l0_scores"], i + 1)
                ch(ve.tensor_reduce(sm(NEGR + par), flat[:, 0:L], AX, ALU.max, negate=True))
                ve.tensor_scalar(sm(NEGM + par), sm(NEGR + par), SCALE0, None, ALU.mult) \
                    .then_inc(S["l0_negmax"], 1)
                ve.wait_ge(S["l0_negmax"], i + 1)
            if routed:
                ve.wait_ge(S["l0_routed"], i)
                ch(ve.reciprocal(sm(RS0), sm(SUM0 + 1 - par)))
                ch(ve.tensor_scalar(E1[:], PS[:, 6, 0:D], sm(RS0), None, ALU.mult))
                stats(E1[:], 1, ch)
            if routed or finish:
                rsqrt(routed + finish, ch, i=0 if finish else 1)
            if routed:
                ve.tensor_scalar(XHS[:, 1 - par, 1, :], E1[:], sm(AG + 2), sm(NY + 1), ALU.subtract, ALU.mult)
                ve.tensor_scalar(XHS[:, 1 - par, 0, :], X[:, bass.ds(i - 1, 1), :].rearrange("p o d -> p (o d)"),
                                 small[:, bass.ds(AGX + 2 * (i - 1), 1)], small[:, bass.ds(NYX + i - 1, 1)],
                                 ALU.subtract, ALU.mult).then_inc(S["l0_hat"], 1)
                ve.wait_ge(S["l0_hat"], i)
            if gates:
                ve.wait_ge(S["l0_rtanh"], i - 1)
                ve.tensor_tensor(UZ[:], PS[:, 7, D:2 * D], row("L0_xattn_b_u"), ALU.add) \
                    .then_inc(S["l0_ubiased"], 1)
                ve.wait_ge(S["l0_ubiased"], i - 1)
                ch(ve.tensor_scalar(RPS[:], TR[:], 0.5, 0.5, ALU.mult, ALU.add))
                ve.tensor_tensor(RPS[:], RPS[:], CF[:, par, 0:2, :], ALU.mult).then_inc(S["l0_rps"], 1)
                ve.wait_ge(S["l0_rps"], i - 1)
            if finish:
                xt = X[:, bass.ds(i - 3, 1), :].rearrange("p o d -> p (o d)")
                ch(ve.tensor_scalar(E2[:], E2[:], sm(AG), sm(NY), ALU.subtract, ALU.mult))
                ch(ve.tensor_tensor(E2[:], E2[:], row("L0_xattn_g_out"), ALU.mult))
                ve.tensor_tensor(xt, E2[:], row("L0_xattn_beta_out"), ALU.add).then_inc(S["l0_x1"], 1)
                ve.wait_ge(S["l0_x1"], i - 2)
            if isinstance(i, int) and i == TILES + 1:
                ln1(0)
            if gates:
                ve.wait_ge(S["l0_candps"], i - 1)
                ve.tensor_tensor(CZ[:], PS[:, 6, 0:D], row("L0_xattn_b_n"), ALU.add) \
                    .then_inc(S["l0_candz"], 1)
                ve.wait_ge(S["l0_candz"], i - 1)
                ve.wait_ge(S["l0_cand"], i - 1)
                xt = X[:, bass.ds(i - 2, 1), :].rearrange("p o d -> p (o d)")
                ch(ve.tensor_tensor(E2[:], CD[:], xt, ALU.subtract))
                ch(ve.scalar_tensor_tensor(out=E2[:], in0=TU[:], scalar=1.0, in1=E2[:],
                                           op0=ALU.add, op1=ALU.mult))
                ch(ve.scalar_tensor_tensor(out=E2[:], in0=E2[:], scalar=0.5, in1=xt,
                                           op0=ALU.mult, op1=ALU.add))
                stats(E2[:], 0, ch)

        for i in range(4):
            l0(i, i % 2, True, i >= 1, i >= 2, i >= 3)
        per_tile = 25
        before = ch.n
        with ve.Fori(2, TILES // 2) as k:
            for par in range(2):
                ch.base, ch.n = before + (2 * k + par - 4) * per_tile, 0
                l0(2 * k + par, par, True, True, True, True)
                assert ch.n == per_tile, ch.n
        ch.base, ch.n = 0, before + (TILES - 4) * per_tile
        for i in range(TILES, TILES + 3):
            l0(i, i % 2, False, i < TILES + 1, i < TILES + 2, True)
            if i == TILES + 1:
                ln1(1)

        split_unit = SQK
        for u, kind, n, w, mm in stage3:
            if kind == "LN":
                ln1(n)
            if kind == "norm" and n % 2 == 1:
                k_norm(n, 0, (n - CHUNKS) // 2, w)
            elif kind == "norm":
                c = (n - CHUNKS) // 2
                ve.wait_ge(S["norms"], n + 1)
                ch(ve.tensor_copy(NQ[:, c, :], PS[0:HEADS, 6, :]))
                ve.tensor_reduce(sm(QM + c, 1, HEADS), PS[0:HEADS, 6, :], AX, ALU.max) \
                    .then_inc(S["norms_taken"], 1)
                ve.wait_ge(S["norms_taken"], n + 1)
            if kind == "v":
                ve.wait_ge(S["qkv_unit"], u + 1)
                if n == 0:
                    ve.wait_ge(S["v_cross_stored"], 16)
                ve.tensor_tensor(V[:, n, :, 0:HD],
                                 PS[:, u % 4, 0:D].rearrange("p (h e) -> p h e", h=HEADS),
                                 row("L1_xattn_sa_bv").rearrange("p (h e) -> p h e", h=HEADS),
                                 ALU.add).then_inc(S["v_unit_taken"], 1)
            if kind in ("k", "q"):
                lower_parts(split_unit, w, mm)
                split_unit += 1

        for a in range(2):
            NK, at = NKS[a], A[a]
            def self_shift(c):
                ch(ve.tensor_scalar(R[:], NQ[:, c, :], sm(NCF, 1, HEADS), -AMGM / 2, ALU.mult, ALU.add))
                shift_rows(c)

            if a == 0:
                self_shift(0)
            ve.wait_ge(S["norms_taken"], (3 + a) * CHUNKS)
            ch(ve.tensor_reduce(sm(QMT, 1, HEADS), sm(QM, CHUNKS, HEADS), AX, ALU.max))
            ve.tensor_tensor(sm(TB + a, 1, HEADS), sm(QMT, 1, HEADS), sm(KMT + a, 1, HEADS), ALU.mult) \
                .then_inc(at["flag_row"], 1)
            ve.wait_ge(at["flag_row"], 2)
            ch(ve.tensor_reduce(sm(FM, 1, 1), PS[0:1, 7, 0:HEADS], AX, ALU.max))
            ve.tensor_scalar(flag[0:1, a:a + 1], sm(FM, 1, 1), BOUND * BOUND, None, ALU.is_le) \
                .then_inc(at["flag"], 1)
            ve.wait_ge(at["flag"], 1)
            if a == 0:
                for c in range(1, CHUNKS):
                    self_shift(c)
            bounded = ve.value_load(flag[0:1, a:a + 1], min_val=0, max_val=1)
            with ve.If(bounded < 1):
                gch = Chain(ve, at["g_chain"])
                with ve.Fori(0, CHUNKS) as c:
                    gch.base, gch.n = c * 3, 0
                    for g in range(GROUPS):
                        for j in range(GH):
                            for tt in range(TPC):
                                n = (c * GROUPS + g) * GH * TPC + j * TPC + tt
                                ve.wait_ge(at["g_scores"], n + 1)
                                ve.tensor_reduce(sm(MX + tt * HEADS + g * GH + j), flat[:, 0:KEYS[a]], AX,
                                                 ALU.max, negate=True).then_inc(at["g_max"], 1)
                                ve.wait_ge(at["g_max"], n + 1)
                    ve.wait_ge(at["g_rows"], c + 1)
                    three([Rp[:, r, :] for r in range(3)], PS[0:HEADS, 4, :], FR[0:HEADS, :], gch) \
                        .then_inc(at["g_split"], 1)
                    ve.wait_ge(at["g_split"], c + 1)
                    ve.wait_ge(at["g_stored"], 16 * (c + 1))

            def copy_heads(c, g):
                u = c * GROUPS + g - 1
                ve.wait_ge(at["pv"], (u + 1) * NK)
                ve.tensor_copy(OT[:, (g - 1) % 2, :], PS[:, 6, :]).then_inc(at["heads"], 1)
                ve.wait_ge(at["heads"], u + 1)

            def sums(c, g):
                u = c * GROUPS + g - 1
                ve.wait_ge(at["sums"], u + 1)
                ve.tensor_copy(REC[:], PS[:, 7, :]).then_inc(at["sums_taken"], 1)
                ve.wait_ge(at["sums_taken"], u + 1)

            def divide(c, g, half):
                u = c * GROUPS + g - 1
                part = REC[:, half * D:(half + 1) * D]
                ch(ve.reciprocal(part, part))
                if half == 0:
                    return
                if g == 1 and not isinstance(c, int):
                    ve.wait_ge(at["y"], c * TPC)
                ve.tensor_tensor(ONF[:, (g - 1) % GROUPS, :], OT[:, (g - 1) % 2, :], REC[:], ALU.mult) \
                    .then_inc(at["normed"], 1)
                ve.wait_ge(at["normed"], u + 1)

            def standardise(q):
                rsqrt(TPC, ch)
                for tt in range(TPC):
                    ins = ve.tensor_scalar(
                        XH[:, tt, :], X[:, bass.ds(q * TPC + tt, 1), :].rearrange("p o d -> p (o d)"),
                        sm(AG + 2 * tt), sm(NY + tt), ALU.subtract, ALU.mult)
                ins.then_inc(at["hat"], 1)
                ve.wait_ge(at["hat"], q + 1)

            def piece(kind, i, q, tail=False):
                if kind in "yo":
                    xt = X[:, bass.ds(q * TPC + i, 1), :].rearrange("p o d -> p (o d)")
                if kind == "y":
                    ve.wait_ge(at["y"], q * TPC + i + 1)
                    ve.tensor_tensor(XH[:, i, :], PS[:, i if tail else 7, 0:D], row(("L1_xattn_sa_bo", "L1_xattn_ca_bo")[a]),
                                     ALU.add).then_inc(at["y_taken"], 1)
                    ve.wait_ge(at["y_taken"], q * TPC + i + 1)
                    ch(ve.tensor_tensor(xt, XH[:, i, :], xt, ALU.add))
                    stats(xt, i, ch)
                if kind == "h":
                    ln = ("L1_xattn_ln2_", "L1_xattn_ln3_")[a]
                    ve.wait_ge(at["hT"], 2 * q + i + 1)
                    ve.tensor_scalar(HC[:, i, :], PS[:, i if tail else 7, :], col(ln + "g", i), col(ln + "b", i),
                                     ALU.mult, ALU.add).then_inc(at["hc"], 1)
                    ve.wait_ge(at["hc"], 2 * q + i + 1)
                if kind == "u":
                    if tail:
                        lower_parts(CQ + 2 * q + i, CHUNK, i)
                        return
                    ve.wait_ge(at["unit"], 2 * q + i + 1)
                    ve.tensor_scalar(FQ[:, i, :], PS[:, i if tail else 7, :], col("L1_xattn_ca_bq", i), None, ALU.add) \
                        .then_inc(at["unit_taken"], 1)
                    ve.wait_ge(at["unit_taken"], 2 * q + i + 1)
                    parts(CQ // 2 + q, CHUNK, i)
                if kind == "n":
                    q_norm(3 * CHUNKS + q, q, 7)
                if kind == "m" and not tail:
                    ve.wait_ge(at["unit"], HID // P * q + i + 1)
                    ve.tensor_scalar(HIDT[:, i, :], PS[:, 7, :], col("L1_xattn_mlp_b1", i), None, ALU.add) \
                        .then_inc(at["unit_taken"], 1)
                    ve.wait_ge(at["unit_taken"], HID // P * q + i + 1)
                if kind == "o":
                    ve.wait_ge(at["mlp"], q * TPC + i + 1)
                    ve.tensor_tensor(XH[:, i, :], PS[:, i if tail else 7, 0:D], row("L1_xattn_mlp_b2"), ALU.add) \
                        .then_inc(at["mlp_taken"], 1)
                    ve.wait_ge(at["mlp_taken"], q * TPC + i + 1)
                    ve.tensor_tensor(XH[:, i, :], XH[:, i, :], xt, ALU.add).then_inc(at["out_ready"], 1)
                    ve.wait_ge(at["out_ready"], q * TPC + i + 1)

            def chunk(c, first):
                ev = events(a, None if first else c)
                for t in range(GROUPS * NK):
                    for kind, i, part, last in ev[t]:
                        if kind == "copy":
                            copy_heads(c, i)
                        elif kind == "sums":
                            sums(c, i)
                        elif kind == "divide":
                            divide(c, i, part)
                        elif kind == "hat":
                            standardise(c - 1)
                        elif last:
                            piece(kind, i, c - 1)
                if a == 1 and not first:
                    ve.wait_ge(S["out_stored"], 16 * TPC * c)

            chunk(0, True)
            before = ch.n
            per_chunk = (42, 32)[a]
            with ve.Fori(1, CHUNKS) as c:
                ch.base, ch.n = before + (c - 1) * per_chunk, 0
                chunk(c, False)
                assert ch.n == per_chunk, ch.n
            ch.base, ch.n = 0, before + (CHUNKS - 1) * per_chunk
            copy_heads(CHUNKS, 0)
            sums(CHUNKS, 0)
            for half in range(2):
                divide(CHUNKS, 0, half)
            for kind, at_steps in REST[a].items():
                for i in range(len(at_steps) // PARTS_OF[kind]):
                    piece(kind, i, CHUNKS - 1, True)
                if kind == "y":
                    standardise(CHUNKS - 1)


INPUTS = ["x", "xT", "ctxT", "Wproj", "Wu", "Wr", "Wn", "saq", "sak", "sav", "caq", "cak", "cav",
          "sawo", "cawo", "w1T", "w2T", "cols", "rows0", "rows1", "headsum", "ident", "spread", "ones"]


def kernel(**inputs):
    import numpy as _np
    import concourse.bacc as _bacc
    from concourse import mybir as _mybir
    from concourse.bass_utils import run_bass_kernel_spmd as _run

    v = {n: _np.asarray(a) for n, a in inputs.items()}
    x, c = v["x"][0], v["ctx_768"][0]
    data = {
        "x": x, "xT": x.T, "ctxT": c.T, "Wproj": v["L0_xattn_W_proj"],
        "Wu": v["L0_xattn_W_u"], "Wr": v["L0_xattn_W_r"], "Wn": v["L0_xattn_W_n"],
        "saq": v["L1_xattn_sa_wq"].T, "sak": v["L1_xattn_sa_wk"].T, "sav": v["L1_xattn_sa_wv"].T,
        "caq": v["L1_xattn_ca_wq"].T, "cak": v["L1_xattn_ca_wk"].T, "cav": v["L1_xattn_ca_wv"].T,
        "sawo": v["L1_xattn_sa_wo"].T, "cawo": v["L1_xattn_ca_wo"].T,
        "w1T": v["L1_xattn_mlp_w1"].T, "w2T": v["L1_xattn_mlp_w2"].T,
        "cols": _np.concatenate([v[n].reshape(-1, P).T for n in COLS], 1),
        "rows0": _np.stack([v[n] for n in ROWS0]),
        "rows1": _np.stack([v[n] for n in ROWS1]),
    }
    headsum = _np.zeros((P, 2, HEADS), _np.float32)
    spread = _np.zeros((P, P), _np.float32)
    for p in range(P):
        for half in range(2):
            headsum[p, half, 8 * half + p // HD] = 1.0
        spread[32 * (p // 32) + HD, p] = 1.0
    ones = _np.full((NROW - ROWS, HEADS * T // 2), 0x3F803F80, _np.uint32).view(_np.float32)
    data.update(headsum=headsum, spread=spread, ident=_np.eye(P, dtype=_np.float32), ones=ones)

    nc = _bacc.Bacc("TRN2", target_bir_lowering=False, num_devices=1)
    arrays, d = {}, {}
    for n in INPUTS:
        a = _np.ascontiguousarray(data[n])
        arrays[f"in_{n}"] = a
        d[n] = nc.dram_tensor(f"in_{n}", a.shape, _mybir.dt.from_np(a.dtype), kind="ExternalInput").ap()
    out = nc.dram_tensor("out", (T, D), _mybir.dt.float32, kind="ExternalOutput").ap()
    program(nc, d, out)
    r = _run(nc, [arrays], core_ids=[0])
    return r.results[0]["out"].reshape(1, T, D)
```

```python
from contextlib import ExitStack

import numpy as np

import concourse.bass as bass
from concourse import mybir

F32 = mybir.dt.float32
BF16 = mybir.dt.bfloat16
I32 = mybir.dt.int32
ALU = mybir.AluOpType
ACT = mybir.ActivationFunctionType
AX = mybir.AxisListType.X

P = 128
T = 2048
L = 1601
D = 256
CTX = 192
KC = CTX // 2
TILES = T // P
CHUNK = 512
CHUNKS = T // CHUNK
TPC = CHUNK // P
LT = -(-L // P)
LLAST = L - (LT - 1) * P
HEADS, HD = 16, 16
GROUPS = 4
GH = HEADS // GROUPS
HID = 4 * D
SCALE = HD ** -0.5
SCALE0 = D ** -0.5
EPS = 1e-5
ROWS = 6 * HD
SROW = ROWS
NROW = ROWS + 3
QBLOCK = (0, 0, 0, 1, 1, 2)
KBLOCK = (0, 1, 2, 0, 1, 0)
BOUND = 32.0 / SCALE
AMGM = 64.0

COLS = ["L0_xattn_b_proj", "L0_xattn_g_state", "L0_xattn_beta_state", "L0_xattn_g_input",
        "L0_xattn_beta_input", "L0_xattn_b_r", "L1_xattn_ln1_g", "L1_xattn_ln1_b",
        "L1_xattn_ln2_g", "L1_xattn_ln2_b", "L1_xattn_ln3_g", "L1_xattn_ln3_b",
        "L1_xattn_sa_bq", "L1_xattn_sa_bk", "L1_xattn_ca_bq", "L1_xattn_ca_bk",
        "L1_xattn_mlp_b1"]
ROWS0 = ["L0_xattn_b_proj", "L0_xattn_b_u", "L0_xattn_b_n", "L0_xattn_g_out", "L0_xattn_beta_out",
         "L1_xattn_ca_bv"]
ROWS1 = ["L1_xattn_sa_bv", "L1_xattn_sa_bo", "L1_xattn_ca_bo", "L1_xattn_mlp_b2"]
NCOL = 2 * (len(COLS) - 1) + HID // P

PARTS_OF = {"y": 2, "h": 1, "u": 2, "n": 2, "m": 2, "o": 4, "flag": 1}
REST = [
    {"y": [5, 5, 8, 8, 11, 11, 14, 14], "h": [21, 23], "u": [26, 28, 30, 32], "n": [38, 40]},
    {"y": list(range(5, 13)), "h": [17, 18], "m": list(range(19, 27)) + list(range(29, 35)) + [35, 35],
     "o": [37, 37, 39, 39, 42, 42, 43, 43, 45, 45, 46, 46, 48, 48, 49, 49]},
]
LAST_REST = {"y": list(range(5, 13)), "h": [18, 19], "u": [22, 23, 24, 25], "n": [30, 31], "flag": [36]}
HAT_STEP = (16, 13)
GELU_STEP = 36
LOOK = 3

class Map:

    def __init__(self, nc, start, end):
        self.nc, self.at, self.end = nc, start, end

    def region(self, nbytes):
        off = self.at
        self.at += -(-nbytes // 32) * 32
        assert self.at <= self.end, (self.at, self.end)
        return off

    def put(self, name, shape, dt, off):
        return self.nc.alloc_sbuf_tensor_at(name, shape, dt, offset=off)

    def new(self, name, shape, dt):
        size = 2 if dt == BF16 else 4
        return self.put(name, shape, dt, self.region(int(np.prod(shape[1:])) * size))


class Chain:

    def __init__(self, eng, sem):
        self.eng, self.sem, self.base, self.n = eng, sem, 0, 0

    def __call__(self, ins):
        self.n += 1
        ins.then_inc(self.sem, 1)
        self.eng.wait_ge(self.sem, self.base + self.n)


def wait(eng, s, value):
    if not isinstance(value, int) or value > 0:
        eng.wait_ge(s, value)


def pieces(keys):
    return [(n, min(CHUNK, keys - n)) for n in range(0, keys, CHUNK)]


def program(nc, d, out):
    ctx = ExitStack()
    with ctx:
        build(nc, ctx, d, out)


def build(nc, ctx, d, out):
    def sem(name):
        return ctx.enter_context(nc.semaphore(name))

    m = Map(nc, -(-nc.sbuf_base // 32) * 32, nc.sbuf_usable_end)
    ident = m.new("ident", [P, P], F32)
    spread = m.new("spread", [P, P], F32)
    headsum = m.new("headsum", [P, 2, HEADS], F32)
    cols = m.new("cols", [P, NCOL], F32)
    rows1 = m.new("rows1", [P, len(ROWS1), D], F32)
    X = m.new("X", [P, TILES, D], F32)
    small = m.new("small", [P, 256], F32)
    flag = m.new("flag", [1, 3], I32)
    oKST = m.region(HEADS * T * 2)
    oV = m.region(TILES * HEADS * 32 * 4)
    oQST = m.region(HEADS * CHUNK * 2)
    oP = m.region(4 * 2 * CHUNK * 4)
    oON = m.region(GROUPS * CHUNK * 4 + 2 * CHUNK * 4)
    oREC = m.region(CHUNK * 4)
    oWOP = m.region(GROUPS * D * 4)
    oXH = m.region(TPC * D * 4 + 2 * CHUNK * 4)
    Rp = m.new("Rp", [HEADS, 3, CHUNK], BF16)
    oW1 = m.region(2 * HID * 4)
    oSCR = m.region(10 * CHUNK * 4)

    stack = m.put("stack", [P, HEADS * T], BF16, oKST)
    KST = [stack[:, 0:HEADS * n].rearrange("p (h n) -> p h n", h=HEADS) for n in (T, L + 3)]
    V = m.put("V", [P, TILES, HEADS, 32], F32, oV)
    QST = m.put("QST", [P, HEADS, CHUNK], BF16, oQST)
    PX = m.put("PX", [P, 4, 2, CHUNK], F32, oP)
    ONF = m.put("ONF", [P, GROUPS, CHUNK], F32, oON)
    OT = m.put("OT", [P, 2, CHUNK], F32, oON + GROUPS * CHUNK * 4)
    REC = m.put("REC", [P, CHUNK], F32, oREC)
    WOP = m.put("WOP", [P, GROUPS, D], F32, oWOP)
    XH = m.put("XH", [P, TPC, D], F32, oXH)
    HC = m.put("HC", [P, 2, CHUNK], F32, oXH + TPC * D * 4)
    W1 = m.put("W1", [P, 2, HID], F32, oW1)
    W2 = m.put("W2", [P, HID // P, D], F32, oKST + -(-HEADS * (L + 3) * 2 // 32) * 32)
    HIDT = m.put("HIDT", [P, HID // P, CHUNK], F32, oSCR)
    s = Map(nc, oSCR, m.at)
    FQ = s.new("FQ", [P, 2, CHUNK], F32)
    FR = s.new("FR", [P, CHUNK], F32)
    SQ = s.new("SQ", [P, 2, CHUNK], F32)
    PARTS = s.new("PARTS", [P, 2, 3, CHUNK], BF16)
    R = s.new("R", [HEADS, CHUNK], F32)
    CAWQ = s.new("CAWQ", [P, 2, D], F32)
    NQ = m.put("NQ", [HEADS, CHUNKS, CHUNK], F32, oON)
    assert CHUNKS * CHUNK * 4 + 12 * CHUNK <= oWOP - oON
    KPARTS = m.put("KPARTS", [P, 2, 3, CHUNK], BF16, oON + CHUNKS * CHUNK * 4)
    hF = m.put("hF", [P, 2, T], F32, oP)
    SAW = m.put("SAW", [P, 3, 2, D], F32, oXH)
    s = Map(nc, oKST, oV)
    ctxT = s.new("ctxT", [KC, 2, L], F32)
    tokF = s.new("tokF", [P, 2, L], F32)
    tokT = s.new("tokT", [P, LT, D], F32)
    WPJ = s.new("WPJ", [KC, 2, D], F32)
    CAKV = s.new("CAKV", [KC, 2, 2, D], F32)
    PR = s.new("PR", [P, L], F32)
    PT = s.new("PT", [P, LT, P], F32)
    rows0 = s.new("rows0", [P, len(ROWS0), D], F32)
    s = Map(nc, oQST, oP)
    CF = s.new("CF", [P, 2, 4, P], F32)
    XT = s.new("XT", [P, 2, 2, P], F32)
    XHS = s.new("XHS", [P, 2, 2, D], F32)
    RPS = s.new("RPS", [P, 2, P], F32)
    TR = s.new("TR", [P, 2, P], F32)
    TU = s.new("TU", [P, D], F32)
    W0 = m.put("W0", [P, 3, 4, D], F32, oON)
    XH1 = m.put("XH1", [P, 2, D], F32, oW1)
    UZ = m.put("UZ", [P, D], F32, oREC)
    CZ = m.put("CZ", [P, D], F32, oREC + D * 4)
    CD = m.put("CD", [P, D], F32, oWOP)
    E1 = m.put("E1", [P, D], F32, oWOP + D * 4)
    E2 = m.put("E2", [P, D], F32, oWOP + 2 * D * 4)
    PS = ctx.enter_context(nc.psum_tensor("PS", [P, 8, CHUNK], F32))
    flat = PS[:, :, :].rearrange("p b n -> p (b n)")

    qd = [nc.dram_tensor(f"q_parts_{a}", [3, D, T], BF16, kind="Internal").ap() for a in range(2)]
    kd = [nc.dram_tensor(f"k_parts_{a}", [3, D, (T, L)[a]], BF16, kind="Internal").ap() for a in range(2)]
    sd = [nc.dram_tensor(f"shift_{a}", [3, HEADS, T], BF16, kind="Internal").ap() for a in range(2)]
    vd = nc.dram_tensor("v_cross", [P, LT * HEADS * 32], F32, kind="Internal").ap()

    def col(name, c=0):
        i = 2 * COLS.index(name) + c
        return cols[:, i:i + 1]

    def row(name):
        if name in ROWS0:
            return rows0[:, ROWS0.index(name), :]
        return rows1[:, ROWS1.index(name), :]

    BRH, NEGM, NEGR, SUM0, RS0, STAT, AG, NVAR, NA, NB, NY, NI = 0, 2, 4, 6, 8, 10, 40, 50, 54, 58, 62, 66
    KM, KMT, NCF, QM, QMT, TB, FM, MX = 70, 80, 82, 84, 92, 94, 97, 128
    AGX, NYX = 192, 224

    def sm(o, n=1, p=P):
        return small[0:p, o:o + n]

    names = """const_loaded x_loaded w0_loaded wproj_loaded cakv_loaded cols_loaded rows1_loaded
        saw_loaded w1_loaded w2_loaded v_cleared ones_loaded half_bias dve_chain dve_stepped
        pool_stepped ctx_unit ctx_taken_act ctx_taken_dve parts_ready parts_stored0 parts_stored1
        k_parts_stored0 k_parts_stored1 squares norms norms_taken shift_ready shift_stored
        v_cross_stored
        l0_scores l0_negmax l0_exp l0_pT l0_pT_taken l0_routed l0_hat l0_hatT l0_concat
        l0_gates l0_rtanh l0_ubiased l0_utanh l0_rps l0_candps l0_candz l0_cand l0_x1
        ln1_hat ln1_T ln1_taken qkv_unit v_unit_taken wop_cleared out_stored""".split()
    S = {n: sem(n) for n in names}
    s_ctx = [sem(f"ctx_loaded{i}") for i in range(len(pieces(L)))]
    s_xt = [sem(f"xt_loaded{i}") for i in range(2)]
    per = """scores exp pv heads sums sums_taken normed y y_taken hat hT hc unit unit_taken gelu mlp
        mlp_taken out_ready flag_row flag wop""".split()
    A = [{n: sem(f"{('self', 'cross')[a]}_{n}") for n in per} for a in range(2)]
    maxima = "q scores max rows split stored chain".split()
    G = [{n: sem(f"{f}_exact_{n}") for n in maxima} for f in ("self", "cross", "last")]
    DECIDES = ((0, 0, CHUNKS), (1, 0, CHUNKS - 1), (1, CHUNKS - 1, 1))
    s_kst = [[sem(f"k_stack{a}_{g}") for g in range(GROUPS)] for a in range(2)]
    s_vst = [sem(f"v_cross_loaded{g}") for g in range(GROUPS)]
    s_qst = [[sem(f"q_stack{a}_{g}") for g in range(GROUPS)] for a in range(2)]

    NKS = (TILES, LT)
    KEYS = (T, L)

    def key_rows(a, kt):
        return min(P, KEYS[a] - kt * P)

    CK, SQK, CQ = 0, 2 * CHUNKS, 6 * CHUNKS

    def numbered(entries):
        out, u = [], 0
        for e in entries:
            out.append((None if e[0] in ("norm", "T", "shift") else u,) + e)
            u += e[0] not in ("norm", "T", "shift")
        return out

    pcs = pieces(L)
    stage1 = ([("tokF", n, w, mm) for n, w in pcs for mm in range(2)] + [("tokT", kt, 0, 0) for kt in range(LT)])
    for i, (n, w) in enumerate(pcs):
        stage1 += [("k", n, w, mm) for mm in range(2)]
        stage1 += [("v", kt, 0, 0) for kt in range(LT * i // len(pcs), LT * (i + 1) // len(pcs))]
        stage1 += [("norm", i, w, 0)]
    stage1 = numbered(stage1)
    stage3 = []
    for n in range(CHUNKS):
        stage3 += [("q", n * CHUNK, CHUNK, mm) for mm in range(2)]
        if n == 0:
            stage3 += [("T", i, 0, 0) for i in range(TILES - 2, TILES)]
        stage3 += [("k", n * CHUNK, CHUNK, 0), ("norm", CHUNKS + 2 * n, CHUNK, 0), ("k", n * CHUNK, CHUNK, 1)]
        vs = [("v", kt, 0, 0) for kt in range(n * TPC, (n + 1) * TPC)]
        k_norm_ = [("norm", CHUNKS + 2 * n + 1, CHUNK, 0)]
        stage3 += vs + k_norm_ if n + 1 < CHUNKS else k_norm_ + [("shift", 0, 0, 0)] + vs
    stage3 = numbered(stage3)

    def taken(plan, u, before):
        kinds = [e[1] for e in plan if e[0] is not None]
        kind = kinds[u]
        if kind in ("k", "q"):
            return S["squares"], before + sum(k in ("k", "q") for k in kinds[:u + 1])
        if kind == "tokF":
            return S["ctx_taken_act"], kinds[:u + 1].count("tokF")
        if before:
            return S["v_unit_taken"], kinds[:u + 1].count("v")
        return S["ctx_taken_dve"], sum(k in ("tokT", "v") for k in kinds[:u + 1])

    def part_buffer(u):
        i, mm = u // 2, u % 2
        if CHUNKS <= i < 3 * CHUNKS and (i - CHUNKS) % 2:
            return KPARTS[:, mm], S[f"k_parts_stored{mm}"], (i - CHUNKS) // 2
        n = i if i < CHUNKS else CHUNKS + (i - CHUNKS) // 2 if i < 3 * CHUNKS else i - CHUNKS
        return PARTS[:, mm], S[f"parts_stored{mm}"], n

    def wait_parts_stored(eng, n, kind=""):
        for mm in range(2):
            eng.wait_ge(S[f"{kind}parts_stored{mm}"], 16 * n)

    def events(a, first):
        NK = NKS[a]
        ev = {t: [] for t in range(GROUPS * NK)}

        def divide_unit(o, t, g):
            ev[t].append((o, "copy", g, 0, True))
            ev[t + 2].append((o, "sums", g, 0, True))
            ev[t + 3].append((o, "divide", g, 0, False))
            ev[t + 4].append((o, "divide", g, 1, True))

        o, rest = (a, REST[a]) if not first else (0, LAST_REST)
        for g in range(GROUPS):
            if g or not first:
                divide_unit(a, g * NK, g)
            elif a == 1:
                divide_unit(0, 0, 0)
        if a == 1 or not first:
            for kind, at in rest.items():
                n = PARTS_OF[kind]
                for j, t in enumerate(at):
                    ev[t].append((o, kind, j // n, j % n, j % n == n - 1))
            ev[HAT_STEP[a]].append((o, "hat", 0, 0, True))
        return ev

    def decision(f):
        return (3, 4, 2) if f == 2 else (1, 2, 1)

    block = ctx.enter_context(nc.Block())

    @block.sync
    def _(sp):
        sp.dma_start(WPJ[:], d["Wproj"].rearrange("(c p) n -> p c n", p=KC)).then_inc(S["wproj_loaded"], 16)
        for i, (n, w) in enumerate(pcs):
            sp.dma_start(ctxT[:, :, n:n + w], d["ctxT"].rearrange("(c p) l -> p c l", p=KC)[:, :, n:n + w]) \
                .then_inc(s_ctx[i], 16)
            if i == 0:
                sp.dma_start(cols[:], d["cols"]).then_inc(S["cols_loaded"], 16)
        for i in range(len(ROWS0)):
            sp.dma_start(rows0[:, i, :], d["rows0"][i, :].partition_broadcast(P)).then_inc(S["const_loaded"], 16)
            if i == 0:
                for j, n in enumerate(("cak", "cav")):
                    sp.dma_start(CAKV[:, j], d[n].rearrange("(c p) n -> p c n", p=KC)).then_inc(S["cakv_loaded"], 16)
        sp.dma_start(headsum[:], d["headsum"]).then_inc(S["const_loaded"], 16)
        sp.dma_start(ident[:], d["ident"]).then_inc(S["const_loaded"], 16)
        sp.dma_start(spread[:], d["spread"]).then_inc(S["const_loaded"], 16)
        for i in range(2):
            sp.dma_start(XT[:, i], d["xT"].rearrange("(c p) t -> p c t", p=P)[:, :, i * P:(i + 1) * P]) \
                .then_inc(s_xt[i], 16)
        sp.dma_start(X[:], d["x"].rearrange("(n p) d -> p n d", p=P)).then_inc(S["x_loaded"], 16)
        for i, n in enumerate(("Wu", "Wr", "Wn")):
            sp.dma_start(W0[:, i], d[n].rearrange("(c p) n -> p c n", p=P)).then_inc(S["w0_loaded"], 16)
        for i in range(len(ROWS1)):
            sp.dma_start(rows1[:, i, :], d["rows1"][i, :].partition_broadcast(P)).then_inc(S["rows1_loaded"], 16)
        for i, n in enumerate(("saq", "sak", "sav")):
            sp.dma_start(SAW[:, i], d[n].rearrange("(c p) n -> p c n", p=P)).then_inc(S["saw_loaded"], 16)
        sp.dma_start(CAWQ[:], d["caq"].rearrange("(c p) n -> p c n", p=P)).then_inc(S["saw_loaded"], 16)
        with sp.Fori(1, TILES // 2) as k:
            for par in range(2):
                sp.wait_ge(S["l0_scores"], 2 * k - 1 + par)
                sp.dma_start(XT[:, par], d["xT"].rearrange("(c p) t -> p c t", p=P)
                             [:, :, bass.ds((2 * k + par) * P, P)]).then_inc(s_xt[par], 16)
        sp.wait_ge(S["wop_cleared"], 1)
        for j in range(GH):
            sp.dma_start(WOP[32 * j:32 * j + HD, :, :],
                         d["sawo"].rearrange("(g j d) n -> j d g n", g=GROUPS, j=GH)[j]) \
                .then_inc(A[0]["wop"], 16)
        for a in range(2):
            steps = GROUPS * NKS[a]
            def load_q(c, g, s_to):
                for b, part in enumerate(QBLOCK):
                    sp.dma_start(QST[b * HD:(b + 1) * HD, g * GH:(g + 1) * GH, :],
                                 qd[a][part, g * GH * HD:(g + 1) * GH * HD, bass.ds(c * CHUNK, CHUNK)]
                                 .rearrange("(j d) n -> d j n", j=GH)).then_inc(s_to, 16)

            def load_shift(c, g, s_to):
                sp.dma_start(QST[SROW:NROW, g * GH:(g + 1) * GH, :],
                             sd[a][:, g * GH:(g + 1) * GH, bass.ds(c * CHUNK, CHUNK)]).then_inc(s_to, 16)

            if a == 0:
                sp.wait_ge(S["l0_x1"], TILES)
                sp.dma_start(stack[SROW:NROW, :].bitcast(F32), d["ones"]).then_inc(S["ones_loaded"], 16)
                for n in range(CHUNKS):
                    if n == 1:
                        wait_parts_stored(sp, CHUNKS + 1)
                        for g in range(GROUPS):
                            load_q(0, g, s_qst[0][g])
                    wait_parts_stored(sp, n + 1, "k_")
                    for b, part in enumerate(KBLOCK):
                        sp.dma_start(KST[0][b * HD:(b + 1) * HD, :, n * CHUNK:(n + 1) * CHUNK],
                                     kd[0][part, :, n * CHUNK:(n + 1) * CHUNK]
                                     .rearrange("(j d) n -> d j n", j=HEADS)).then_inc(s_kst[0][0], 16)
                sp.wait_ge(S["shift_stored"], 16)
                for g in range(GROUPS):
                    load_shift(0, g, s_qst[0][g])
            else:
                wait_parts_stored(sp, 2 * CHUNKS + 1)
                sp.wait_ge(S["shift_stored"], 16 * (CHUNKS + 1))
                sp.wait_ge(S["v_cross_stored"], 16)
                for g in range(GROUPS):
                    last = (CHUNKS - 1) * GROUPS * NKS[0] + (g + 1) * NKS[0]
                    sp.wait_ge(A[0]["scores"], 2 * last)
                    for b, part in enumerate(KBLOCK):
                        sp.dma_start(KST[1][b * HD:(b + 1) * HD, g * GH:(g + 1) * GH, 0:L],
                                     kd[1][part, g * GH * HD:(g + 1) * GH * HD, :]
                                     .rearrange("(j d) n -> d j n", j=GH)).then_inc(s_kst[1][g], 16)
                    load_q(0, g, s_qst[1][g])
                    load_shift(0, g, s_qst[1][g])
                    sp.wait_ge(A[0]["pv"], last)
                    sp.dma_start(V[:, 0:LT, g * GH:(g + 1) * GH, :],
                                 vd.rearrange("p (k h e) -> p k h e", k=LT, h=HEADS)[:, :, g * GH:(g + 1) * GH, :]) \
                        .then_inc(s_vst[g], 16)

            def general(f):
                _, c0, n = DECIDES[f]
                sp.wait_ge(A[a]["flag"], decision(f)[2])
                bounded = sp.value_load(flag[0:1, f:f + 1], min_val=0, max_val=1)

                def one(c):
                    for g in range(GROUPS):
                        if g:
                            sp.wait_ge(G[f]["max"], (c * GROUPS + g) * GH * TPC)
                        load_q(c0 + c, g, G[f]["q"])
                    sp.wait_ge(G[f]["split"], c + 1)
                    sp.dma_start(sd[a][:, :, bass.ds((c0 + c) * CHUNK, CHUNK)].rearrange("r h n -> h r n"), Rp[:]) \
                        .then_inc(G[f]["stored"], 16)

                with sp.If(bounded < 1):
                    wait_parts_stored(sp, (1 + a) * CHUNKS + c0 + n)
                    sp.wait_ge(S["shift_stored"], 16 * (a * CHUNKS + c0 + n))
                    if f == 2:
                        sp.wait_ge(A[a]["scores"], 2 * steps)
                        one(0)
                    else:
                        for g in range(GROUPS):
                            sp.wait_ge(s_qst[a][g], 16 * (len(QBLOCK) + 1))
                        with sp.Fori(0, n) as c:
                            one(c)
                    sp.wait_ge(G[f]["stored"], 16 * n)
                    if f < 2:
                        for g in range(GROUPS):
                            load_q(0, g, G[f]["q"])
                            load_shift(0, g, G[f]["q"])

            general(a)

            if a == 0:
                sp.wait_ge(S["ln1_T"], TILES)
                sp.dma_start(W1[:], d["w1T"].rearrange("(c p) n -> p c n", p=P)).then_inc(S["w1_loaded"], 16)
            else:
                sp.dma_start(W2[:], d["w2T"].rearrange("(c p) n -> p c n", p=P)).then_inc(S["w2_loaded"], 16)
                sp.wait_ge(A[0]["y"], CHUNKS * TPC)
                for j in range(GH):
                    sp.dma_start(WOP[32 * j:32 * j + HD, :, :],
                                 d["cawo"].rearrange("(g j d) n -> j d g n", g=GROUPS, j=GH)[j]) \
                        .then_inc(A[1]["wop"], 16)
                general(2)
            wait_parts_stored(sp, (2 + a) * CHUNKS)
            sp.wait_ge(S["shift_stored"], 16 * CHUNKS * (a + 1))
            with sp.Fori(1, CHUNKS) as c:
                for g in range(GROUPS):
                    sp.wait_ge(A[a]["scores"], ((c - 1) * steps + (g + 1) * NKS[a]) * 2)
                    load_q(c, g, s_qst[a][g])
                    load_shift(c, g, s_qst[a][g])

    @block.gpsimd
    def _(gp):
        gp.memset(V[:], 0.0).then_inc(S["v_cleared"], 1)
        gp.wait_ge(S["v_cleared"], 1)
        gp.memset(V[:, :, :, HD:HD + 1], 1.0).then_inc(S["v_cleared"], 1)

        def store_parts(u, dst, n, w, mm, place=None):
            buffer, stored, _ = part_buffer(u if place is None else place)
            gp.wait_ge(S["parts_ready"], u + 1)
            gp.sem_inc(S["pool_stepped"], 1)
            gp.dma_start(dst[:, mm * P:(mm + 1) * P, bass.ds(n, w)].rearrange("r p n -> p r n"),
                         buffer[:, :, 0:w]).then_inc(stored, 16)

        def store_shift(i, a, n):
            gp.wait_ge(S["shift_ready"], i + 1)
            gp.sem_inc(S["pool_stepped"], 1)
            gp.dma_start(sd[a][:, :, bass.ds(n, CHUNK)].rearrange("r h n -> h r n"), Rp[:]) \
                .then_inc(S["shift_stored"], 16)

        for i, (n, w) in enumerate(pieces(L)):
            for mm in range(2):
                store_parts(CK + 2 * i + mm, kd[1], n, w, mm)
        gp.wait_ge(S["ctx_taken_dve"], 2 * LT)
        gp.dma_start(vd, V[:, 0:LT].rearrange("p k h e -> p (k h e)")).then_inc(S["v_cross_stored"], 16)
        gp.wait_ge(S["l0_x1"], TILES)
        gp.memset(WOP[:], 0.0).then_inc(S["wop_cleared"], 1)
        for i in range(CHUNKS):
            for half, dst in enumerate((qd[0], kd[0])):
                for mm in range(2):
                    store_parts(SQK + 4 * i + 2 * half + mm, dst, i * CHUNK, CHUNK, mm)
        for i in range(CHUNKS):
            store_shift(i, 0, i * CHUNK)
        with gp.Fori(0, CHUNKS) as c:
            for mm in range(2):
                store_parts(CQ + 2 * c + mm, qd[1], c * CHUNK, CHUNK, mm, CQ + mm)
            store_shift(CHUNKS + c, 1, c * CHUNK)
        with gp.Fori(0, CHUNKS) as c:
            for tt in range(TPC):
                gp.wait_ge(A[1]["out_ready"], c * TPC + tt + 1)
                gp.sem_inc(S["pool_stepped"], 1)
                gp.dma_start(out[bass.ds((c * TPC + tt) * P, P), :], XH[:, tt, :]) \
                    .then_inc(S["out_stored"], 16)
        gp.wait_ge(S["out_stored"], 16 * TILES)

    @block.scalar
    def _(act):
        act.wait_ge(S["cols_loaded"], 16)
        for c in range(2):
            act.mul(sm(BRH + c), col("L0_xattn_b_r", c), 0.5).then_inc(S["half_bias"], 1)
        act.wait_ge(S["half_bias"], 2)

        def split(u, bank, w, mm, bias):
            wait(act, S["parts_ready"], u - 1)
            buffer, stored, before = part_buffer(u)
            wait(act, stored, 16 * before)
            wait(act, S["norms"], u // 2)
            act.activation(FQ[:, mm, 0:w], PS[:, bank, 0:w], ACT.Identity, bias=bias)
            act.activation(buffer[:, 0, 0:w], PS[:, bank, 0:w], ACT.Identity, bias=bias)
            act.activation(SQ[:, mm, 0:w], PS[:, bank, 0:w], ACT.Square, bias=bias).then_inc(S["squares"], 1)

        split_unit = CK
        for u, kind, n, w, mm in stage1:
            if kind == "tokF":
                act.wait_ge(S["ctx_unit"], u + 1)
                act.activation(tokF[:, mm, n:n + w], PS[:, u % 4, 0:w], ACT.Identity,
                               bias=col("L0_xattn_b_proj", mm)).then_inc(S["ctx_taken_act"], 1)
            if kind == "k":
                act.wait_ge(S["ctx_unit"], u + 1)
                split(split_unit, u % 4, w, mm, col("L1_xattn_ca_bk", mm))
                split_unit += 1

        def h_taken(i):
            act.wait_ge(S["ln1_T"], i + 1)
            for c in range(2):
                ins = act.activation(hF[:, c, bass.ds(i * P, P)], PS[:, 5, (c + 1) * P:(c + 2) * P], ACT.Identity,
                                     scale=col("L1_xattn_ln1_g", c), bias=col("L1_xattn_ln1_b", c))
            ins.then_inc(S["ln1_taken"], 1)

        def l0(i, par, exp, routed, gates, norm1):
            if exp:
                act.wait_ge(S["l0_negmax"], i + 1)
                wait(act, S["l0_pT"], 4 * i)
                act.activation(PR[:], flat[:, 0:L], ACT.Exp, bias=sm(NEGM + par), scale=SCALE0,
                               accum_out=sm(SUM0 + par)).then_inc(S["l0_exp"], 1)
            if gates:
                act.wait_ge(S["l0_gates"], i - 1)
                wait(act, S["l0_rps"], i - 2)
                for c in range(2):
                    ins = act.activation(TR[:, c, :], PS[:, 7, c * P:(c + 1) * P], ACT.Tanh,
                                         bias=sm(BRH + c), scale=0.5)
                ins.then_inc(S["l0_rtanh"], 1)
            if exp:
                for k in range(4):
                    act.wait_ge(S["l0_pT"], 4 * i + k + 1)
                    if k < 3:
                        act.copy(PT[:, 4 * k:4 * k + 4, :].rearrange("p k q -> p (k q)"), PS[:, 4 + k % 2, :]) \
                            .then_inc(S["l0_pT_taken"], 1)
                    else:
                        act.copy(PT[0:LLAST, LT - 1, :], PS[0:LLAST, 5, 0:P]).then_inc(S["l0_pT_taken"], 1)
            if routed:
                act.wait_ge(S["l0_hatT"], i)
                for k, (g_, b_) in enumerate(2 * [("L0_xattn_g_state", "L0_xattn_beta_state")]
                                             + 2 * [("L0_xattn_g_input", "L0_xattn_beta_input")]):
                    ins = act.activation(CF[:, 1 - par, k, :], PS[:, 4, k * P:(k + 1) * P], ACT.Identity,
                                         scale=col(g_, k % 2), bias=col(b_, k % 2))
                ins.then_inc(S["l0_concat"], 1)
            if gates:
                act.wait_ge(S["l0_ubiased"], i - 1)
                act.activation(TU[:], UZ[:], ACT.Tanh, scale=0.5).then_inc(S["l0_utanh"], 1)
                act.wait_ge(S["l0_candz"], i - 1)
                act.activation(CD[:], CZ[:], ACT.Tanh).then_inc(S["l0_cand"], 1)
            if norm1:
                h_taken(i - 4)

        for i in range(4):
            l0(i, i % 2, True, i >= 1, i >= 2, False)
        with act.Fori(2, TILES // 2) as k:
            for par in range(2):
                l0(2 * k + par, par, True, True, True, True)
        for i in range(TILES, TILES + 2):
            l0(i, i % 2, False, i < TILES + 1, True, True)

        split_unit = SQK
        for u, kind, n, w, mm in stage3:
            if kind == "T":
                h_taken(n)
            if kind in ("k", "q"):
                act.wait_ge(S["qkv_unit"], u + 1)
                split(split_unit, u % 4, w, mm, col("L1_xattn_sa_b" + kind, mm))
                split_unit += 1

        for a in range(2):
            NK, at = NKS[a], A[a]
            steps = GROUPS * NK

            def gelu(q):
                act.wait_ge(at["unit_taken"], HID // P * (q + 1))
                act.activation(HIDT[:], HIDT[:], ACT.Gelu).then_inc(at["gelu"], 1)

            def chunk(c, first):
                for t in range(steps):
                    kr = key_rows(a, t % NK)
                    for half in range(2):
                        h = (c * steps + t) * 2 + half
                        act.wait_ge(at["scores"], h + 1)
                        if half == 0:
                            wait(act, at["pv"], c * steps + t - 1)
                            if a == 1 and first and t < 2:
                                act.wait_ge(A[0]["pv"], CHUNKS * GROUPS * NKS[0] - 1 + t)
                        slot = 2 * ((2 * t + half) % LOOK)
                        act.activation(PX[0:kr, (2 * t + half) % 4, :, :], PS[0:kr, slot:slot + 2, :],
                                       ACT.Exp, scale=SCALE).then_inc(at["exp"], 1)
                    if a == 1 and t == GELU_STEP and not first:
                        gelu(c - 1)

            chunk(0, True)
            with act.Fori(1, CHUNKS) as c:
                chunk(c, False)
            if a == 1:
                for i in range(HID // P):
                    u = HID // P * (CHUNKS - 1) + i
                    act.wait_ge(at["unit"], u + 1)
                    if i == 0:
                        act.wait_ge(at["mlp"], (CHUNKS - 1) * TPC)
                    act.activation(HIDT[:, i, :], PS[:, i % 4, :], ACT.Gelu, bias=col("L1_xattn_mlp_b1", i)) \
                        .then_inc(at["unit_taken"], 1)

    @block.tensor
    def _(pe):
        def norm(i, w, bank, halves=range(2)):
            pe.wait_ge(S["squares"], 2 * (i + 1))
            for mm in halves:
                ins = pe.matmul(PS[0:HEADS, bank, 0:w], headsum[:, mm, :], SQ[:, mm, 0:w],
                                start=(mm == 0), stop=(mm == 1))
            if 1 in halves:
                ins.then_inc(S["norms"], 1)

        pe.wait_ge(S["wproj_loaded"], 16)
        for u, kind, n, w, mm in stage1:
            if kind == "norm":
                if n == 0:
                    pe.wait_ge(S["const_loaded"], 16 * (3 + len(ROWS0)))
                wait(pe, S["norms_taken"], n)
                norm(n, w, 6)
                continue
            if u >= 4:
                pe.wait_ge(*taken(stage1, u - 4, 0))
            if kind == "tokF" and mm == 0:
                pe.wait_ge(s_ctx[n // CHUNK], 16)
            if kind == "k" and n == 0 and mm == 0:
                pe.wait_ge(S["cakv_loaded"], 32)
            bank = u % 4
            for c in range(2):
                if kind in ("tokF", "k"):
                    lhs = (WPJ[:, c, mm * P:(mm + 1) * P] if kind == "tokF" else
                           CAKV[:, 0, c, mm * P:(mm + 1) * P])
                    ins = pe.matmul(PS[:, bank, 0:w], lhs, ctxT[:, c, n:n + w], start=(c == 0), stop=(c == 1))
                else:
                    kr = key_rows(1, n)
                    rhs = WPJ[:, c, :] if kind == "tokT" else CAKV[:, 1, c, :]
                    ins = pe.matmul(PS[0:kr, bank, 0:D], ctxT[:, c, n * P:n * P + kr], rhs,
                                    start=(c == 0), stop=(c == 1))
            ins.then_inc(S["ctx_unit"], 1)

        pe.wait_ge(S["ctx_taken_act"], 2 * len(pcs))
        pe.wait_ge(S["ctx_taken_dve"], 2 * LT)
        pe.wait_ge(S["squares"], SQK)
        pe.wait_ge(S["norms_taken"], CHUNKS)
        pe.wait_ge(S["w0_loaded"], 48)

        def h_transposed(i, par):
            pe.wait_ge(S["ln1_hat"], i + 1)
            for c in range(2):
                ins = pe.transpose(PS[:, 5, (c + 1) * P:(c + 2) * P], XH1[:, par, c * P:(c + 1) * P], ident[:])
            ins.then_inc(S["ln1_T"], 1)

        def l0(i, par, turn, scores, routed, gates, norm1):
            if scores:
                pe.wait_ge(s_xt[par], 16 * (turn + 1))
                wait(pe, S["l0_exp"], i)
                for b, (n, w) in enumerate(pieces(L)):
                    for c in range(2):
                        ins = pe.matmul(PS[:, b, 0:w], XT[:, par, c, :], tokF[:, c, n:n + w],
                                        start=(c == 0), stop=(c == 1))
                ins.then_inc(S["l0_scores"], 1)
            if routed:
                pe.wait_ge(S["l0_pT_taken"], 4 * i)
                wait(pe, S["l0_candz"], i - 2)
                for kt in range(LT):
                    kr = key_rows(1, kt)
                    ins = pe.matmul(PS[:, 6, 0:D], PT[0:kr, kt, :], tokT[0:kr, kt, :],
                                    start=(kt == 0), stop=(kt == LT - 1))
                ins.then_inc(S["l0_routed"], 1)
            if gates:
                pe.wait_ge(S["l0_concat"], i - 1)
                wait(pe, S["l0_rps"], i - 2)
                for mm in range(2):
                    for c in range(4):
                        pe.matmul(PS[:, 7, mm * P:(mm + 1) * P], W0[:, 1, c, mm * P:(mm + 1) * P],
                                  CF[:, par, c, :], start=(c == 0), stop=(c == 3))
                for c in range(4):
                    ins = pe.matmul(PS[:, 7, D:2 * D], CF[:, par, c, :], W0[:, 0, c, :],
                                    start=(c == 0), stop=(c == 3))
                ins.then_inc(S["l0_gates"], 1)
            if scores:
                pe.wait_ge(S["l0_exp"], i + 1)
                for k in range(4):
                    if k >= 2:
                        pe.wait_ge(S["l0_pT_taken"], 4 * i + k - 1)
                    for kt in range(4 * k, min(4 * k + 4, LT)):
                        kr = key_rows(1, kt)
                        ins = pe.transpose(PS[0:kr, 4 + k % 2, (kt % 4) * P:(kt % 4 + 1) * P],
                                           PR[:, kt * P:kt * P + kr], ident[:])
                    ins.then_inc(S["l0_pT"], 1)
            if routed:
                pe.wait_ge(S["l0_hat"], i)
                if scores:
                    pe.wait_ge(S["l0_pT_taken"], 4 * i + 3)
                for k in range(4):
                    ins = pe.transpose(PS[:, 4, k * P:(k + 1) * P],
                                       XHS[:, 1 - par, k // 2, (k % 2) * P:(k % 2 + 1) * P], ident[:])
                ins.then_inc(S["l0_hatT"], 1)
            if gates:
                pe.wait_ge(S["l0_rps"], i - 1)
                for c in range(4):
                    ins = pe.matmul(PS[:, 6, 0:D], RPS[:, c, :] if c < 2 else CF[:, par, c, :],
                                    W0[:, 2, c, :], start=(c == 0), stop=(c == 3))
                ins.then_inc(S["l0_candps"], 1)
            if norm1:
                if scores:
                    pe.wait_ge(S["l0_pT_taken"], 4 * i + 4)
                elif i == TILES:
                    pe.wait_ge(S["l0_pT_taken"], 4 * TILES)
                else:
                    pe.wait_ge(S["ln1_taken"], i - 4)
                h_transposed(i - 4, par)

        for i in range(4):
            l0(i, i % 2, i // 2, True, i >= 1, i >= 2, False)
        with pe.Fori(2, TILES // 2) as k:
            for par in range(2):
                l0(2 * k + par, par, k, True, True, True, True)
        for i in range(TILES, TILES + 2):
            l0(i, i % 2, 0, False, i < TILES + 1, True, True)

        pe.wait_ge(S["saw_loaded"], 64)
        for u, kind, n, w, mm in stage3:
            if kind == "T":
                pe.wait_ge(S["ln1_taken"], n)
                h_transposed(n, n % 2)
                continue
            if kind == "norm":
                pe.wait_ge(S["norms_taken"], n)
                norm(n, w, 6)
                continue
            if u == 0:
                pe.wait_ge(S["l0_candz"], TILES)
            if kind == "shift":
                continue
            if u >= 4:
                pe.wait_ge(*taken(stage3, u - 4, SQK))
            if kind == "q":
                pe.wait_ge(S["ln1_taken"], n // P + TPC)
            for c in range(2):
                if kind == "v":
                    ins = pe.matmul(PS[:, u % 4, 0:D], hF[:, c, n * P:(n + 1) * P], SAW[:, 2, c, :],
                                    start=(c == 0), stop=(c == 1))
                else:
                    ins = pe.matmul(PS[:, u % 4, :], SAW[:, "qk".index(kind), c, mm * P:(mm + 1) * P],
                                    hF[:, c, n:n + w], start=(c == 0), stop=(c == 1))
            ins.then_inc(S["qkv_unit"], 1)
        pe.wait_ge(S["squares"], CQ)
        pe.wait_ge(S["v_unit_taken"], TILES)
        pe.wait_ge(S["ones_loaded"], 16)

        for a in range(2):
            NK, at = NKS[a], A[a]
            steps = GROUPS * NK

            def decide(f):
                row_ready = decision(f)[0]
                pe.wait_ge(A[DECIDES[f][0]]["flag_row"], row_ready)
                pe.matmul(PS[0:1, 7, 0:HEADS], sm(TB + f, 1, HEADS), ident[0:HEADS, 0:HEADS], start=True,
                          stop=True).then_inc(A[DECIDES[f][0]]["flag_row"], 1)

            def wait_k_stack(g):
                if a == 0:
                    pe.wait_ge(s_kst[0][0], 16 * len(KBLOCK) * CHUNKS)
                else:
                    pe.wait_ge(s_kst[1][g], 16 * len(KBLOCK))

            def general(f):
                n_chunks = DECIDES[f][2]
                pe.wait_ge(at["flag"], decision(f)[2])
                bounded = pe.value_load(flag[0:1, f:f + 1], min_val=0, max_val=1)

                def one(c):
                    for g in range(GROUPS):
                        pe.wait_ge(G[f]["q"], 16 * len(QBLOCK) * (c * GROUPS + g + 1))
                        for j in range(GH):
                            for tt in range(TPC):
                                if g or j or tt:
                                    pe.wait_ge(G[f]["max"], (c * GROUPS + g) * GH * TPC + j * TPC + tt)
                                for b, (n, w) in enumerate(pieces(KEYS[a])):
                                    ins = pe.matmul(PS[:, b, 0:w], QST[0:ROWS, g * GH + j, tt * P:(tt + 1) * P],
                                                    KST[a][0:ROWS, g * GH + j, n:n + w], start=True, stop=True)
                                ins.then_inc(G[f]["scores"], 1)
                    pe.wait_ge(G[f]["max"], (c + 1) * GROUPS * GH * TPC)
                    for tt in range(TPC):
                        ins = pe.matmul(PS[0:HEADS, 4, tt * P:(tt + 1) * P], sm(MX + tt * HEADS, HEADS),
                                        ident[:], start=True, stop=True)
                    ins.then_inc(G[f]["rows"], 1)

                with pe.If(bounded < 1):
                    for g in range(GROUPS):
                        wait_k_stack(g)
                    if f == 2:
                        pe.wait_ge(at["exp"], 2 * steps)
                        one(0)
                    else:
                        with pe.Fori(0, n_chunks) as c:
                            one(c)
                    pe.wait_ge(G[f]["split"], n_chunks)
                    if f < 2:
                        pe.wait_ge(G[f]["q"], 16 * GROUPS * (len(QBLOCK) * (n_chunks + 1) + 1))

            decide(a)
            general(a)

            def scores(c, n, first):
                h = c * steps * 2 + n
                t, half = n // 2, n % 2
                g, kt = t // NK, t % NK
                kr = key_rows(a, kt)
                if kt == 0 and half == 0:
                    if first:
                        wait_k_stack(g)
                    pe.wait_ge(s_qst[a][g], 16 * (len(QBLOCK) + 1) * (c + 1))
                wait(pe, at["exp"], h - 1 if n < 2 else h - 2)
                if a == 1 and first and n < 2:
                    pe.wait_ge(A[0]["exp"], 2 * CHUNKS * GROUPS * NKS[0] - 1 + n)
                for jj in range(2):
                    head = g * GH + 2 * half + jj
                    ins = pe.matmul(PS[0:kr, 2 * (n % LOOK) + jj, :], KST[a][0:NROW, head, kt * P:kt * P + kr],
                                    QST[0:NROW, head, :], start=True, stop=True)
                ins.then_inc(at["scores"], 1)

            def pv(c, t):
                g, kt = t // NK, t % NK
                kr = key_rows(a, kt)
                pe.wait_ge(at["exp"], (c * steps + t) * 2 + 2)
                if a == 1 and kt == 0 and isinstance(c, int):
                    pe.wait_ge(s_vst[g], 16)
                if kt == 0:
                    wait(pe, at["heads"], c * GROUPS + g)
                    if a == 1 and isinstance(c, int) and c == 0 and g == 0:
                        pe.wait_ge(A[0]["heads"], CHUNKS * GROUPS)
                for j in range(GH):
                    ins = pe.matmul(PS[32 * j:32 * j + 32, 6, :], V[0:kr, kt, g * GH + j, :],
                                    PX[0:kr, (2 * t + j // 2) % 4, j % 2, :],
                                    start=(kt == 0), stop=(kt == NK - 1))
                ins.then_inc(at["pv"], 1)

            def bank7_taken(c, kind, i, at=at):
                q = c - 1
                s_, value = {"sums": (at["sums_taken"], c * GROUPS + i), "y": (at["y_taken"], q * TPC + i + 1),
                             "h": (at["hc"], 2 * q + i + 1), "u": (at["unit_taken"], 2 * q + i + 1),
                             "n": (S["norms_taken"], 3 * CHUNKS + q + 1),
                             "m": (at["unit_taken"], HID // P * q + i + 1),
                             "o": (at["mlp_taken"], q * TPC + i + 1),
                             "flag": (A[1]["flag"], decision(2)[2])}[kind]
                pe.wait_ge(s_, value)

            def sums(c, g, at=at):
                u = c * GROUPS + g - 1
                pe.wait_ge(at["heads"], u + 1)
                pe.matmul(PS[:, 7, :], spread[:], OT[:, (g - 1) % 2, :], start=True, stop=True) \
                    .then_inc(at["sums"], 1)

            def piece(kind, i, q, part, tail=False, at=at):
                whole = part is None
                first, last = whole or part == 0, whole or part == PARTS_OF[kind] - 1

                def share(n):
                    if whole:
                        return range(n)
                    w = n // PARTS_OF[kind]
                    return range(part * w, (part + 1) * w)

                bank = i % 4 if tail else 7
                if kind == "y":
                    if i == 0 and first:
                        pe.wait_ge(at["normed"], (q + 1) * GROUPS)
                        pe.wait_ge(at["wop"], 16 * GH)
                    for g in share(GROUPS):
                        ins = pe.matmul(PS[:, bank, 0:D], ONF[:, g, i * P:(i + 1) * P], WOP[:, g, :],
                                        start=(g == 0), stop=(g == GROUPS - 1))
                    if last:
                        ins.then_inc(at["y"], 1)
                if kind == "h":
                    pe.wait_ge(at["hat"], q + 1)
                    for tt in range(TPC):
                        ins = pe.transpose(PS[:, bank, tt * P:(tt + 1) * P],
                                           XH[:, tt, i * P:(i + 1) * P], ident[:])
                    ins.then_inc(at["hT"], 1)
                if kind in ("u", "m"):
                    if first:
                        pe.wait_ge(at["hc"], 2 * q + 2)
                        if tail and i >= 4:
                            pe.wait_ge(at["unit_taken"], HID // P * q + i - 3)
                    for c in share(2):
                        ins = pe.matmul(PS[:, bank, :], (CAWQ if kind == "u" else W1)[:, c, i * P:(i + 1) * P],
                                        HC[:, c, :], start=(c == 0), stop=(c == 1))
                    if last:
                        ins.then_inc(at["unit"], 1)
                if kind == "n":
                    norm(3 * CHUNKS + q, CHUNK, 7, share(2))
                if kind == "o":
                    if tail:
                        pe.wait_ge(at["unit_taken"], HID // P * CHUNKS)
                    elif first:
                        pe.wait_ge(at["gelu"], q + 1)
                    for k in share(HID // P):
                        ins = pe.matmul(PS[:, bank, 0:D], HIDT[:, k, i * P:(i + 1) * P], W2[:, k, :],
                                        start=(k == 0), stop=(k == HID // P - 1))
                    if last:
                        ins.then_inc(at["mlp"], 1)

            def chunk(c, first):
                ev = events(a, first)
                held = None if first else (c - 1, "sums", GROUPS - 1, at)
                scores(c, 0, first)
                for t in range(steps):
                    if t == 0:
                        if not first:
                            pv(c - 1, steps - 1)
                        scores(c, 1, first)
                        scores(c, 2, first)
                    else:
                        if 2 * t + 2 < 2 * steps:
                            scores(c, 2 * t + 2, first)
                        pv(c, t - 1)
                    for o, kind, i, part, last in ev[t]:
                        if kind in ("copy", "divide", "hat"):
                            continue
                        if held is not None and part == 0:
                            bank7_taken(*held)
                        co = c if o == a else CHUNKS
                        held = (co, kind, i, A[o])
                        if kind == "sums":
                            sums(co, i, A[o])
                        elif kind == "flag":
                            decide(2)
                        else:
                            piece(kind, i, co - 1, part, at=A[o])
                    if 2 * t + 3 < 2 * steps:
                        scores(c, 2 * t + 3, first)

            chunk(0, True)
            if a == 1:
                general(2)
                pe.wait_ge(S["w1_loaded"], 16)
                pe.wait_ge(S["w2_loaded"], 16)
            with pe.Fori(1, CHUNKS) as c:
                chunk(c, False)
            pv(CHUNKS - 1, steps - 1)
            bank7_taken(CHUNKS - 1, "sums", GROUPS - 1)
            if a == 0:
                continue
            sums(CHUNKS, 0)
            for g in range(GROUPS):
                if g in (0, GROUPS - 1):
                    pe.wait_ge(at["normed"], CHUNKS * GROUPS - (1 if g == 0 else 0))
                if g == 0:
                    pe.wait_ge(at["wop"], 16 * GH)
                for i in range(TPC):
                    ins = pe.matmul(PS[:, i, 0:D], ONF[:, g, i * P:(i + 1) * P], WOP[:, g, :],
                                    start=(g == 0), stop=(g == GROUPS - 1))
                    if g == GROUPS - 1:
                        ins.then_inc(at["y"], 1)
            for kind, at_steps in REST[a].items():
                for i in range(len(at_steps) // PARTS_OF[kind]):
                    if kind != "y":
                        piece(kind, i, CHUNKS - 1, None, True)

    @block.vector
    def _(ve):
        ch = Chain(ve, S["dve_chain"])

        def rsqrt(n, link, i=0, ag=None, y=None, tmp=None):
            y = sm(NY + i, n) if y is None else y
            v, a_, b_, bits = (sm(o, n) for o in tmp or (NVAR, NA, NB, NI))
            ag = AG + 2 * i if ag is None else ag
            var = sm(ag, 2 * n).rearrange("p (n two) -> p n two", two=2)[:, :, 1:2].rearrange("p n o -> p (n o)")
            link(ve.tensor_scalar(v, var, EPS, None, ALU.add))
            link(ve.tensor_scalar(bits.bitcast(I32), v.bitcast(I32), 1, None, ALU.logical_shift_right))
            link(ve.tensor_scalar(y.bitcast(I32), bits.bitcast(I32), -1.0, float(0x5f3759df),
                                  ALU.mult, ALU.add))
            for _ in range(3):
                link(ve.tensor_tensor(a_, y, y, ALU.mult))
                link(ve.scalar_tensor_tensor(out=b_, in0=a_, scalar=-0.5, in1=v, op0=ALU.mult, op1=ALU.mult))
                link(ve.scalar_tensor_tensor(out=y, in0=b_, scalar=1.5, in1=y, op0=ALU.add, op1=ALU.mult))

        def stats(src, i, link):
            ve.sem_inc(S["dve_stepped"], 1)
            link(ve.bn_stats(sm(STAT + 6 * i, 6), src))
            ve.sem_inc(S["dve_stepped"], 1)
            link(ve.bn_aggr(sm(AG + 2 * i, 2), sm(STAT + 6 * i, 6)))

        def three(dst, src, tmp, link):
            link(ve.tensor_copy(dst[0], src))
            link(ve.tensor_tensor(tmp, src, dst[0], ALU.subtract))
            link(ve.tensor_copy(dst[1], tmp))
            return ve.tensor_tensor(dst[2], tmp, dst[1], ALU.subtract)

        def parts(i, w, mm):
            u = 2 * i + mm
            wait(ve, S[f"parts_stored{mm}"], 16 * (i - CHUNKS))
            three([PARTS[:, mm, r, 0:w] for r in range(3)], FQ[:, mm, 0:w], FR[:, 0:w], ch) \
                .then_inc(S["parts_ready"], 1)
            ve.wait_ge(S["parts_ready"], u + 1)
            ve.tensor_tensor(SQ[:, mm, 0:w], FQ[:, mm, 0:w], FQ[:, mm, 0:w], ALU.mult).then_inc(S["squares"], 1)
            ve.wait_ge(S["squares"], u + 1)

        def lower_parts(u, w, mm):
            ve.wait_ge(S["squares"], u + 1)
            hi, mid, lo = (part_buffer(u)[0][:, r, 0:w] for r in range(3))
            ch(ve.tensor_tensor(FR[:, 0:w], FQ[:, mm, 0:w], hi, ALU.subtract))
            ch(ve.tensor_copy(mid, FR[:, 0:w]))
            ve.tensor_tensor(lo, FR[:, 0:w], mid, ALU.subtract).then_inc(S["parts_ready"], 1)
            ve.wait_ge(S["parts_ready"], u + 1)

        def k_norm(i, a, n, w):
            ve.wait_ge(S["norms"], i + 1)
            ve.tensor_reduce(sm(KM + 4 * a + n, 1, HEADS), PS[0:HEADS, 6, 0:w], AX, ALU.max) \
                .then_inc(S["norms_taken"], 1)
            ve.wait_ge(S["norms_taken"], i + 1)
            if n == CHUNKS - 1:
                ch(ve.tensor_reduce(sm(KMT + a, 1, HEADS), sm(KM + 4 * a, 4, HEADS), AX, ALU.max))
                ch(ve.tensor_scalar(sm(NCF + a, 1, HEADS), sm(KMT + a, 1, HEADS), -1.0 / (2 * AMGM), None,
                                    ALU.mult))

        def shift_rows(j):
            wait(ve, S["shift_stored"], 16 * j)
            three([Rp[:, r, :] for r in range(3)], R[:], FR[0:HEADS, :], ch).then_inc(S["shift_ready"], 1)
            ve.wait_ge(S["shift_ready"], j + 1)

        def q_norm(i, n, bank):
            ve.wait_ge(S["norms"], i + 1)
            ch(ve.tensor_scalar(R[:], PS[0:HEADS, bank, :], sm(NCF + 1, 1, HEADS), -AMGM / 2,
                                ALU.mult, ALU.add))
            ve.tensor_reduce(small[0:HEADS, bass.ds(QM + n, 1)], PS[0:HEADS, bank, :], AX, ALU.max) \
                .then_inc(S["norms_taken"], 1)
            ve.wait_ge(S["norms_taken"], i + 1)
            shift_rows(CHUNKS + n)

        ve.wait_ge(S["const_loaded"], 16 * (3 + len(ROWS0)))
        split_unit, took = CK, 0
        for u, kind, n, w, mm in stage1:
            if kind == "norm":
                k_norm(n, 1, n, w)
            if kind == "k":
                lower_parts(split_unit, w, mm)
                split_unit += 1
            if kind in ("tokT", "v"):
                ve.wait_ge(S["ctx_unit"], u + 1)
                kr = key_rows(1, n)
                if kind == "tokT":
                    ve.tensor_tensor(tokT[0:kr, n, :], PS[0:kr, u % 4, 0:D], row("L0_xattn_b_proj")[0:kr],
                                     ALU.add).then_inc(S["ctx_taken_dve"], 1)
                else:
                    if n == 0:
                        ve.wait_ge(S["v_cleared"], 2)
                    ve.tensor_tensor(V[0:kr, n, :, 0:HD],
                                     PS[0:kr, u % 4, 0:D].rearrange("p (h e) -> p h e", h=HEADS),
                                     row("L1_xattn_ca_bv")[0:kr].rearrange("p (h e) -> p h e", h=HEADS),
                                     ALU.add).then_inc(S["ctx_taken_dve"], 1)
                took += 1
        ve.wait_ge(S["ctx_taken_dve"], took)
        def x_stats():
            ve.wait_ge(S["x_loaded"], 16)
            for i in range(TILES):
                ins = ve.bn_stats(sm(96 + 6 * i, 6), X[:, i, :])
            ch(ins)
            for i in range(TILES):
                ins = ve.bn_aggr(sm(AGX + 2 * i, 2), sm(96 + 6 * i, 6))
            ch(ins)
            rsqrt(TILES, ch, ag=AGX, y=sm(NYX, TILES), tmp=(128, 144, 160, 176))

        def l0(i, par, scores, routed, gates, finish, norm1):
            if scores:
                ve.wait_ge(S["l0_scores"], i + 1)
                ch(ve.tensor_reduce(sm(NEGR + par), flat[:, 0:L], AX, ALU.max, negate=True))
                ve.tensor_scalar(sm(NEGM + par), sm(NEGR + par), SCALE0, None, ALU.mult) \
                    .then_inc(S["l0_negmax"], 1)
                ve.wait_ge(S["l0_negmax"], i + 1)
            if isinstance(i, int) and i == 0:
                x_stats()
            if routed:
                ve.wait_ge(S["l0_routed"], i)
                ch(ve.reciprocal(sm(RS0), sm(SUM0 + 1 - par)))
                ch(ve.tensor_scalar(E1[:], PS[:, 6, 0:D], sm(RS0), None, ALU.mult))
                stats(E1[:], 1, ch)
            first, last = (0 if finish else 1 if routed else 2), (2 if norm1 else 1 if routed else 0)
            if last >= first:
                rsqrt(last - first + 1, ch, i=first)
            if routed:
                ve.tensor_scalar(XHS[:, 1 - par, 1, :], E1[:], sm(AG + 2), sm(NY + 1), ALU.subtract, ALU.mult)
                ve.tensor_scalar(XHS[:, 1 - par, 0, :], X[:, bass.ds(i - 1, 1), :].rearrange("p o d -> p (o d)"),
                                 small[:, bass.ds(AGX + 2 * (i - 1), 1)], small[:, bass.ds(NYX + i - 1, 1)],
                                 ALU.subtract, ALU.mult).then_inc(S["l0_hat"], 1)
                ve.wait_ge(S["l0_hat"], i)
            if norm1:
                if not routed:
                    ve.wait_ge(S["ln1_T"], i - 5)
                ve.tensor_scalar(XH1[:, par, :], X[:, bass.ds(i - 4, 1), :].rearrange("p o d -> p (o d)"),
                                 sm(AG + 4), sm(NY + 2), ALU.subtract, ALU.mult).then_inc(S["ln1_hat"], 1)
                ve.wait_ge(S["ln1_hat"], i - 3)
            if gates:
                ve.wait_ge(S["l0_rtanh"], i - 1)
                ve.tensor_tensor(UZ[:], PS[:, 7, D:2 * D], row("L0_xattn_b_u"), ALU.add) \
                    .then_inc(S["l0_ubiased"], 1)
                ve.wait_ge(S["l0_ubiased"], i - 1)
                ch(ve.tensor_scalar(RPS[:], TR[:], 0.5, 0.5, ALU.mult, ALU.add))
                ve.tensor_tensor(RPS[:], RPS[:], CF[:, par, 0:2, :], ALU.mult).then_inc(S["l0_rps"], 1)
                ve.wait_ge(S["l0_rps"], i - 1)
            if finish:
                xt = X[:, bass.ds(i - 3, 1), :].rearrange("p o d -> p (o d)")
                ch(ve.tensor_scalar(E2[:], E2[:], sm(AG), sm(NY), ALU.subtract, ALU.mult))
                ch(ve.tensor_tensor(E2[:], E2[:], row("L0_xattn_g_out"), ALU.mult))
                ve.tensor_tensor(xt, E2[:], row("L0_xattn_beta_out"), ALU.add).then_inc(S["l0_x1"], 1)
                ve.wait_ge(S["l0_x1"], i - 2)
                stats(xt, 2, ch)
            if gates:
                ve.wait_ge(S["l0_candps"], i - 1)
                ve.tensor_tensor(CZ[:], PS[:, 6, 0:D], row("L0_xattn_b_n"), ALU.add) \
                    .then_inc(S["l0_candz"], 1)
                ve.wait_ge(S["l0_candz"], i - 1)
                ve.wait_ge(S["l0_cand"], i - 1)
                xt = X[:, bass.ds(i - 2, 1), :].rearrange("p o d -> p (o d)")
                ch(ve.tensor_tensor(E2[:], CD[:], xt, ALU.subtract))
                ch(ve.scalar_tensor_tensor(out=E2[:], in0=TU[:], scalar=1.0, in1=E2[:],
                                           op0=ALU.add, op1=ALU.mult))
                ch(ve.scalar_tensor_tensor(out=E2[:], in0=E2[:], scalar=0.5, in1=xt,
                                           op0=ALU.mult, op1=ALU.add))
                stats(E2[:], 0, ch)

        for i in range(4):
            l0(i, i % 2, True, i >= 1, i >= 2, i >= 3, False)
        per_tile = 27
        before = ch.n
        with ve.Fori(2, TILES // 2) as k:
            for par in range(2):
                ch.base, ch.n = before + (2 * k + par - 4) * per_tile, 0
                l0(2 * k + par, par, True, True, True, True, True)
                assert ch.n == per_tile, ch.n
        ch.base, ch.n = 0, before + (TILES - 4) * per_tile
        for i in range(TILES, TILES + 4):
            l0(i, i % 2, False, i < TILES + 1, i < TILES + 2, i < TILES + 3, True)

        def self_shift(c):
            ch(ve.tensor_scalar(R[:], NQ[:, c, :], sm(NCF, 1, HEADS), -AMGM / 2, ALU.mult, ALU.add))
            shift_rows(c)

        split_unit = SQK
        for u, kind, n, w, mm in stage3:
            if kind == "shift":
                self_shift(0)
            if kind == "norm" and n % 2 == 1:
                k_norm(n, 0, (n - CHUNKS) // 2, w)
            elif kind == "norm":
                c = (n - CHUNKS) // 2
                ve.wait_ge(S["norms"], n + 1)
                ch(ve.tensor_copy(NQ[:, c, :], PS[0:HEADS, 6, :]))
                ve.tensor_reduce(sm(QM + c, 1, HEADS), PS[0:HEADS, 6, :], AX, ALU.max) \
                    .then_inc(S["norms_taken"], 1)
                ve.wait_ge(S["norms_taken"], n + 1)
            if kind == "v":
                ve.wait_ge(S["qkv_unit"], u + 1)
                if n == 0:
                    ve.wait_ge(S["v_cross_stored"], 16)
                    ve.wait_ge(S["rows1_loaded"], 16 * len(ROWS1))
                ve.tensor_tensor(V[:, n, :, 0:HD],
                                 PS[:, u % 4, 0:D].rearrange("p (h e) -> p h e", h=HEADS),
                                 row("L1_xattn_sa_bv").rearrange("p (h e) -> p h e", h=HEADS),
                                 ALU.add).then_inc(S["v_unit_taken"], 1)
            if kind in ("k", "q"):
                lower_parts(split_unit, w, mm)
                split_unit += 1

        for a in range(2):
            NK, at = NKS[a], A[a]

            def decide(f):
                _, c0, n = DECIDES[f]
                _, column_ready, made = decision(f)
                ve.wait_ge(S["norms_taken"], (3 + a) * CHUNKS if f != 1 else 4 * CHUNKS - 1)
                ch(ve.tensor_reduce(sm(QMT, 1, HEADS), sm(QM + c0, n, HEADS), AX, ALU.max))
                ve.tensor_tensor(sm(TB + f, 1, HEADS), sm(QMT, 1, HEADS), sm(KMT + a, 1, HEADS), ALU.mult) \
                    .then_inc(at["flag_row"], 1)
                ve.wait_ge(at["flag_row"], column_ready)
                ch(ve.tensor_reduce(sm(FM, 1, 1), PS[0:1, 7, 0:HEADS], AX, ALU.max))
                ve.tensor_scalar(flag[0:1, f:f + 1], sm(FM, 1, 1), BOUND * BOUND, None, ALU.is_le) \
                    .then_inc(at["flag"], 1)
                ve.wait_ge(at["flag"], made)

            def general(f):
                bounded = ve.value_load(flag[0:1, f:f + 1], min_val=0, max_val=1)
                gch = Chain(ve, G[f]["chain"])

                def one(c):
                    gch.base, gch.n = c * 3, 0
                    for g in range(GROUPS):
                        for j in range(GH):
                            for tt in range(TPC):
                                n = (c * GROUPS + g) * GH * TPC + j * TPC + tt
                                ve.wait_ge(G[f]["scores"], n + 1)
                                ve.tensor_reduce(sm(MX + tt * HEADS + g * GH + j), flat[:, 0:KEYS[a]], AX,
                                                 ALU.max, negate=True).then_inc(G[f]["max"], 1)
                                ve.wait_ge(G[f]["max"], n + 1)
                    ve.wait_ge(G[f]["rows"], c + 1)
                    three([Rp[:, r, :] for r in range(3)], PS[0:HEADS, 4, :], FR[0:HEADS, :], gch) \
                        .then_inc(G[f]["split"], 1)
                    ve.wait_ge(G[f]["split"], c + 1)
                    ve.wait_ge(G[f]["stored"], 16 * (c + 1))

                with ve.If(bounded < 1):
                    if f == 2:
                        one(0)
                    else:
                        with ve.Fori(0, DECIDES[f][2]) as c:
                            one(c)

            decide(a)
            if a == 0:
                for c in range(1, CHUNKS):
                    self_shift(c)
            general(a)

            def copy_heads(c, g, at=at, NK=NK):
                u = c * GROUPS + g - 1
                ve.wait_ge(at["pv"], (u + 1) * NK)
                ve.tensor_copy(OT[:, (g - 1) % 2, :], PS[:, 6, :]).then_inc(at["heads"], 1)
                ve.wait_ge(at["heads"], u + 1)

            def sums(c, g, at=at):
                u = c * GROUPS + g - 1
                ve.wait_ge(at["sums"], u + 1)
                ve.tensor_copy(REC[:], PS[:, 7, :]).then_inc(at["sums_taken"], 1)
                ve.wait_ge(at["sums_taken"], u + 1)

            def divide(c, g, half, a=a, at=at):
                u = c * GROUPS + g - 1
                part = REC[:, half * D:(half + 1) * D]
                ch(ve.reciprocal(part, part))
                if half == 0:
                    return
                if g == 1 and not isinstance(c, int):
                    ve.wait_ge(at["y"], c * TPC)
                elif a == 1 and g == 1:
                    ve.wait_ge(A[0]["y"], CHUNKS * TPC)
                ve.tensor_tensor(ONF[:, (g - 1) % GROUPS, :], OT[:, (g - 1) % 2, :], REC[:], ALU.mult) \
                    .then_inc(at["normed"], 1)
                ve.wait_ge(at["normed"], u + 1)

            def standardise(q, at=at):
                rsqrt(TPC, ch)
                for tt in range(TPC):
                    ins = ve.tensor_scalar(
                        XH[:, tt, :], X[:, bass.ds(q * TPC + tt, 1), :].rearrange("p o d -> p (o d)"),
                        sm(AG + 2 * tt), sm(NY + tt), ALU.subtract, ALU.mult)
                ins.then_inc(at["hat"], 1)
                ve.wait_ge(at["hat"], q + 1)

            def piece(kind, i, q, tail=False, a=a, at=at):
                if kind in "yo":
                    xt = X[:, bass.ds(q * TPC + i, 1), :].rearrange("p o d -> p (o d)")
                if kind == "y":
                    ve.wait_ge(at["y"], q * TPC + i + 1)
                    ve.tensor_tensor(XH[:, i, :], PS[:, 7, 0:D], row(("L1_xattn_sa_bo", "L1_xattn_ca_bo")[a]),
                                     ALU.add).then_inc(at["y_taken"], 1)
                    ve.wait_ge(at["y_taken"], q * TPC + i + 1)
                    ch(ve.tensor_tensor(xt, XH[:, i, :], xt, ALU.add))
                    stats(xt, i, ch)
                if kind == "h":
                    ln = ("L1_xattn_ln2_", "L1_xattn_ln3_")[a]
                    ve.wait_ge(at["hT"], 2 * q + i + 1)
                    ve.tensor_scalar(HC[:, i, :], PS[:, i if tail else 7, :], col(ln + "g", i), col(ln + "b", i),
                                     ALU.mult, ALU.add).then_inc(at["hc"], 1)
                    ve.wait_ge(at["hc"], 2 * q + i + 1)
                if kind == "u":
                    ve.wait_ge(at["unit"], 2 * q + i + 1)
                    ve.tensor_scalar(FQ[:, i, :], PS[:, 7, :], col("L1_xattn_ca_bq", i), None, ALU.add) \
                        .then_inc(at["unit_taken"], 1)
                    ve.wait_ge(at["unit_taken"], 2 * q + i + 1)
                    parts(CQ // 2 + q, CHUNK, i)
                if kind == "n":
                    q_norm(3 * CHUNKS + q, q, 7)
                if kind == "m" and not tail:
                    ve.wait_ge(at["unit"], HID // P * q + i + 1)
                    ve.tensor_scalar(HIDT[:, i, :], PS[:, 7, :], col("L1_xattn_mlp_b1", i), None, ALU.add) \
                        .then_inc(at["unit_taken"], 1)
                    ve.wait_ge(at["unit_taken"], HID // P * q + i + 1)
                if kind == "o":
                    ve.wait_ge(at["mlp"], q * TPC + i + 1)
                    ve.tensor_tensor(XH[:, i, :], PS[:, i if tail else 7, 0:D], row("L1_xattn_mlp_b2"), ALU.add) \
                        .then_inc(at["mlp_taken"], 1)
                    ve.wait_ge(at["mlp_taken"], q * TPC + i + 1)
                    ve.tensor_tensor(XH[:, i, :], XH[:, i, :], xt, ALU.add).then_inc(at["out_ready"], 1)
                    ve.wait_ge(at["out_ready"], q * TPC + i + 1)

            def y_tail():
                q = CHUNKS - 1
                ve.wait_ge(at["y"], (q + 1) * TPC)
                for i in range(TPC):
                    ve.tensor_tensor(XH[:, i, :], PS[:, i, 0:D], row(("L1_xattn_sa_bo", "L1_xattn_ca_bo")[a]),
                                     ALU.add).then_inc(at["y_taken"], 1)
                ve.wait_ge(at["y_taken"], (q + 1) * TPC)
                for i in range(TPC):
                    ins = ve.tensor_tensor(X[:, q * TPC + i, :], XH[:, i, :], X[:, q * TPC + i, :], ALU.add)
                ch(ins)
                for i in range(TPC):
                    ins = ve.bn_stats(sm(STAT + 6 * i, 6), X[:, q * TPC + i, :])
                ch(ins)
                for i in range(TPC):
                    ins = ve.bn_aggr(sm(AG + 2 * i, 2), sm(STAT + 6 * i, 6))
                ch(ins)
                standardise(q)

            def chunk(c, first):
                ev = events(a, first)
                for t in range(GROUPS * NK):
                    for o, kind, i, part, last in ev[t]:
                        co = c if o == a else CHUNKS
                        if kind == "copy":
                            copy_heads(co, i, A[o], NKS[o])
                        elif kind == "sums":
                            sums(co, i, A[o])
                        elif kind == "divide":
                            divide(co, i, part, o, A[o])
                        elif kind == "hat":
                            standardise(co - 1, A[o])
                        elif kind == "flag":
                            decide(2)
                        elif last:
                            piece(kind, i, co - 1, a=o, at=A[o])
                if a == 1 and not first:
                    ve.wait_ge(S["out_stored"], 16 * TPC * c)

            chunk(0, True)
            if a == 1:
                general(2)
            before = ch.n
            per_chunk = (42, 32)[a]
            with ve.Fori(1, CHUNKS) as c:
                ch.base, ch.n = before + (c - 1) * per_chunk, 0
                chunk(c, False)
                assert ch.n == per_chunk, ch.n
            ch.base, ch.n = 0, before + (CHUNKS - 1) * per_chunk
            if a == 0:
                continue
            copy_heads(CHUNKS, 0)
            sums(CHUNKS, 0)
            for half in range(2):
                divide(CHUNKS, 0, half)
            y_tail()
            for kind, at_steps in REST[a].items():
                for i in range(len(at_steps) // PARTS_OF[kind]):
                    if kind != "y":
                        piece(kind, i, CHUNKS - 1, True)


INPUTS = ["x", "xT", "ctxT", "Wproj", "Wu", "Wr", "Wn", "saq", "sak", "sav", "caq", "cak", "cav",
          "sawo", "cawo", "w1T", "w2T", "cols", "rows0", "rows1", "headsum", "ident", "spread", "ones"]


def kernel(**inputs):
    import numpy as _np
    import concourse.bacc as _bacc
    from concourse import mybir as _mybir
    from concourse.bass_utils import run_bass_kernel_spmd as _run

    v = {n: _np.asarray(a) for n, a in inputs.items()}
    x, c = v["x"][0], v["ctx_768"][0]
    data = {
        "x": x, "xT": x.T, "ctxT": c.T, "Wproj": v["L0_xattn_W_proj"],
        "Wu": v["L0_xattn_W_u"], "Wr": v["L0_xattn_W_r"], "Wn": v["L0_xattn_W_n"],
        "saq": v["L1_xattn_sa_wq"].T, "sak": v["L1_xattn_sa_wk"].T, "sav": v["L1_xattn_sa_wv"].T,
        "caq": v["L1_xattn_ca_wq"].T, "cak": v["L1_xattn_ca_wk"].T, "cav": v["L1_xattn_ca_wv"].T,
        "sawo": v["L1_xattn_sa_wo"].T, "cawo": v["L1_xattn_ca_wo"].T,
        "w1T": v["L1_xattn_mlp_w1"].T, "w2T": v["L1_xattn_mlp_w2"].T,
        "cols": _np.concatenate([v[n].reshape(-1, P).T for n in COLS], 1),
        "rows0": _np.stack([v[n] for n in ROWS0]),
        "rows1": _np.stack([v[n] for n in ROWS1]),
    }
    headsum = _np.zeros((P, 2, HEADS), _np.float32)
    spread = _np.zeros((P, P), _np.float32)
    for p in range(P):
        for half in range(2):
            headsum[p, half, 8 * half + p // HD] = 1.0
        spread[32 * (p // 32) + HD, p] = 1.0
    ones = _np.full((NROW - ROWS, HEADS * T // 2), 0x3F803F80, _np.uint32).view(_np.float32)
    data.update(headsum=headsum, spread=spread, ident=_np.eye(P, dtype=_np.float32), ones=ones)

    nc = _bacc.Bacc("TRN2", target_bir_lowering=False, num_devices=1)
    arrays, d = {}, {}
    for n in INPUTS:
        a = _np.ascontiguousarray(data[n])
        arrays[f"in_{n}"] = a
        d[n] = nc.dram_tensor(f"in_{n}", a.shape, _mybir.dt.from_np(a.dtype), kind="ExternalInput").ap()
    out = nc.dram_tensor("out", (T, D), _mybir.dt.float32, kind="ExternalOutput").ap()
    program(nc, d, out)
    r = _run(nc, [arrays], core_ids=[0])
    return r.results[0]["out"].reshape(1, T, D)
```
